# Optimizing a Trainium2 kernel written in Bass

```python
import numpy as np
import jax
import jax.numpy as jnp

def _softmax(x, axis=-1):
    return jax.nn.softmax(x, axis=axis)

def _gelu(x):
    return jax.nn.gelu(x, approximate=True)

def _silu(x):
    return jax.nn.silu(x)

def _sigmoid(x):
    return jax.nn.sigmoid(x)

def _layernorm(x, axis=-1, eps=1e-05):
    m = jnp.mean(x, axis=axis, keepdims=True)
    v = jnp.var(x, axis=axis, keepdims=True)
    return (x - m) / jnp.sqrt(v + eps)

def _scatter_add(tgt, idx, src, axis=0):
    return tgt.at[idx].add(src)

def _segment_sum(src, seg, n):
    return jax.ops.segment_sum(src, seg, n)
kernel_name = 'mk_macaron_d1_jaxref_r4_0581ff'

def setup_inputs(seed: int=0):
    np.random.seed(seed)
    _w = jnp.asarray

    def _L0_attn_setup():
        import jax, jax.numpy as jnp
        import numpy as np
        D_K = 128
        key = jax.random.key(seed)
        ks = jax.random.split(key, 5)
        B, T, D = (4, 512, 256)
        scale = 0.02
        return {'x': jax.random.normal(ks[0], (B, T, D), dtype=jnp.float32), 'Wq': jax.random.normal(ks[1], (D, D_K), dtype=jnp.float32) * scale, 'Wk': jax.random.normal(ks[2], (D, D_K), dtype=jnp.float32) * scale, 'Wv': jax.random.normal(ks[3], (D, D_K), dtype=jnp.float32) * scale, 'Wo': jax.random.normal(ks[4], (D_K, D), dtype=jnp.float32) * scale}
    _L0_attn_in = _L0_attn_setup()

    def _L0_ffn_setup():
        import jax, jax.numpy as jnp
        import numpy as np

        def _ln(x, w, b):
            m = jnp.mean(x, axis=-1, keepdims=True)
            v = jnp.var(x, axis=-1, keepdims=True)
            return (x - m) / jnp.sqrt(v + 1e-05) * w + b
        B, T, C = (4, 512, 256)
        E_RWKV, E = (2, 3)
        H = 4 * C
        S = 0.02
        key = jax.random.key(seed)
        ks = jax.random.split(key, 20)
        d = {}
        d['x'] = jax.random.normal(ks[0], (B, T, C), jnp.float32)
        d['v_first'] = jax.random.normal(ks[1], (B, T, C), jnp.float32)
        d['capital_shares'] = jax.random.uniform(ks[2], (E,), jnp.float32)
        d['ln1_w'] = jnp.ones((C,), jnp.float32)
        d['ln1_b'] = jnp.zeros((C,), jnp.float32)
        d['ln2_w'] = jnp.ones((C,), jnp.float32)
        d['ln2_b'] = jnp.zeros((C,), jnp.float32)
        d['Wr'] = S * jax.random.normal(ks[3], (C, C), jnp.float32)
        d['Wv'] = S * jax.random.normal(ks[4], (C, C), jnp.float32)
        d['Wo'] = S * jax.random.normal(ks[5], (C, C), jnp.float32)
        d['Ws'] = S * jax.random.normal(ks[6], (C, C), jnp.float32)
        d['K_rwkv'] = S * jax.random.normal(ks[7], (E_RWKV, C, H), jnp.float32)
        d['V_rwkv'] = S * jax.random.normal(ks[8], (E_RWKV, H, C), jnp.float32)
        d['conf_rwkv'] = S * jax.random.normal(ks[9], (E_RWKV, C), jnp.float32)
        d['W1'] = S * jax.random.normal(ks[10], (C, C), jnp.float32)
        d['W2'] = S * jax.random.normal(ks[11], (C, C), jnp.float32)
        d['W3'] = S * jax.random.normal(ks[12], (C, C), jnp.float32)
        d['conf_trans'] = S * jax.random.normal(ks[13], (C,), jnp.float32)
        d['w_diff'] = S * jax.random.normal(ks[14], (C,), jnp.float32)
        d['W_aff'] = S * jax.random.normal(ks[15], (C, E), jnp.float32)
        d['W_bridge'] = S * jax.random.normal(ks[16], (C, C), jnp.float32)
        return d
    _L0_ffn_in = _L0_ffn_setup()
    _d = {'L0_attn_x': _L0_attn_in['x'], 'L0_attn_Wq': _L0_attn_in['Wq'], 'L0_attn_Wk': _L0_attn_in['Wk'], 'L0_attn_Wv': _L0_attn_in['Wv'], 'L0_attn_Wo': _L0_attn_in['Wo'], 'L0_ffn_v_first': _L0_ffn_in['v_first'], 'L0_ffn_capital_shares': _L0_ffn_in['capital_shares'], 'L0_ffn_ln1_w': _L0_ffn_in['ln1_w'], 'L0_ffn_ln1_b': _L0_ffn_in['ln1_b'], 'L0_ffn_ln2_w': _L0_ffn_in['ln2_w'], 'L0_ffn_ln2_b': _L0_ffn_in['ln2_b'], 'L0_ffn_Wr': _L0_ffn_in['Wr'], 'L0_ffn_Wv': _L0_ffn_in['Wv'], 'L0_ffn_Wo': _L0_ffn_in['Wo'], 'L0_ffn_Ws': _L0_ffn_in['Ws'], 'L0_ffn_K_rwkv': _L0_ffn_in['K_rwkv'], 'L0_ffn_V_rwkv': _L0_ffn_in['V_rwkv'], 'L0_ffn_conf_rwkv': _L0_ffn_in['conf_rwkv'], 'L0_ffn_W1': _L0_ffn_in['W1'], 'L0_ffn_W2': _L0_ffn_in['W2'], 'L0_ffn_W3': _L0_ffn_in['W3'], 'L0_ffn_conf_trans': _L0_ffn_in['conf_trans'], 'L0_ffn_w_diff': _L0_ffn_in['w_diff'], 'L0_ffn_W_aff': _L0_ffn_in['W_aff'], 'L0_ffn_W_bridge': _L0_ffn_in['W_bridge']}
    _x0 = _d['L0_attn_x']
    _d['L0_attn_x'] = jax.random.normal(jax.random.fold_in(jax.random.key(seed), 1), (2, 2048, 256), dtype=_x0.dtype)
    del _x0
    return _d

def reference(L0_attn_x, L0_attn_Wq, L0_attn_Wk, L0_attn_Wv, L0_attn_Wo, L0_ffn_v_first, L0_ffn_capital_shares, L0_ffn_ln1_w, L0_ffn_ln1_b, L0_ffn_ln2_w, L0_ffn_ln2_b, L0_ffn_Wr, L0_ffn_Wv, L0_ffn_Wo, L0_ffn_Ws, L0_ffn_K_rwkv, L0_ffn_V_rwkv, L0_ffn_conf_rwkv, L0_ffn_W1, L0_ffn_W2, L0_ffn_W3, L0_ffn_conf_trans, L0_ffn_w_diff, L0_ffn_W_aff, L0_ffn_W_bridge):

    def _L0_attn_ref(x, Wq, Wk, Wv, Wo):
        import jax, jax.numpy as jnp
        import numpy as np
        D_K = 128
        Q = x @ Wq
        K = x @ Wk
        V = x @ Wv
        d_k = Q.shape[-1]
        logits = jnp.einsum('bqd,bkd->bqk', Q, K) * d_k ** (-0.5)
        T = logits.shape[-1]
        causal = jnp.triu(jnp.ones((T, T), dtype=bool), k=1)
        logits = jnp.where(causal, -jnp.inf, logits)
        attn = jax.nn.softmax(logits, axis=-1)
        out = jnp.einsum('bqk,bkd->bqd', attn, V)
        return out @ Wo

    def _L0_ffn_ref(x, v_first, capital_shares, ln1_w, ln1_b, ln2_w, ln2_b, Wr, Wv, Wo, Ws, K_rwkv, V_rwkv, conf_rwkv, W1, W2, W3, conf_trans, w_diff, W_aff, W_bridge):
        import jax, jax.numpy as jnp
        import numpy as np

        def _ln(x, w, b):
            m = jnp.mean(x, axis=-1, keepdims=True)
            v = jnp.var(x, axis=-1, keepdims=True)
            return (x - m) / jnp.sqrt(v + 1e-05) * w + b
        B, T, C = x.shape
        xln = _ln(x, ln1_w, ln1_b)
        att_out = jax.nn.sigmoid(xln @ Wr) * (xln @ Wv) @ Wo
        rwkv_state = xln @ Ws
        x = x + att_out
        h = _ln(x, ln2_w, ln2_b)
        conf_r = jax.nn.sigmoid(jnp.einsum('btc,ec->bte', h, conf_rwkv))
        conf_t = jax.nn.sigmoid(h @ conf_trans)[..., None]
        confidences = jnp.concatenate([conf_r, conf_t], axis=-1)
        E = confidences.shape[-1]
        difficulty = jax.nn.sigmoid(h @ w_diff)[..., None]
        affinity = h @ W_aff
        bids = confidences * capital_shares * difficulty + affinity
        winners = jnp.argmax(bids, axis=-1)
        flat_h = h.reshape(-1, C)
        flat_state = rwkv_state.reshape(-1, C)
        flat_w = winners.reshape(-1)
        flat_conf = confidences.reshape(-1, E)
        win_conf = jnp.take_along_axis(flat_conf, flat_w[:, None], axis=1)
        scale = win_conf / (jax.lax.stop_gradient(win_conf) + 1e-06)
        hr = jnp.square(jax.nn.relu(jnp.einsum('nc,ech->enh', flat_h, K_rwkv)))
        out_rwkv = jnp.einsum('enh,ehc->enc', hr, V_rwkv)
        out_trans = flat_h @ W1 * jax.nn.sigmoid(flat_state @ W2) @ W3
        all_out = jnp.concatenate([out_rwkv, out_trans[None]], axis=0)
        onehot = jax.nn.one_hot(flat_w, E, dtype=flat_h.dtype)
        final = jnp.einsum('ne,enc->nc', onehot, all_out) * scale
        return x + final.reshape(B, T, C)
    x = L0_attn_x
    x = x + 0.5 * _L0_ffn_ref(_layernorm(x, axis=-1), L0_ffn_v_first, L0_ffn_capital_shares, L0_ffn_ln1_w, L0_ffn_ln1_b, L0_ffn_ln2_w, L0_ffn_ln2_b, L0_ffn_Wr, L0_ffn_Wv, L0_ffn_Wo, L0_ffn_Ws, L0_ffn_K_rwkv, L0_ffn_V_rwkv, L0_ffn_conf_rwkv, L0_ffn_W1, L0_ffn_W2, L0_ffn_W3, L0_ffn_conf_trans, L0_ffn_w_diff, L0_ffn_W_aff, L0_ffn_W_bridge)
    x = x + _L0_attn_ref(_layernorm(x, axis=-1), L0_attn_Wq, L0_attn_Wk, L0_attn_Wv, L0_attn_Wo)
    x = x + 0.5 * _L0_ffn_ref(_layernorm(x, axis=-1), L0_ffn_v_first, L0_ffn_capital_shares, L0_ffn_ln1_w, L0_ffn_ln1_b, L0_ffn_ln2_w, L0_ffn_ln2_b, L0_ffn_Wr, L0_ffn_Wv, L0_ffn_Wo, L0_ffn_Ws, L0_ffn_K_rwkv, L0_ffn_V_rwkv, L0_ffn_conf_rwkv, L0_ffn_W1, L0_ffn_W2, L0_ffn_W3, L0_ffn_conf_trans, L0_ffn_w_diff, L0_ffn_W_aff, L0_ffn_W_bridge)
    return x

_drawn_inputs = setup_inputs


def setup_inputs(seed=0):
    import zlib

    import numpy as np

    out = dict(_drawn_inputs(seed))
    spreads = {'L0_ffn_ln1_w': (1.0, 0.6),
     'L0_ffn_ln1_b': (0.0, 0.8),
     'L0_ffn_ln2_w': (1.0, 0.6),
     'L0_ffn_ln2_b': (0.0, 0.501)}
    factors = {'L0_attn_Wq': 8.0,
     'L0_attn_Wk': 8.0,
     'L0_attn_Wv': 8.0,
     'L0_attn_Wo': 8.0,
     'L0_ffn_Wr': 8.0,
     'L0_ffn_Ws': 8.0,
     'L0_ffn_conf_rwkv': 5.13,
     'L0_ffn_W1': 3.498,
     'L0_ffn_W2': 8.0,
     'L0_ffn_W3': 3.493,
     'L0_ffn_conf_trans': 8.0,
     'L0_ffn_w_diff': 8.0}
    for name, (base, spread) in spreads.items():
        noise = np.random.default_rng([zlib.crc32(name.encode()), seed]).standard_normal(out[name].shape)
        drawn = base * np.exp(spread * noise) if base else spread * noise
        out[name] = jnp.asarray(drawn.astype(out[name].dtype))
    for name, factor in factors.items():
        out[name] = (out[name] * factor).astype(out[name].dtype)
    return out
```

```python
from contextlib import ExitStack

import numpy as np
import concourse.bass as bass
from concourse import mybir

F32, F32R = mybir.dt.float32, mybir.dt.float32r
BF16, I32, U32 = mybir.dt.bfloat16, mybir.dt.int32, mybir.dt.uint32
ALU, ACT, AX = mybir.AluOpType, mybir.ActivationFunctionType, mybir.AxisListType

P = 128
EPS = 1e-5
BATCH, SEQ, C = 2, 2048, 256
N = BATCH * SEQ
CC = C // P
HID = 1024
HC = HID // P
DK = 128
GT = 4
GROUP = GT * P
NG = N // GROUP
ST = 2
SLOT = ST * P
NSLOT = N // SLOT + 1
ROWS = NSLOT * SLOT
ROW = 2 * C + 2
BIDS = 8
QB = SEQ // SLOT
SCALE = float(DK) ** -0.5
PASSES = ((0, 0), (1, 0), (0, 1))


class Named:
    pass


def hold(eng, sem, value, carrier):
    if isinstance(value, int):
        if value > 0:
            eng.wait_ge(sem, value)
        return
    eng.wait_ge(sem, value)
    eng.sem_inc(carrier, 1)


def build_kernel(nc, x, w256, w_st, k_w, v_w, w_qkv, ln, shares, ident, tri, mask, tok, slot_row, out):
    with ExitStack() as ctx:
        def sb(name, shape, dt=F32):
            return ctx.enter_context(nc.sbuf_tensor(name, shape, dt))

        def sem(name):
            return ctx.enter_context(nc.semaphore(name))

        b, s = Named(), Named()
        b.x1 = nc.dram_tensor("x_after_ffn1", (N, C), F32, kind="Internal").ap()
        b.x2 = nc.dram_tensor("x_after_attention", (N, C), F32, kind="Internal").ap()
        b.routed = [nc.dram_tensor(f"routed_rows{i}", (ROWS, ROW), F32, kind="Internal").ap() for i in range(2)]

        b.W = [sb(f"w_{p}", [P, 5, CC, C], F32R) for p in ("hi", "lo")]
        b.W3 = [sb(f"w3_{p}", [P, CC, C], F32R) for p in ("hi", "lo")]
        b.K = [sb(f"k_{p}", [P, 2, CC, HID], F32R) for p in ("hi", "lo")]
        b.V = [sb(f"v_{p}", [P, 2, HC, C], F32R) for p in ("hi", "lo")]
        b.Wb = sb("w_bid", [P, CC, P], F32R)
        b.Wqk = [sb(f"wqk_{p}", [P, 2, CC, DK], F32R) for p in ("hi", "lo")]
        b.Wvv = sb("wv_hilo", [P, CC, 2 * DK], F32R)
        b.Wao = [sb(f"wao_{p}", [P, C], F32R) for p in ("hi", "lo")]
        b.ln = sb("ln_cols", [P, 4, CC])
        b.ident = sb("ident_sb", [P, P])
        b.trif = sb("tri_f32", [P, 2, P])
        b.tri = sb("tri_sb", [P, 2, P], BF16)
        b.mask = sb("mask_sb", [P, ST, SLOT])
        b.tok = sb("tok_sb", [P, 2, N // P])
        b.slot_row = sb("slot_row_sb", [P, NSLOT + ST])
        b.shares = sb("shares_sb", [P, 3])
        b.bias = sb("bias_cols", [P, 4, CC])
        b.kbias = sb("k_bias", [P, 2, HC])
        b.bbias = sb("bid_bias", [P, 1])
        b.half = sb("minus_half", [P, 8])
        b.ones4 = sb("ones4", [P, GT])
        FA, RA = 13184, 12800
        af, ar = sb("arena_f32", [P, FA]), sb("arena_f32r", [P, RA], F32R)
        pos = {"f": 0, "r": 0}

        def view(which, *dims):
            n = int(np.prod(dims))
            start = pos[which]
            pos[which] += n
            assert pos[which] <= (FA if which == "f" else RA), (pos, dims)
            v = (af if which == "f" else ar)[:, start:start + n]
            if len(dims) == 2:
                v = v.rearrange("p (a b) -> p a b", a=dims[0])
            if len(dims) == 3:
                v = v.rearrange("p (a b c) -> p a b c", a=dims[0], b=dims[1])
            return v

        b.stage = [view("f", 4096) for _ in range(2)]
        b.raw_sf = view("f", CC, C)
        b.raw_w3 = b.stage[1][:, 2 * CC * C:3 * CC * C].rearrange("p (c n) -> p c n", c=CC)
        pos["f"] = pos["r"] = 0
        b.x = [view("f", GT, C) for _ in range(2)]
        b.z = view("f", GT, C)
        b.y = view("f", GT, C)
        b.rg = view("f", CC, GROUP)
        b.sg = [view("f", CC, GROUP) for _ in range(2)]
        b.xa = view("f", GT, C)
        b.rows = [view("f", GT, ROW) for _ in range(2)]
        b.bd = view("f", GROUP)
        b.zT = [view("r", CC, GROUP) for _ in range(2)]
        b.gT = [view("r", CC, GROUP) for _ in range(2)]
        b.hT = [view("r", CC, GROUP) for _ in range(2)]
        b.g2T = [view("r", CC, GROUP) for _ in range(2)]
        fa_end = pos["f"]
        pos["f"] = pos["r"] = 0
        b.sz = [view("f", ST, C) for _ in range(2)]
        b.srow = [view("f", ST, ROW - C) for _ in range(2)]
        b.r = [view("f", 2 * SLOT) for _ in range(2)]
        b.sq = [view("f", 2 * SLOT) for _ in range(2)]
        b.o = [view("f", ST, C) for _ in range(2)]
        b.shT = [view("r", CC, SLOT) for _ in range(2)]
        b.hr = [[view("r", HC, SLOT) for _ in range(2)] for _ in range(2)]
        pos["f"] = pos["r"] = 0
        b.ax = [view("f", ST, C) for _ in range(2)]
        b.az = view("f", ST, C)
        b.vt = view("f", ST, DK)
        b.vs = view("f", ST, DK)
        b.p = [view("f", ST, SEQ), view("f", ST, SEQ - SLOT)]
        b.ao = view("f", ST, C)
        b.azT = [view("r", CC, SLOT) for _ in range(2)]
        b.qT = [view("r", SLOT) for _ in range(2)]
        b.kT = [view("r", SEQ) for _ in range(2)]
        b.v = [view("r", SEQ // P, DK) for _ in range(2)]
        b.pT = [[view("r", 2, SLOT) for _ in range(2)] for _ in range(2)]
        b.oT = [view("r", SLOT) for _ in range(2)]
        b.st = sb("bn_parts", [P, 2, GT, 6])
        b.mv = sb("mean_var", [P, 2, GT, 2])
        b.rs = sb("rsqrt_work", [P, 2, 4, GT])
        b.bid = sb("bid_rows", [P, GT, BIDS])
        b.conf = sb("conf_rows", [P, GT, 4])
        b.gw = sb("gate_work", [P, 12, GT])
        b.gt = [sb(f"trans_gate{i}", [P, GT]) for i in range(2)]
        b.cnt = sb("expert1_count", [P, GT + 1])
        b.e16 = sb("expert1_bf16", [P, 2 * GT + 2], BF16)
        b.posi = [sb(f"row_index{i}", [P, GT], I32) for i in range(2)]
        b.padrow = sb("pad_rows", [P, ROW])
        b.padi = sb("pad_index", [P, ST], I32)
        b.n1 = sb("n_expert1", [P, 1])
        b.flag = sb("slot_expert", [P, NSLOT])
        b.flagi = sb("slot_expert_int", [P, NSLOT], I32)
        b.nflag = sb("slot_expert0", [P, NSLOT])
        b.idx = [sb(f"token_index{i}", [P, ST], I32) for i in range(2)]
        b.kbt = sb("slot_k_bias_part", [P, HC])
        b.kbs = [sb(f"slot_k_bias{i}", [P, HC]) for i in range(2)]
        b.mx = sb("row_max", [P, 8, ST])
        b.sum = sb("row_sum", [P, 2, ST])

        b.ps = [ctx.enter_context(nc.psum_tensor(f"bank{i}", [P, 512], F32)) for i in range(4)]
        b.ps4 = ctx.enter_context(nc.psum_tensor("banks4to7", [P, 4, 512], F32))
        b.bank = lambda i: b.ps[i][:, :] if i < 4 else b.ps4[:, i - 4, :]

        b.carry = {e: sem(f"carry_{e}") for e in ("pe", "act", "dve", "pool", "sp")}
        s.barrier, s.fence = sem("phase_done"), sem("fence")
        s.const = sem("const_loaded")
        s.stage = [sem(f"stage_loaded{i}") for i in range(2)]
        s.w_hi, s.w_lo, s.pe_set, s.set_done = sem("w_hi"), sem("w_lo"), sem("pe_setup"), sem("setup_done")
        s.memz, s.w_raw, s.link0 = sem("wb_zeroed"), sem("w_s_w_2"), sem("pad_row_zero")
        names = ("stats1", "rs1", "z1", "y1", "T1", "zhi", "zlo", "U", "sigr", "gv", "sigs", "ghi", "glo", "Wo",
                 "x2", "stats2", "rs2", "z2", "T2", "hhi", "hlo", "bid", "bd", "bidT", "b7", "conf", "e", "pref",
                 "posr", "W", "g2", "g2hi", "g2lo", "W3", "rdone", "link", "plink", "n1", "flag", "padi",
                 "sT", "shi", "slo", "Ks", "relu", "hrhi", "sq", "hrlo", "kbs", "Vs", "orow")
        shared = {n: sem(f"f_{n}") for n in names}
        pairs = {n: [sem(f"f_{n}{k}") for k in range(2)] for n in ("x_in", "r_in", "s_in")}
        s.cleared = [*shared.values(), *(one for pair in pairs.values() for one in pair)]
        s.ffn = [dict(shared, **pairs, pad=sem(f"f{i}_pad"), scat=[sem(f"f{i}_scattered{k}") for k in range(2)],
                      o_out=[sem(f"f{i}_slot_out{k}") for k in range(2)]) for i in range(2)]
        names = ("stats", "rs", "z", "T", "zhi", "zlo", "vp", "vs", "vsum", "vhi", "vlo", "qk", "qkhi", "qklo", "S", "nb",
                 "exp", "PT", "pthi", "ptlo", "PV", "ohi", "olo", "Y", "y", "link", "plink")
        s.a = dict({n: sem(f"a_{n}") for n in names}, out=sem("a_out"), x_in=[sem(f"a_x_in{k}") for k in range(2)])

        block = ctx.enter_context(nc.Block())
        src = [x, b.x2]
        dst = [b.x1, out]

        def barrier(eng, k):
            eng.drain().then_inc(s.barrier, 1)
            eng.wait_ge(s.barrier, 5 * k)
            eng.sem_inc(s.fence, 1)

        loads = ([("w", w256, 4 * CC * C), ("sf", w_st, 3 * CC * C + CC * BIDS)]
                 + [("k", k_w[:, e], CC * HID) for e in range(2)] + [("v", v_w[:, e], HC * C) for e in range(2)]
                 + [("a", w_qkv, 3 * CC * DK + C)])
        SF = 3 * CC * C

        @block.sync
        def _(sp):
            c = b.carry["sp"]
            for dstv, srcv in ((b.ln, ln), (b.ident, ident), (b.trif, tri), (b.mask, mask), (b.tok, tok),
                               (b.slot_row, slot_row), (b.shares, shares)):
                sp.dma_start(dstv[:], srcv).then_inc(s.const, 16)
            for n, (_, w, cols) in enumerate(loads):
                if n >= 2:
                    sp.wait_ge(s.set_done, n - 1)
                sp.dma_start(b.stage[n % 2][:, 0:cols], w).then_inc(s.stage[n % 2], 16)
            barrier(sp, 1)
            for i in range(2):
                f = s.ffn[i]
                xg = src[i].rearrange("(g t p) c -> g p t c", t=GT, p=P)
                for g in range(2):
                    sp.dma_start(b.x[g][:], xg[g]).then_inc(f["x_in"][g], 16)
                with sp.Fori(0, NG // 2 - 1) as it:
                    for par in range(2):
                        g = it * 2 + 2 + par
                        hold(sp, f["z2"], g - 1, c)
                        sp.dma_start(b.x[par][:], xg[g]).then_inc(f["x_in"][par], 16)
                sp.wait_ge(f["z2"], NG - 1)
                sp.dma_start(b.x[0][:], xg[NG - 2]).then_inc(f["x_in"][0], 16)
                sp.wait_ge(f["x_in"][0], 16 * (NG // 2 + 1))
                barrier(sp, 2 + 3 * i)
                rg = b.routed[i].rearrange("(j t p) c -> j p t c", t=ST, p=P)

                def slot_in(j, p):
                    hold(sp, f["sT"], j - 1, c)
                    sp.dma_start(b.sz[p][:], rg[j][:, :, 0:C]).then_inc(f["s_in"][p], 16)
                    hold(sp, f["orow"], j - 1, c)
                    sp.dma_start(b.srow[p][:], rg[j][:, :, C:ROW]).then_inc(f["r_in"][p], 16)

                for j in range(2):
                    slot_in(j, j)
                with sp.Fori(0, (NSLOT - 3) // 2) as it:
                    for par in range(2):
                        slot_in(it * 2 + 2 + par, par)
                slot_in(NSLOT - 1, 0)
                barrier(sp, 3 + 3 * i)
                if i == 0:
                    for one in s.cleared:
                        sp.sem_clear(one)
                    attention_sync(sp, b, s.a)
                    barrier(sp, 4)

        @block.tensor
        def _(pe):
            setup_tensor(pe, b, s, loads, SF)
            barrier(pe, 1)
            for i in range(2):
                ffn_a_tensor(pe, b, s.ffn[i])
                barrier(pe, 2 + 3 * i)
                ffn_b_tensor(pe, b, s.ffn[i])
                barrier(pe, 3 + 3 * i)
                if i == 0:
                    attention_tensor(pe, b, s.a)
                    barrier(pe, 4)

        @block.scalar
        def _(act):
            setup_scalar(act, b, s, SF)
            barrier(act, 1)
            for i in range(2):
                ffn_a_scalar(act, b, s.ffn[i])
                barrier(act, 2 + 3 * i)
                ffn_b_scalar(act, b, s.ffn[i])
                barrier(act, 3 + 3 * i)
                if i == 0:
                    attention_scalar(act, b, s.a)
                    barrier(act, 4)

        @block.vector
        def _(dve):
            setup_vector(dve, b, s, SF)
            barrier(dve, 1)
            for i in range(2):
                ffn_a_vector(dve, b, s.ffn[i])
                barrier(dve, 2 + 3 * i)
                ffn_b_vector(dve, b, s.ffn[i])
                barrier(dve, 3 + 3 * i)
                if i == 0:
                    attention_vector(dve, b, s.a)
                    barrier(dve, 4)

        @block.gpsimd
        def _(pool):
            pool.memset(b.half[:], -0.5).then_inc(s.memz, 1)
            barrier(pool, 1)
            for i in range(2):
                ffn_a_gpsimd(pool, b, s.ffn[i], b.routed[i])
                barrier(pool, 2 + 3 * i)
                ffn_b_gpsimd(pool, b, s.ffn[i], dst[i])
                barrier(pool, 3 + 3 * i)
                if i == 0:
                    attention_gpsimd(pool, b, s.a)
                    barrier(pool, 4)



def split_plan(b, SF):
    plan = []
    st = b.stage
    w = st[0][:, 0:4 * CC * C].rearrange("p (m c n) -> p m c n", m=4, c=CC)
    for m, (to, row) in enumerate(((0, 0), (1, 0), (3, 2), (4, None))):
        for c in range(CC):
            plan.append((0, w[:, m, c], None if row is None else b.ln[:, row, c:c + 1],
                         b.W[0][:, to, c], b.W[1][:, to, c]))
    for c in range(CC):
        plan.append((1, b.raw_sf[:, c], b.ln[:, 0, c:c + 1], b.W[0][:, 2, c], b.W[1][:, 2, c]))
    sf = st[1]
    for c in range(CC):
        plan.append((1, b.raw_w3[:, c], None, b.W3[0][:, c], b.W3[1][:, c]))
    wb = sf[:, SF:SF + CC * BIDS].rearrange("p (c n) -> p c n", c=CC)
    for c in range(CC):
        plan.append((1, wb[:, c], b.ln[:, 2, c:c + 1], b.Wb[:, c, 0:BIDS], b.Wb[:, c, BIDS:2 * BIDS]))
    for e in range(2):
        k = st[e % 2][:, 0:CC * HID].rearrange("p (c n) -> p c n", c=CC)
        for c in range(CC):
            plan.append((2 + e, k[:, c], b.ln[:, 2, c:c + 1], b.K[0][:, e, c], b.K[1][:, e, c]))
    for e in range(2):
        v = st[e % 2][:, 0:HC * C].rearrange("p (h n) -> p h n", h=HC)
        plan.append((4 + e, v, None, b.V[0][:, e], b.V[1][:, e]))
    a = st[0]
    qkv = a[:, 0:3 * CC * DK].rearrange("p (m c n) -> p m c n", m=3, c=CC)
    for m in range(2):
        plan.append((6, qkv[:, m], None, b.Wqk[0][:, m], b.Wqk[1][:, m]))
    for c in range(CC):
        plan.append((6, qkv[:, 2, c], None, b.Wvv[:, c, 0:DK], b.Wvv[:, c, DK:2 * DK]))
    plan.append((6, a[:, 3 * CC * DK:3 * CC * DK + C], None, b.Wao[0][:], b.Wao[1][:]))
    return plan


def setup_scalar(act, b, s, SF):
    act.wait_ge(s.const, 16 * 7)
    act.wait_ge(s.memz, 3)
    load = -1
    for n, (ld, raw, scale, hi, _) in enumerate(split_plan(b, SF)):
        if ld != load:
            load = ld
            act.wait_ge(s.stage[ld % 2], 16 * (ld // 2 + 1))
            if ld == 1:
                act.wait_ge(s.pe_set, 2)
                act.copy(b.raw_sf[:, :, :], b.bank(1).rearrange("p (c n) -> p c n", c=CC)).then_inc(s.w_raw, 1)
                act.wait_ge(s.w_raw, 1)
        if scale is None:
            act.copy(hi, raw).then_inc(s.w_hi, 1)
        else:
            act.mul(hi, raw, scale).then_inc(s.w_hi, 1)


def setup_vector(dve, b, s, SF):
    dve.memset(b.Wb[:].bitcast(F32), 0.0).then_inc(s.memz, 1)
    dve.memset(b.bbias[:], 0.0).then_inc(s.memz, 1)
    dve.memset(b.ones4[:], 1.0)
    dve.memset(b.cnt[:], 0.0)
    dve.memset(b.padrow[:], 0.0).then_inc(s.link0, 1)
    dve.wait_ge(s.link0, 1)
    dve.memset(b.padrow[:, 2 * C + 1:ROW].bitcast(I32), ROWS)
    dve.wait_ge(s.const, 16 * 7)
    dve.tensor_copy(b.tri[:], b.trif[:])
    plan = split_plan(b, SF)
    for n, (ld, raw, scale, hi, lo) in enumerate(plan):
        dve.wait_ge(s.w_hi, n + 1)
        last = dve.scalar_tensor_tensor(lo, raw, 1.0 if scale is None else scale, hi.bitcast(F32), ALU.mult,
                                        ALU.subtract)
        if n + 1 == len(plan) or plan[n + 1][0] != ld:
            if ld == 0:
                dve.wait_ge(s.pe_set, 1)
                for m in (0, 1, 3):
                    last = dve.tensor_copy(b.bias[:, m, :], b.bank(0)[:, m * CC:(m + 1) * CC])
            elif ld == 1:
                dve.wait_ge(s.pe_set, 3)
                dve.wait_ge(s.memz, 3)
                dve.tensor_copy(b.bias[:, 2, :], b.bank(2)[:, 0:CC])
                last = dve.tensor_copy(b.bbias[0:BIDS, :], b.bank(2)[0:BIDS, 2 * CC:2 * CC + 1])
            elif ld in (2, 3):
                dve.wait_ge(s.pe_set, 2 + ld)
                last = dve.tensor_copy(b.kbias[:, ld - 2, :], b.bank(ld - 2)[:, 16:16 + HC])
            last.then_inc(s.set_done, 1)


def setup_tensor(pe, b, s, loads, SF):
    def column(bank, col, raw, m, row, size=P):
        for c in range(CC):
            mm = pe.matmul(bank[0:size, col:col + 1], raw(c)[:, m:m + size], b.ln[:, row, c:c + 1],
                           start=(c == 0), stop=(c == CC - 1))
        return mm

    pe.wait_ge(s.const, 16 * 7)
    pe.wait_ge(s.stage[0], 16)
    w = b.stage[0][:, 0:4 * CC * C].rearrange("p (m c n) -> p m c n", m=4, c=CC)
    for m, (to, row) in enumerate(((0, 1), (1, 1), (3, 3))):
        for f in range(CC):
            mm = column(b.bank(0), to * CC + f, lambda c, m=m: w[:, m, c], f * P, row)
    mm.then_inc(s.pe_set, 1)
    pe.wait_ge(s.stage[1], 16)
    sf = b.stage[1][:, 0:2 * CC * C].rearrange("p (m c n) -> p m c n", m=2, c=CC)
    for o in range(CC):
        for k in range(CC):
            mm = pe.matmul(b.bank(1)[:, o * C:(o + 1) * C], sf[:, 0, k, o * P:(o + 1) * P], sf[:, 1, k],
                           start=(k == 0), stop=(k == CC - 1))
    mm.then_inc(s.pe_set, 1)
    pe.wait_ge(s.w_raw, 1)
    for f in range(CC):
        column(b.bank(2), f, lambda c: b.raw_sf[:, c], f * P, 1)
    wb = b.stage[1][:, SF:SF + CC * BIDS].rearrange("p (c n) -> p c n", c=CC)
    column(b.bank(2), 2 * CC, lambda c: wb[:, c], 0, 3, BIDS).then_inc(s.pe_set, 1)
    for e in range(2):
        pe.wait_ge(s.stage[e], 32)
        k = b.stage[e][:, 0:CC * HID].rearrange("p (c n) -> p c n", c=CC)
        if e == 0:
            pe.wait_ge(s.set_done, 1)
        else:
            pe.wait_ge(s.set_done, 2)
        for h in range(HC):
            mm = column(b.bank(e), 16 + h, lambda c: k[:, c], h * P, 3)
        mm.then_inc(s.pe_set, 1)



def passes(pe, outv, w, m, n_first=True, n_last=True):
    for k, (pw, pm) in enumerate(PASSES):
        mm = pe.matmul(outv, w(pw), m(pm), start=(n_first and k == 0), stop=(n_last and k == 2))
    return mm


def ffn_a_tensor(pe, b, f):
    cr = b.carry["pe"]

    def T1(g):
        hold(pe, f["z1"], g + 1, cr)
        hold(pe, f["rdone"], g - 1, cr)
        for c in range(CC):
            for t in range(GT):
                mm = pe.transpose(b.bank(c)[:, t * P:(t + 1) * P], b.z[:, t, c * P:(c + 1) * P], b.ident[:])
        mm.then_inc(f["T1"], 1)

    def U(g):
        hold(pe, f["zlo"], 2 * g + 2, cr)
        for n, (m, fc) in enumerate(((0, 0), (1, 0), (0, 1), (1, 1), (2, 0), (2, 1))):
            if n == 0:
                hold(pe, f["bd"], g - 1, cr)
            if n == 1:
                hold(pe, f["g2"], g * 2 - 3, cr)
            if n == 2:
                hold(pe, f["g2"], g * 2 - 2, cr)
            if n == 3:
                hold(pe, f["sigr"], g * 2 + 1, cr)
            if n == 4:
                hold(pe, f["gv"], g * 2 + 1, cr)
            if n == 5:
                hold(pe, f["sigr"], g * 2 + 2, cr)
            for c in range(CC):
                mm = passes(pe, b.bank(2 + n % 3), lambda p: b.W[p][:, m, c, fc * P:(fc + 1) * P],
                            lambda p: b.zT[p][:, c], c == 0, c == CC - 1)
            mm.then_inc(f["U"], 1)

    def rows_out(g, act, w, bank0, done):
        for t in range(GT):
            for c in range(CC):
                mm = passes(pe, b.bank(bank0 + t // 2)[:, (t % 2) * C:(t % 2 + 1) * C],
                            lambda p: act[p][:, c, t * P:(t + 1) * P], lambda p: w(p, c), c == 0, c == CC - 1)
            if t % 2:
                mm.then_inc(done, 1)

    def Wo(g):
        hold(pe, f["glo"], 2 * g + 2, cr)
        hold(pe, f["hlo"], 2 * g, cr)
        rows_out(g, b.gT, lambda p, c: b.W[p][:, 4, c], 6, f["Wo"])

    def T2(g):
        hold(pe, f["z2"], g + 1, cr)
        hold(pe, f["x2"], 2 * g + 2, cr)
        for c in range(CC):
            for t in range(GT):
                mm = pe.transpose(b.bank(6 + c)[:, t * P:(t + 1) * P], b.rows[g_par(g)][:, t, c * P:(c + 1) * P],
                                  b.ident[:])
        mm.then_inc(f["T2"], 1)

    def bids(g):
        hold(pe, f["hlo"], 2 * g + 2, cr)
        hold(pe, f["gv"], gnext(g) * 2 + 2, cr)
        for c in range(CC):
            for p in range(2):
                mm = pe.matmul(b.bank(2), b.Wb[:, c], b.hT[p][:, c], start=(c == 0 and p == 0), stop=(c == 1 and p == 1))
        mm.then_inc(f["bid"], 1)

    def W1(g):
        for fc in range(CC):
            hold(pe, f["sigs"], gnext(g) * 2 + 1 + fc, cr)
            for c in range(CC):
                mm = passes(pe, b.bank(3 + fc), lambda p: b.W[p][:, 3, c, fc * P:(fc + 1) * P],
                            lambda p: b.hT[p][:, c], c == 0, c == CC - 1)
            mm.then_inc(f["W"], 1)

    def bidT(g):
        hold(pe, f["bd"], g + 1, cr)
        hold(pe, f["posr"], g, cr)
        for t in range(GT):
            mm = pe.transpose(b.bank(5)[:, t * P:(t + 1) * P], b.bd[:, t * P:(t + 1) * P], b.ident[:])
        mm.then_inc(f["bidT"], 1)

    def W3(g):
        hold(pe, f["g2lo"], 2 * g + 2, cr)
        hold(pe, f["zlo"], gnext(g) * 2 + 2, cr)
        rows_out(g, b.g2T, lambda p, c: b.W3[p][:, c], 0, f["W3"])

    def prefix(g):
        hold(pe, f["e"], g + 1, cr)
        pe.matmul(b.bank(5)[:, 0:GT], b.tri[:, 0], b.e16[:, 0:GT], start=True, stop=False)
        pe.matmul(b.bank(5)[:, 0:GT], b.tri[:, 1], b.e16[:, GT:2 * GT], start=False, stop=True).then_inc(f["pref"], 1)

    par = [0]

    def g_par(g):
        return par[0]

    def gnext(g):
        return g if isinstance(g, int) and g == NG - 1 else g + 1

    def body(g, p, last=False):
        par[0] = p
        if not last:
            T1(g + 1)
        T2(g)
        if not last:
            U(g + 1)
        bids(g)
        W1(g)
        bidT(g)
        if not last:
            Wo(g + 1)
        W3(g)
        prefix(g)

    T1(0)
    U(0)
    Wo(0)
    body(0, 0)
    with pe.Fori(0, (NG - 2) // 2) as it:
        for k in range(2):
            body(it * 2 + 1 + k, (1 + k) % 2)
    body(NG - 1, (NG - 1) % 2, True)
    pe.wait_ge(f["posr"], NG)
    pe.matmul(b.bank(5)[:, 0:1], b.tri[:, 1], b.e16[:, 2 * GT:2 * GT + 1], start=True, stop=True).then_inc(f["n1"], 1)


def ffn_a_scalar(act, b, f):
    cr = b.carry["act"]

    def y(g):
        hold(act, f["rs1"], g + 1, cr)
        hold(act, f["x2"], g * 2, cr)
        for t in range(GT):
            last = act.activation(b.y[:, t], b.x[par(g)][:, t], ACT.Identity, bias=b.rs[:, 0, 3, t:t + 1],
                                  scale=b.rs[:, 0, 1, t:t + 1])
        last.then_inc(f["y1"], 1)

    pp = [0]

    def par(g):
        return pp[0]

    def hi(g, T, bank, to, done, prev):
        hold(act, T, g + 1, cr)
        if prev is not None:
            hold(act, prev[0], prev[1], cr)
        for c in range(CC):
            act.copy(to[0][:, c], b.bank(bank + c)).then_inc(done, 1)

    def sig_r(g, fc):
        hold(act, f["U"], g * 6 + 1 + 2 * fc, cr)
        hold(act, f["glo"], g * 2, cr)
        act.activation(b.rg[:, fc], b.bank(2 + 2 * fc), ACT.Sigmoid, bias=b.bias[:, 0, fc:fc + 1]).then_inc(f["sigr"], 1)

    def g_hi(g, fc):
        hold(act, f["gv"], g * 2 + 1 + fc, cr)
        hold(act, f["Wo"], g * 2, cr)
        act.copy(b.gT[0][:, fc], b.rg[:, fc]).then_inc(f["ghi"], 1)

    def sig_s(g, fc):
        hold(act, f["U"], g * 6 + 5 + fc, cr)
        hold(act, f["g2lo"], g * 2 - 2, cr)
        act.activation(b.sg[pp[0]][:, fc], b.bank(3 + fc), ACT.Sigmoid, bias=b.bias[:, 2, fc:fc + 1]).then_inc(f["sigs"], 1)

    def bd(g):
        hold(act, f["bid"], g + 1, cr)
        hold(act, f["bidT"], g, cr)
        act.activation(b.bd[:, :], b.bank(2), ACT.Identity, bias=b.bbias[:, 0:1]).then_inc(f["bd"], 1)

    def conf(g):
        hold(act, f["b7"], g + 1, cr)
        act.activation(b.conf[:], b.bid[:, :, 0:4], ACT.Sigmoid).then_inc(f["conf"], 1)

    def g2_hi(g, fc, p):
        hold(act, f["g2"], g * 2 + 1 + fc, cr)
        if fc == 0:
            hold(act, f["W3"], g * 2, cr)
        act.copy(b.g2T[0][:, fc], b.sg[p][:, fc]).then_inc(f["g2hi"], 1)

    def first(g, p, mid=None):
        pp[0] = p
        hi(g, f["T1"], 0, b.zT, f["zhi"], (f["U"], g * 6))
        y(g)
        if mid:
            mid()
        sig_r(g, 0)
        sig_r(g, 1)
        g_hi(g, 0)
        g_hi(g, 1)
        sig_s(g, 0)
        sig_s(g, 1)

    def second(g, p):
        bd(g)
        conf(g)
        g2_hi(g, 0, p)
        g2_hi(g, 1, p)

    def h_hi(g):
        hi(g, f["T2"], 6, b.hT, f["hhi"], (f["W"], g * 2))

    first(0, 0)
    first(1, 1, lambda: h_hi(0))
    second(0, 0)
    with act.Fori(0, (NG - 2) // 2) as it:
        for k in range(2):
            g = it * 2 + 1 + k
            first(g + 1, k % 2, lambda: h_hi(g))
            second(g, (1 + k) % 2)
    h_hi(NG - 1)
    second(NG - 1, (NG - 1) % 2)


def ffn_a_gpsimd(pool, b, f, routed):
    cr = b.carry["pool"]
    n = [0]

    def link(ins, v):
        ins.then_inc(f["plink"], 1)
        n[0] += 1
        hold(pool, f["plink"], v(n[0]), cr)

    def rs1(g, v):
        hold(pool, f["stats1"], g + 1, cr)
        hold(pool, f["y1"], g, cr)
        mean, var = b.mv[:, 0, :, 0], b.mv[:, 0, :, 1]
        a, r1, r, sh = (b.rs[:, 0, k] for k in range(4))
        half = b.half[:, 0:GT]
        link(pool.tensor_scalar(a, var, EPS, 0.0, ALU.add, ALU.add), v)
        link(pool.tensor_tensor(r1, a, half, ALU.pow), v)
        link(pool.tensor_tensor(a, var, r1, ALU.mult), v)
        link(pool.tensor_tensor(a, a, r1, ALU.mult), v)
        link(pool.tensor_scalar(a, a, EPS, 0.0, ALU.add, ALU.add), v)
        link(pool.tensor_tensor(r, a, half, ALU.pow), v)
        link(pool.tensor_tensor(r, r, r1, ALU.mult), v)
        link(pool.tensor_tensor(sh, mean, r1, ALU.mult), v)
        pool.tensor_scalar(sh, sh, -1.0, 0.0, ALU.mult, ALU.add).then_inc(f["rs1"], 1)

    def rs2(g, v):
        hold(pool, f["stats2"], g + 1, cr)
        var, a, r = b.mv[:, 1, :, 1], b.rs[:, 1, 0], b.rs[:, 1, 1]
        link(pool.tensor_scalar(a, var, EPS, 0.0, ALU.add, ALU.add), v)
        pool.tensor_tensor(r, a, b.half[:, 0:GT], ALU.pow).then_inc(f["rs2"], 1)

    def lo(g, fc, src, to, hi_sem, done):
        hold(pool, hi_sem, g * 2 + 1 + fc, cr)
        pool.tensor_tensor(to[1][:, fc], src[:, fc], to[0][:, fc].bitcast(F32), ALU.subtract).then_inc(done, 1)

    def scatter(g, p):
        hold(pool, f["rdone"], g + 1, cr)
        hold(pool, f["posr"], g + 1, cr)
        for t in range(GT):
            pool.indirect_dma_start(routed, bass.IndirectOffsetOnAxis(b.posi[p][:, t:t + 1].bitcast(U32), 0),
                                    b.rows[p][:, t, :], None).then_inc(f["scat"][p], 16)

    def first(g):
        lo(g, 0, b.rg, b.gT, f["ghi"], f["glo"])
        lo(g, 1, b.rg, b.gT, f["ghi"], f["glo"])

    def second(g, p):
        lo(g, 0, b.sg[p], b.g2T, f["g2hi"], f["g2lo"])
        lo(g, 1, b.sg[p], b.g2T, f["g2hi"], f["g2lo"])

    PER = 9
    fixed = lambda k: k
    rs1(0, fixed)
    first(0)
    rs1(1, fixed)
    rs2(0, fixed)
    first(1)
    second(0, 0)
    rs2(1, fixed)
    rs1(2, fixed)
    scatter(0, 0)
    with pool.Fori(0, (NG - 2) // 2) as it:
        for k in range(2):
            g = it * 2 + 1 + k
            v = lambda q: it * (2 * PER) + q
            first(g + 1)
            second(g, (1 + k) % 2)
            rs2(g + 1, v)
            rs1(g + 2, v)
            scatter(g, (1 + k) % 2)
    second(NG - 1, (NG - 1) % 2)
    scatter(NG - 1, (NG - 1) % 2)
    pool.wait_ge(f["padi"], 1)
    for t in range(ST):
        pool.indirect_dma_start(routed, bass.IndirectOffsetOnAxis(b.padi[:, t:t + 1].bitcast(U32), 0),
                                b.padrow[:], None).then_inc(f["pad"], 16)
    pool.wait_ge(f["pad"], 16 * ST)
    for p in range(2):
        pool.wait_ge(f["scat"][p], 16 * GT * NG // 2)


def ffn_a_vector(dve, b, f):
    cr = b.carry["dve"]
    n = [0]
    pp = [0]

    def stats(which, src, g, done, v):
        for t in range(GT):
            last = dve.bn_stats(b.st[:, which, t], src[:, t])
        last.then_inc(f["link"], 1)
        n[0] += 1
        hold(dve, f["link"], v(n[0]), cr)
        for t in range(GT):
            last = dve.bn_aggr(b.mv[:, which, t], b.st[:, which, t])
        last.then_inc(done, 1)

    def link(ins, v):
        ins.then_inc(f["link"], 1)
        n[0] += 1
        hold(dve, f["link"], v(n[0]), cr)

    def norm1(g, p, v):
        hold(dve, f["x_in"][p], (g // 2 + 1) * 16 if isinstance(g, int) else x_count(g), cr)
        hold(dve, f["rs1"], g, cr)
        stats(0, b.x[p], g, f["stats1"], v)
        hold(dve, f["rs1"], g + 1, cr)
        hold(dve, f["T1"], g, cr)
        for t in range(GT):
            last = dve.tensor_scalar(b.z[:, t], b.x[p][:, t], b.mv[:, 0, t, 0:1], b.rs[:, 0, 2, t:t + 1],
                                     ALU.subtract, ALU.mult)
        last.then_inc(f["z1"], 1)

    xc = [None]

    def x_count(g):
        return xc[0]

    def lo(g, hi_sem, bank, to, done):
        for c in range(CC):
            hold(dve, hi_sem, g * 2 + 1 + c, cr)
            dve.tensor_tensor(to[1][:, c], b.bank(bank + c), to[0][:, c].bitcast(F32), ALU.subtract).then_inc(done, 1)

    def gv(g, fc):
        hold(dve, f["sigr"], g * 2 + 1 + fc, cr)
        hold(dve, f["U"], g * 6 + 2 + 2 * fc, cr)
        bank = b.bank(3 if fc == 0 else 2)
        dve.scalar_tensor_tensor(b.rg[:, fc], bank, b.bias[:, 1, fc:fc + 1], b.rg[:, fc], ALU.add,
                                 ALU.mult).then_inc(f["gv"], 1)

    def x2(g, p, v):
        hold(dve, f["y1"], g + 1, cr)
        for q in range(GT // 2):
            hold(dve, f["Wo"], g * 2 + 1 + q, cr)
            dve.tensor_tensor(b.xa[:, 2 * q:2 * q + 2], b.bank(6 + q).rearrange("p (t c) -> p t c", t=2),
                              b.y[:, 2 * q:2 * q + 2], ALU.add).then_inc(f["x2"], 1)
        hold(dve, f["x2"], g * 2 + 2, cr)
        hold(dve, f["z2"], g, cr)
        stats(1, b.xa, g, f["stats2"], v)
        if isinstance(g, int):
            hold(dve, f["scat"][p], 16 * GT * (g // 2), cr)
        else:
            hold(dve, f["scat"][p], sc[0], cr)
        dve.scalar_tensor_tensor(b.rows[p][:, :, C:2 * C], b.xa[:, :, :], 0.5, b.x[p][:, :, :], ALU.mult, ALU.add)
        hold(dve, f["rs2"], g + 1, cr)
        for t in range(GT):
            last = dve.tensor_scalar(b.rows[p][:, t, 0:C], b.xa[:, t], b.mv[:, 1, t, 0:1], b.rs[:, 1, 1, t:t + 1],
                                     ALU.subtract, ALU.mult)
        last.then_inc(f["z2"], 1)

    sc = [None]

    def gates(g, p, v, tokc):
        hold(dve, f["bidT"], g + 1, cr)
        raw = b.bank(5).rearrange("p (t k) -> p t k", t=GT)
        link(dve.tensor_copy(b.bid[:], raw[:, :, BIDS:2 * BIDS]), v)
        dve.tensor_tensor(b.bid[:], raw[:, :, 0:BIDS], b.bid[:], ALU.add).then_inc(f["b7"], 1)
        w = lambda k: b.gw[:, k]
        hold(dve, f["conf"], g + 1, cr)
        for e in range(3):
            last = dve.scalar_tensor_tensor(w(e), b.conf[:, :, e], b.shares[:, e:e + 1], b.conf[:, :, 3], ALU.mult,
                                            ALU.mult)
        link(last, v)
        for e in range(3):
            last = dve.tensor_tensor(w(e), w(e), b.bid[:, :, 4 + e], ALU.add)
        link(last, v)
        dve.tensor_tensor(w(3), w(1), w(0), ALU.is_gt)
        dve.tensor_tensor(w(4), w(0), w(1), ALU.max)
        link(dve.tensor_tensor(w(6), b.conf[:, :, 1], b.conf[:, :, 0], ALU.subtract), v)
        dve.tensor_tensor(w(5), w(2), w(4), ALU.is_gt)
        link(dve.tensor_tensor(w(6), w(6), w(3), ALU.mult), v)
        dve.tensor_copy(b.e16[:, 0:GT], w(3))
        link(dve.tensor_copy(b.cnt[:, 0:1], b.cnt[:, GT:GT + 1]), v)
        link(dve.tensor_tensor_scan(b.cnt[:, 1:GT + 1], b.ones4[:], w(3), b.cnt[:, 0:1], ALU.mult, ALU.add), v)
        dve.tensor_copy(b.e16[:, 2 * GT:2 * GT + 1], b.cnt[:, GT:GT + 1])
        dve.tensor_copy(b.e16[:, GT:2 * GT], b.cnt[:, 0:GT]).then_inc(f["e"], 1)
        link(dve.tensor_tensor(w(6), w(6), b.conf[:, :, 0], ALU.add), v)
        link(dve.tensor_tensor(w(7), b.conf[:, :, 2], w(6), ALU.subtract), v)
        link(dve.tensor_tensor(w(7), w(7), w(5), ALU.mult), v)
        link(dve.tensor_tensor(w(7), w(7), w(6), ALU.add), v)
        link(dve.tensor_scalar(w(8), w(7), 1e-6, None, ALU.add), v)
        link(dve.reciprocal(w(9), w(8)), v)
        link(dve.scalar_tensor_tensor(w(10), w(7), 0.5, w(9), ALU.mult, ALU.mult), v)
        link(dve.tensor_tensor(b.gt[p][:], w(10), w(5), ALU.mult), v)
        dve.tensor_tensor(b.rows[p][:, :, 2 * C], w(10), b.gt[p][:], ALU.subtract)
        dve.tensor_copy(b.rows[p][:, :, 2 * C + 1].bitcast(I32), b.tok[:, 0, tokc])
        link(dve.tensor_tensor(w(9), w(3), b.tok[:, 1, tokc], ALU.mult), v)
        link(dve.tensor_tensor(w(11), w(9), b.tok[:, 0, tokc], ALU.add), v)
        hold(dve, f["pref"], g + 1, cr)
        dve.tensor_tensor(b.posi[p][:], w(11), b.bank(5)[:, 0:GT], ALU.subtract).then_inc(f["posr"], 1)

    def g2(g, p):
        for fc in range(CC):
            hold(dve, f["W"], g * 2 + 1 + fc, cr)
            dve.scalar_tensor_tensor(b.sg[p][:, fc], b.bank(3 + fc), b.bias[:, 3, fc:fc + 1], b.sg[p][:, fc],
                                     ALU.add, ALU.mult).then_inc(f["g2"], 1)

    def w3(g, p):
        for t in range(GT):
            if t % 2 == 0:
                hold(dve, f["W3"], g * 2 + 1 + t // 2, cr)
            last = dve.scalar_tensor_tensor(b.rows[p][:, t, C:2 * C], b.bank(t // 2)[:, (t % 2) * C:(t % 2 + 1) * C],
                                            b.gt[p][:, t:t + 1], b.rows[p][:, t, C:2 * C], ALU.mult, ALU.add)
        last.then_inc(f["rdone"], 1)

    fixed = lambda k: k

    def body(g, p, v, tokc, last=False):
        q = 1 - p
        if not last:
            lo(g + 1, f["zhi"], 0, b.zT, f["zlo"])
        lo(g, f["hhi"], 6, b.hT, f["hlo"])
        if not last:
            gv(g + 1, 0)
            gv(g + 1, 1)
        g2(g, p)
        gates(g, p, v, tokc)
        if not last:
            x2(g + 1, q, v)
        w3(g, p)
        if not last:
            norm1(g + 2, p, v)

    norm1(0, 0, fixed)
    lo(0, f["zhi"], 0, b.zT, f["zlo"])
    gv(0, 0)
    gv(0, 1)
    norm1(1, 1, fixed)
    x2(0, 0, fixed)
    body(0, 0, fixed, slice(0, GT))
    start = n[0]
    with dve.Fori(0, (NG - 2) // 2) as it:
        per = [0]
        for k in range(2):
            g = it * 2 + 1 + k
            xc[0] = it * 16 + 16 * ((3 + k) // 2 + 1)
            sc[0] = it * (16 * GT) + 16 * GT * ((2 + k) // 2)
            v = (lambda q: it * LINKS + q)
            body(g, (1 + k) % 2, v, bass.ds(g * GT, GT))
        assert n[0] - start == LINKS, n[0] - start
    n[0] = start + LINKS * ((NG - 2) // 2)
    body(NG - 1, (NG - 1) % 2, fixed, slice((NG - 1) * GT, NG * GT), True)
    dve.wait_ge(f["n1"], 1)
    link(dve.tensor_copy(b.n1[:], b.bank(5)[:, 0:1]), fixed)
    dve.tensor_scalar(b.padi[:], b.slot_row[:, NSLOT:NSLOT + ST], b.n1[:, 0:1], None, ALU.subtract).then_inc(f["padi"], 1)
    link(dve.tensor_scalar(b.flag[:], b.slot_row[:, 0:NSLOT], b.n1[:, 0:1], float(N), ALU.add, ALU.is_ge), fixed)
    dve.tensor_scalar(b.nflag[:], b.flag[:], -1.0, 1.0, ALU.mult, ALU.add)
    dve.tensor_copy(b.flagi[:], b.flag[:])
    dve.memset(b.cnt[:], 0.0).then_inc(f["flag"], 1)
    b.link_total = n[0]


LINKS = 38



def slots(eng, first, body):
    first()
    for j in (1, 2):
        body(j, j % 2, False)
    with eng.Fori(0, (NSLOT - 5) // 2) as it:
        for k in range(2):
            body(it * 2 + 3 + k, (3 + k) % 2, False)
    for j in (NSLOT - 2, NSLOT - 1):
        body(j, j % 2, j == NSLOT - 1)


def ffn_b_tensor(pe, b, f):
    cr = b.carry["pe"]

    def sT(j, p, loads):
        hold(pe, f["s_in"][p], loads * 16, cr)
        hold(pe, f["slo"], j, cr)
        for c in range(CC):
            for t in range(ST):
                mm = pe.transpose(b.bank(0)[:, c * SLOT + t * P:c * SLOT + (t + 1) * P],
                                  b.sz[p][:, t, c * P:(c + 1) * P], b.ident[:])
        mm.then_inc(f["sT"], 1)

    def K(j, e):
        for q in range(HC // 2):
            hold(pe, f["relu"], j * 4 - 3 + q, cr)
            for h in (2 * q, 2 * q + 1):
                for c in range(CC):
                    mm = passes(pe, b.bank(1 + q)[:, (h % 2) * SLOT:(h % 2 + 1) * SLOT],
                                lambda p: b.K[p][:, e, c, h * P:(h + 1) * P], lambda p: b.shT[p][:, c], c == 0,
                                c == CC - 1)
            mm.then_inc(f["Ks"], 1)

    def V(j, p, e):
        for t in range(ST):
            for h in range(HC):
                mm = passes(pe, b.bank(5)[:, t * C:(t + 1) * C], lambda q: b.hr[p][q][:, h, t * P:(t + 1) * P],
                            lambda q: b.V[q][:, e, h], h == 0, h == HC - 1)
        mm.then_inc(f["Vs"], 1)

    def either(j, run):
        e = pe.value_load(b.flagi[0:1, bass.ds(j, 1)], min_val=0, max_val=1)
        with pe.If(e < 1):
            run(0)
        with pe.Else():
            run(1)

    def Kj(j):
        hold(pe, f["slo"], j + 1, cr)
        either(j, lambda e: K(j, e))

    def Vj(j, p):
        hold(pe, f["hrlo"], j * 4 + 4, cr)
        hold(pe, f["orow"], j, cr)
        either(j, lambda e: V(j, p, e))

    def first():
        sT(0, 0, 1)
        Kj(0)
        sT(1, 1, 1)

    def body(j, p, last):
        Kj(j)
        if not last:
            sT(j + 1, 1 - p, (j + 1) // 2 + 1 if isinstance(j, int) else loads_of(j, p))
        Vj(j - 1, 1 - p)

    def loads_of(j, p):
        return half[0] + (1 if p else 0)

    half = [None]
    first()
    for j in (1, 2):
        body(j, j % 2, False)
    with pe.Fori(0, (NSLOT - 5) // 2) as it:
        for k in range(2):
            half[0] = it + 2 if k == 0 else it + 3
            body(it * 2 + 3 + k, (3 + k) % 2, False)
    for j in (NSLOT - 2, NSLOT - 1):
        body(j, j % 2, j == NSLOT - 1)
    Vj(NSLOT - 1, (NSLOT - 1) % 2)


def ffn_b_scalar(act, b, f):
    cr = b.carry["act"]

    def shi(j):
        hold(act, f["sT"], j + 1, cr)
        hold(act, f["Ks"], j * 4, cr)
        act.copy(b.shT[0][:, :, :], b.bank(0).rearrange("p (c n) -> p c n", c=CC)).then_inc(f["shi"], 1)

    def relu(j, p):
        hold(act, f["kbs"], j + 1, cr)
        for q in range(HC // 2):
            hold(act, f["Ks"], j * 4 + q + 1, cr)
            if q >= 2 or not (isinstance(j, int) and j == 0):
                hold(act, f["sq"], j * 4 + q - 1, cr)
            for h in (2 * q, 2 * q + 1):
                last = act.activation(b.r[q % 2][:, (h % 2) * SLOT:(h % 2 + 1) * SLOT],
                                      b.bank(1 + q)[:, (h % 2) * SLOT:(h % 2 + 1) * SLOT], ACT.Relu,
                                      bias=b.kbs[p][:, h:h + 1])
            last.then_inc(f["relu"], 1)
            hold(act, f["relu"], j * 4 + q + 1, cr)
            if q == 0:
                hold(act, f["Vs"], j - 1, cr)
            act.activation(b.hr[p][0][:, 2 * q:2 * q + 2].rearrange("p h n -> p (h n)"), b.r[q % 2][:, :],
                           ACT.Square).then_inc(f["hrhi"], 1)

    def first():
        shi(0)
        relu(0, 0)
        shi(1)

    def body(j, p, last):
        relu(j, p)
        if not last:
            shi(j + 1)

    slots(act, first, body)


def ffn_b_vector(dve, b, f):
    cr = b.carry["dve"]

    def kbs(j, p):
        hold(dve, f["relu"], j * 4 - 4, cr)
        hold(dve, f["kbs"], j, cr)
        at = slice(j, j + 1) if isinstance(j, int) else bass.ds(j, 1)
        dve.tensor_scalar(b.kbt[:], b.kbias[:, 0], b.nflag[:, at], None, ALU.mult).then_inc(f["link"], 1)
        n[0] += 1
        hold(dve, f["link"], n[0] if isinstance(j, int) else base[0] + n[0], cr)
        dve.scalar_tensor_tensor(b.kbs[p][:], b.kbias[:, 1], b.flag[:, at], b.kbt[:], ALU.mult,
                                 ALU.add).then_inc(f["kbs"], 1)

    def slo(j):
        hold(dve, f["shi"], j + 1, cr)
        dve.tensor_tensor(b.shT[1][:, :, :], b.bank(0).rearrange("p (c n) -> p c n", c=CC),
                          b.shT[0][:, :, :].bitcast(F32), ALU.subtract).then_inc(f["slo"], 1)

    def sq(j, p):
        for q in range(HC // 2):
            hold(dve, f["relu"], j * 4 + q + 1, cr)
            if q >= 2 or not (isinstance(j, int) and j == 0):
                hold(dve, f["hrlo"], j * 4 + q - 1, cr)
            dve.tensor_tensor(b.sq[q % 2][:, :], b.r[q % 2][:, :], b.r[q % 2][:, :], ALU.mult).then_inc(f["sq"], 1)

    def orow(j, p, uses):
        hold(dve, f["Vs"], j + 1, cr)
        hold(dve, f["o_out"][p], uses * 16 * ST, cr)
        hold(dve, f["r_in"][p], uses * 16 + 16, cr)
        dve.tensor_copy(b.idx[p][:], b.srow[p][:, :, C + 1].bitcast(I32))
        for t in range(ST):
            last = dve.scalar_tensor_tensor(b.o[p][:, t], b.bank(5)[:, t * C:(t + 1) * C],
                                            b.srow[p][:, t, C:C + 1], b.srow[p][:, t, 0:C], ALU.mult,
                                            ALU.add)
        last.then_inc(f["orow"], 1)

    n, base = [b.link_total], [0]

    def body(j, p, last, uses):
        if not last:
            kbs(j + 1, 1 - p)
        sq(j, p)
        if not last:
            slo(j + 1)
        orow(j - 1, 1 - p, uses)

    kbs(0, 0)
    slo(0)
    kbs(1, 1)
    sq(0, 0)
    slo(1)
    for j in (1, 2):
        body(j, j % 2, False, 0)
    n0 = n[0]
    with dve.Fori(0, (NSLOT - 5) // 2) as it:
        base[0] = it * 2
        for k in range(2):
            body(it * 2 + 3 + k, (3 + k) % 2, False, it + 1)
    n[0] = n0 + NSLOT - 5
    for j in (NSLOT - 2, NSLOT - 1):
        body(j, j % 2, j == NSLOT - 1, (j - 1) // 2)
    orow(NSLOT - 1, (NSLOT - 1) % 2, (NSLOT - 1) // 2)


def ffn_b_gpsimd(pool, b, f, dst):
    cr = b.carry["pool"]

    def hrlo(j, p):
        for q in range(HC // 2):
            hold(pool, f["hrhi"], j * 4 + q + 1, cr)
            hold(pool, f["sq"], j * 4 + q + 1, cr)
            pool.tensor_tensor(b.hr[p][1][:, 2 * q:2 * q + 2].rearrange("p h n -> p (h n)"), b.sq[q % 2][:, :],
                               b.hr[p][0][:, 2 * q:2 * q + 2].rearrange("p h n -> p (h n)").bitcast(F32),
                               ALU.subtract).then_inc(f["hrlo"], 1)

    def send(j, p):
        hold(pool, f["orow"], j + 1, cr)
        for t in range(ST):
            pool.indirect_dma_start(dst, bass.IndirectOffsetOnAxis(b.idx[p][:, t:t + 1].bitcast(U32), 0),
                                    b.o[p][:, t, :], None, bounds_check=N - 1, oob_is_err=False
                                    ).then_inc(f["o_out"][p], 16)

    def body(j, p, last):
        hrlo(j, p)
        send(j - 1, 1 - p)

    slots(pool, lambda: hrlo(0, 0), body)
    send(NSLOT - 1, (NSLOT - 1) % 2)
    pool.wait_ge(f["o_out"][0], 16 * ST * ((NSLOT + 1) // 2))
    pool.wait_ge(f["o_out"][1], 16 * ST * (NSLOT // 2))




def att_sizes(q):
    return (q + 1) * SLOT, (q + 1) * ST


def key_pairs_before(q):
    return q * (q + 1) // 2


PAIRS = key_pairs_before(QB)


def attention_sync(sp, b, a):
    cr = b.carry["sp"]
    xin = b.x1.rearrange("(n t p) c -> n p t c", t=ST, p=P)
    xout = b.x2.rearrange("(n t p) c -> n p t c", t=ST, p=P)

    def load(n, q):
        hold(sp, a["y"], n - 1, cr)
        sp.dma_start(b.ax[q % 2][:], xin[n]).then_inc(a["x_in"][q % 2], 16)

    def store(n):
        hold(sp, a["y"], n + 1, cr)
        sp.dma_start(xout[n], b.ao[:]).then_inc(a["out"], 16)

    for n in range(BATCH * QB + 1):
        if n < BATCH * QB:
            load(n, n)
        if n >= 1:
            store(n - 1)
    sp.wait_ge(a["out"], 16 * BATCH * QB)


def attention_tensor(pe, b, a):
    cr = b.carry["pe"]

    def project(n, q):
        hold(pe, a["z"], n + 1, cr)
        hold(pe, a["olo"], max(n - 1, 0), cr)
        for c in range(CC):
            for t in range(ST):
                mm = pe.transpose(b.bank(2)[:, c * SLOT + t * P:c * SLOT + (t + 1) * P],
                                  b.az[:, t, c * P:(c + 1) * P], b.ident[:])
        mm.then_inc(a["T"], 1)
        hold(pe, a["zlo"], n + 1, cr)
        hold(pe, a["y"], n - 1, cr)
        for t in range(ST):
            for c in range(CC):
                for p in range(2):
                    mm = pe.matmul(b.bank(3)[:, t * C:(t + 1) * C], b.azT[p][:, c, t * P:(t + 1) * P], b.Wvv[:, c],
                                   start=(c == 0 and p == 0), stop=(c == 1 and p == 1))
        mm.then_inc(a["vp"], 1)
        for m in range(2):
            for c in range(CC):
                mm = passes(pe, b.bank(2)[:, m * SLOT:(m + 1) * SLOT], lambda p: b.Wqk[p][:, m, c],
                            lambda p: b.azT[p][:, c], c == 0, c == CC - 1)
        mm.then_inc(a["qk"], 1)

    def scores(n, q, t):
        hold(pe, a["qklo"], n + 1, cr)
        hold(pe, a["exp"], 2 * n + t, cr)
        keys = att_sizes(q)[0]
        for k0 in range(0, keys, 512):
            w = min(512, keys - k0)
            mm = passes(pe, b.bank(4 + k0 // 512)[:, 0:w], lambda p: b.qT[p][:, t * P:(t + 1) * P],
                        lambda p: b.kT[p][:, k0:k0 + w])
        mm.then_inc(a["S"], 1)

    def transpose_pair(n, q, j, m):
        hold(pe, a["ptlo"], m - 1, cr)
        for kt in range(2):
            for t in range(ST):
                mm = pe.transpose(b.bank(m % 2)[:, kt * SLOT + t * P:kt * SLOT + (t + 1) * P],
                                  b.p[1 - q % 2][:, t, (2 * j + kt) * P:(2 * j + kt + 1) * P], b.ident[:])
        mm.then_inc(a["PT"], 1)

    def weigh_pair(n, q, j, m):
        hold(pe, a["ptlo"], m + 1, cr)
        for kt in range(2):
            mm = passes(pe, b.bank(2)[:, 0:SLOT], lambda p: b.v[p][:, 2 * j + kt],
                        lambda p: b.pT[m % 2][p][:, kt], j == 0 and kt == 0, j == q and kt == 1)
        mm.then_inc(a["PV"], 1)

    def attend(n, q):
        m0 = (n // QB) * PAIRS + key_pairs_before(q)
        hold(pe, a["exp"], 2 * n + 2, cr)
        transpose_pair(n, q, 0, m0)
        for j in range(q + 1):
            if j < q:
                transpose_pair(n, q, j + 1, m0 + j + 1)
            if j == 0:
                hold(pe, a["qklo"], min(n + 2, BATCH * QB) if q < QB - 1 else n + 1, cr)
            weigh_pair(n, q, j, m0 + j)

    def output(n, q):
        hold(pe, a["olo"], n + 1, cr)
        hold(pe, a["vlo"], n + 2 if q < QB - 1 else n + 1, cr)
        for t in range(ST):
            mm = passes(pe, b.bank(3)[:, t * C:(t + 1) * C], lambda p: b.oT[p][:, t * P:(t + 1) * P],
                        lambda p: b.Wao[p][:])
        mm.then_inc(a["Y"], 1)

    for bt in range(BATCH):
        for q in range(QB + 1):
            n = bt * QB + q
            if q < QB:
                project(n, q)
                scores(n, q, 0)
            if q >= 1:
                attend(n - 1, q - 1)
            if q < QB:
                scores(n, q, 1)
            if q >= 1:
                output(n - 1, q - 1)


def attention_scalar(act, b, a):
    cr = b.carry["act"]

    def project(n, q):
        hold(act, a["T"], n + 1, cr)
        act.copy(b.azT[0][:, :, :], b.bank(2).rearrange("p (c n) -> p c n", c=CC)).then_inc(a["zhi"], 1)
        hold(act, a["vp"], n + 1, cr)
        hold(act, a["vsum"], n, cr)
        act.copy(b.vs[:, :, :], b.bank(3).rearrange("p (t n) -> p t n", t=ST)[:, :, 0:DK]).then_inc(a["vs"], 1)
        hold(act, a["qk"], n + 1, cr)
        hold(act, a["S"], 2 * n, cr)
        act.copy(b.qT[0][:, :], b.bank(2)[:, 0:SLOT])
        act.copy(b.kT[0][:, q * SLOT:(q + 1) * SLOT], b.bank(2)[:, SLOT:2 * SLOT]).then_inc(a["qkhi"], 1)
        hold(act, a["vsum"], n + 1, cr)
        act.copy(b.v[0][:, 2 * q:2 * q + 2], b.vt[:, :, :]).then_inc(a["vhi"], 1)

    def expo(n, q, t):
        keys = att_sizes(q)[0]
        hold(act, a["nb"], 2 * n + t + 1, cr)
        if n >= 2:
            hold(act, a["PT"], (n // QB) * PAIRS + key_pairs_before(q) - (q if q >= 1 else 0), cr)
        act.activation(b.p[1 - q % 2][:, t, 0:keys], b.ps4[:, :, :].rearrange("p a n -> p (a n)")[:, 0:keys], ACT.Exp,
                       bias=b.mx[:, 4 + n % 2, t:t + 1], scale=SCALE,
                       accum_out=b.sum[:, n % 2, t:t + 1]).then_inc(a["exp"], 1)

    def pair(m):
        hold(act, a["PT"], m + 1, cr)
        hold(act, a["PV"], m - 1, cr)
        act.copy(b.pT[m % 2][0][:, :, :], b.bank(m % 2).rearrange("p (k n) -> p k n", k=2)).then_inc(a["pthi"], 1)

    def o_hi(n):
        m_end = (n // QB) * PAIRS + key_pairs_before(n % QB + 1)
        hold(act, a["PV"], m_end, cr)
        hold(act, a["Y"], n, cr)
        act.copy(b.oT[0][:, :], b.bank(2)[:, 0:SLOT]).then_inc(a["ohi"], 1)

    for bt in range(BATCH):
        for q in range(QB + 1):
            n = bt * QB + q
            if q < QB:
                project(n, q)
                expo(n, q, 0)
            if q >= 1:
                m0 = bt * PAIRS + key_pairs_before(q - 1)
                for j in range(q):
                    pair(m0 + j)
                o_hi(n - 1)
            if q < QB:
                expo(n, q, 1)


def attention_vector(dve, b, a):
    cr = b.carry["dve"]
    links = [0]

    def link(ins):
        ins.then_inc(a["link"], 1)
        links[0] += 1
        dve.wait_ge(a["link"], links[0])

    def norm(n, q):
        x = b.ax[q % 2]
        hold(dve, a["x_in"][q % 2], (n // 2 + 1) * 16, cr)
        for t in range(ST):
            last = dve.bn_stats(b.st[:, 0, t], x[:, t])
        link(last)
        for t in range(ST):
            last = dve.bn_aggr(b.mv[:, 0, t], b.st[:, 0, t])
        last.then_inc(a["stats"], 1)
        hold(dve, a["rs"], n + 1, cr)
        hold(dve, a["T"], n, cr)
        for t in range(ST):
            last = dve.tensor_scalar(b.az[:, t], x[:, t], b.mv[:, 0, t, 0:1], b.rs[:, 1, 1, t:t + 1], ALU.subtract,
                                     ALU.mult)
        last.then_inc(a["z"], 1)

    def project(n, q):
        hold(dve, a["zhi"], n + 1, cr)
        dve.tensor_tensor(b.azT[1][:, :, :], b.bank(2).rearrange("p (c n) -> p c n", c=CC),
                          b.azT[0][:, :, :].bitcast(F32), ALU.subtract).then_inc(a["zlo"], 1)
        hold(dve, a["vs"], n + 1, cr)
        hold(dve, a["vlo"], n, cr)
        dve.tensor_tensor(b.vt[:, :, :], b.bank(3).rearrange("p (t n) -> p t n", t=ST)[:, :, DK:2 * DK], b.vs[:, :, :],
                          ALU.add).then_inc(a["vsum"], 1)
        hold(dve, a["qkhi"], n + 1, cr)
        dve.tensor_tensor(b.qT[1][:, :], b.bank(2)[:, 0:SLOT], b.qT[0][:, :].bitcast(F32), ALU.subtract)
        at = slice(q * SLOT, (q + 1) * SLOT)
        dve.tensor_tensor(b.kT[1][:, at], b.bank(2)[:, SLOT:2 * SLOT], b.kT[0][:, at].bitcast(F32),
                          ALU.subtract).then_inc(a["qklo"], 1)
        hold(dve, a["vhi"], n + 1, cr)
        dve.tensor_tensor(b.v[1][:, 2 * q:2 * q + 2], b.vt[:, :, :], b.v[0][:, 2 * q:2 * q + 2].bitcast(F32),
                          ALU.subtract).then_inc(a["vlo"], 1)

    def maxima(n, q, t):
        keys = att_sizes(q)[0]
        s = b.ps4[:, :, :].rearrange("p a n -> p (a n)")
        hold(dve, a["S"], 2 * n + t + 1, cr)
        link(dve.tensor_tensor(s[:, keys - SLOT:keys], s[:, keys - SLOT:keys], b.mask[:, t], ALU.add))
        link(dve.tensor_reduce(b.mx[:, 0, t:t + 1], s[:, 0:keys], AX.X, ALU.max))
        hold(dve, a["exp"], 2 * n + t - 2, cr)
        dve.tensor_scalar(b.mx[:, 4 + n % 2, t:t + 1], b.mx[:, 0, t:t + 1], -SCALE, None, ALU.mult).then_inc(a["nb"], 1)

    def pair(m):
        hold(dve, a["pthi"], m + 1, cr)
        dve.tensor_tensor(b.pT[m % 2][1][:, :, :], b.bank(m % 2).rearrange("p (k n) -> p k n", k=2),
                          b.pT[m % 2][0][:, :, :].bitcast(F32), ALU.subtract).then_inc(a["ptlo"], 1)

    def o_lo(n):
        hold(dve, a["ohi"], n + 1, cr)
        dve.tensor_tensor(b.oT[1][:, :], b.bank(2)[:, 0:SLOT], b.oT[0][:, :].bitcast(F32),
                          ALU.subtract).then_inc(a["olo"], 1)

    def y(n, q):
        link(dve.reciprocal(b.mx[:, 2, :], b.sum[:, n % 2, :]))
        hold(dve, a["Y"], n + 1, cr)
        hold(dve, a["out"], 16 * n, cr)
        for t in range(ST):
            last = dve.scalar_tensor_tensor(b.ao[:, t], b.bank(3)[:, t * C:(t + 1) * C], b.mx[:, 2, t:t + 1],
                                            b.ax[q % 2][:, t], ALU.mult, ALU.add)
        last.then_inc(a["y"], 1)

    norm(0, 0)
    for bt in range(BATCH):
        for q in range(QB + 1):
            n = bt * QB + q
            if q < QB:
                project(n, q)
                maxima(n, q, 0)
            if q >= 1:
                m0 = bt * PAIRS + key_pairs_before(q - 1)
                for j in range(q):
                    pair(m0 + j)
                o_lo(n - 1)
            if q < QB:
                maxima(n, q, 1)
            if q >= 1:
                y(n - 1, q - 1)
            if q < QB and n + 1 < BATCH * QB:
                norm(n + 1, q + 1)


def attention_gpsimd(pool, b, a):
    for n in range(BATCH * QB):
        pool.wait_ge(a["stats"], n + 1)
        var, t, r = (v[:, 0:ST] for v in (b.mv[:, 0, :, 1], b.rs[:, 1, 0], b.rs[:, 1, 1]))
        if n >= 1:
            pool.wait_ge(a["z"], n)
        pool.tensor_scalar(t, var, EPS, 0.0, ALU.add, ALU.add).then_inc(a["plink"], 1)
        pool.wait_ge(a["plink"], n + 1)
        pool.tensor_tensor(r, t, b.half[:, 0:ST], ALU.pow).then_inc(a["rs"], 1)



def laid_out(inp):
    def chunks(w, k=CC):
        return w.reshape(k, P, -1).transpose(1, 0, 2).reshape(P, -1)

    g = lambda n: np.asarray(inp[n])
    f = "L0_ffn_"
    bid = np.zeros((C, BIDS), np.float32)
    bid[:, 0:2] = g(f + "conf_rwkv").T
    bid[:, 2] = g(f + "conf_trans")
    bid[:, 3] = g(f + "w_diff")
    bid[:, 4:7] = g(f + "W_aff")
    t = np.arange(N, dtype=np.float32).reshape(N // P, P).T
    k = np.arange(P)
    tri = np.stack([(k[:, None] < k[None, :]), np.ones((P, P), bool)], 1).astype(np.float32)
    mask = np.zeros((P, ST, SLOT), np.float32)
    for i in range(ST):
        mask[:, i] = np.where(np.arange(SLOT)[None, :] > k[:, None] + i * P, np.float32(-3e38), np.float32(0))
    slot_row = np.zeros((P, NSLOT + ST), np.float32)
    slot_row[:, 0:NSLOT] = np.arange(NSLOT) * SLOT
    slot_row[:, NSLOT:] = N + k[:, None] + P * np.arange(ST)
    return {
        "x": g("L0_attn_x").reshape(N, C),
        "w256": np.concatenate([chunks(g(f + n)) for n in ("Wr", "Wv", "W1", "Wo")], 1),
        "w_st": np.concatenate([chunks(g(f + "Ws").T), chunks(g(f + "W2")), chunks(g(f + "W3")), chunks(bid)], 1),
        "k_w": np.stack([chunks(g(f + "K_rwkv")[e]) for e in range(2)], 1),
        "v_w": np.stack([chunks(g(f + "V_rwkv")[e], HC) for e in range(2)], 1),
        "w_qkv": np.concatenate([chunks(g("L0_attn_" + n)) for n in ("Wq", "Wk", "Wv")] + [g("L0_attn_Wo")], 1),
        "ln": np.concatenate([g(f + n).reshape(CC, P).T for n in ("ln1_w", "ln1_b", "ln2_w", "ln2_b")], 1
                             ).reshape(P, 4, CC),
        "shares": np.broadcast_to(g(f + "capital_shares")[None, :], (P, 3)),
        "ident": np.eye(P, dtype=np.float32),
        "tri": tri,
        "mask": mask,
        "tok": np.stack([t, ROWS - 1 - t], 1),
        "slot_row": slot_row,
    }


def kernel(**inputs):
    import concourse.bacc as bacc
    from concourse.bass_utils import run_bass_kernel_spmd as run

    nc = bacc.Bacc("TRN2", target_bir_lowering=False, num_devices=1)
    arrays, args = {}, {}
    for name, v in laid_out(inputs).items():
        v = np.ascontiguousarray(v)
        arrays[f"in_{name}"] = v
        args[name] = nc.dram_tensor(f"in_{name}", v.shape, mybir.dt.from_np(v.dtype), kind="ExternalInput").ap()
    out = nc.dram_tensor("out_x", (N, C), F32, kind="ExternalOutput").ap()
    build_kernel(nc, **args, out=out)
    r = run(nc, [arrays], core_ids=[0])
    return r.results[0]["out_x"].reshape(BATCH, SEQ, C)
```

```python
from contextlib import ExitStack

import numpy as np
import concourse.bass as bass
from concourse import mybir

F32, F32R = mybir.dt.float32, mybir.dt.float32r
BF16, I32, U32 = mybir.dt.bfloat16, mybir.dt.int32, mybir.dt.uint32
ALU, ACT, AX = mybir.AluOpType, mybir.ActivationFunctionType, mybir.AxisListType

P = 128
EPS = 1e-5
BATCH, SEQ, C = 2, 2048, 256
N = BATCH * SEQ
CC = C // P
HID = 1024
HC = HID // P
DK = 128
GT = 4
GROUP = GT * P
NG = N // GROUP
ST = 2
SLOT = ST * P
NSLOT = N // SLOT + 1
ROWS = NSLOT * SLOT
ROW = 2 * C + 2
BIDS = 8
QB = SEQ // SLOT
SCALE = float(DK) ** -0.5
AX_BUFS = 4
PASSES = ((0, 0), (1, 0), (0, 1))


class Named:
    pass


def hold(eng, sem, value, carrier):
    if isinstance(value, int):
        if value > 0:
            eng.wait_ge(sem, value)
        return
    eng.wait_ge(sem, value)
    eng.sem_inc(carrier, 1)


def build_kernel(nc, x, w256, w_st, k_w, v_w, w_qkv, ln, shares, ident, tri, mask, tok, slot_row, out):
    with ExitStack() as ctx:
        def sb(name, shape, dt=F32):
            return ctx.enter_context(nc.sbuf_tensor(name, shape, dt))

        def sem(name):
            return ctx.enter_context(nc.semaphore(name))

        b, s = Named(), Named()
        b.x1 = nc.dram_tensor("x_after_ffn1", (N, C), F32, kind="Internal").ap()
        b.x2 = nc.dram_tensor("x_after_attention", (N, C), F32, kind="Internal").ap()
        b.routed = [nc.dram_tensor(f"routed_rows{i}", (ROWS, ROW), F32, kind="Internal").ap() for i in range(2)]

        b.W = [sb(f"w_{p}", [P, 5, CC, C], F32R) for p in ("hi", "lo")]
        b.W3 = [sb(f"w3_{p}", [P, CC, C], F32R) for p in ("hi", "lo")]
        b.K = [sb(f"k_{p}", [P, 2, CC, HID], F32R) for p in ("hi", "lo")]
        b.V = [sb(f"v_{p}", [P, 2, HC, C], F32R) for p in ("hi", "lo")]
        b.Wb = sb("w_bid", [P, CC, P], F32R)
        b.Wqk = [sb(f"wqk_{p}", [P, 2, CC, DK], F32R) for p in ("hi", "lo")]
        b.Wvv = sb("wv_hilo", [P, CC, 2 * DK], F32R)
        b.Wao = [sb(f"wao_{p}", [P, C], F32R) for p in ("hi", "lo")]
        b.ln = sb("ln_cols", [P, 4, CC])
        b.ident = sb("ident_sb", [P, P])
        b.trif = sb("tri_f32", [P, 2, P])
        b.tri = sb("tri_sb", [P, 2, P], BF16)
        b.mask = sb("mask_sb", [P, ST, SLOT])
        b.tok = sb("tok_sb", [P, 2, N // P])
        b.slot_row = sb("slot_row_sb", [P, NSLOT + ST])
        b.shares = sb("shares_sb", [P, 3])
        b.bias = sb("bias_cols", [P, 4, CC])
        b.kbias = sb("k_bias", [P, 2, HC])
        b.bbias = sb("bid_bias", [P, 1])
        b.half = sb("minus_half", [P, 8])
        b.ones4 = sb("ones4", [P, GT])
        FA, RA = 13184, 12800
        af, ar = sb("arena_f32", [P, FA]), sb("arena_f32r", [P, RA], F32R)
        pos = {"f": 0, "r": 0}

        def view(which, *dims):
            n = int(np.prod(dims))
            start = pos[which]
            pos[which] += n
            assert pos[which] <= (FA if which == "f" else RA), (pos, dims)
            v = (af if which == "f" else ar)[:, start:start + n]
            if len(dims) == 2:
                v = v.rearrange("p (a b) -> p a b", a=dims[0])
            if len(dims) == 3:
                v = v.rearrange("p (a b c) -> p a b c", a=dims[0], b=dims[1])
            return v

        b.stage = [view("f", 4096) for _ in range(2)]
        b.raw_sf = view("f", CC, C)
        b.raw_w3 = b.stage[1][:, 2 * CC * C:3 * CC * C].rearrange("p (c n) -> p c n", c=CC)
        pos["f"] = pos["r"] = 0
        b.x = [view("f", GT, C) for _ in range(2)]
        b.z = view("f", GT, C)
        b.y = view("f", GT, C)
        b.rg = view("f", CC, GROUP)
        b.sg = [view("f", CC, GROUP) for _ in range(2)]
        b.xa = view("f", GT, C)
        b.rows = [view("f", GT, ROW) for _ in range(2)]
        b.bd = view("f", GROUP)
        b.zT = [view("r", CC, GROUP) for _ in range(2)]
        b.gT = [view("r", CC, GROUP) for _ in range(2)]
        b.hT = [view("r", CC, GROUP) for _ in range(2)]
        b.g2T = [view("r", CC, GROUP) for _ in range(2)]
        fa_end = pos["f"]
        pos["f"] = pos["r"] = 0
        b.sz = [view("f", ST, C) for _ in range(2)]
        b.srow = [view("f", ST, ROW - C) for _ in range(2)]
        b.r = [view("f", 2 * SLOT) for _ in range(2)]
        b.sq = [view("f", 2 * SLOT) for _ in range(2)]
        b.o = [view("f", ST, C) for _ in range(2)]
        b.shT = [view("r", CC, SLOT) for _ in range(2)]
        b.hr = [[view("r", HC, SLOT) for _ in range(2)] for _ in range(2)]
        pos["f"] = pos["r"] = 0
        b.ax = [view("f", ST, C) for _ in range(AX_BUFS)]
        b.az = view("f", ST, C)
        b.vt = view("f", ST, DK)
        b.vs = view("f", ST, DK)
        b.p = [view("f", ST, SEQ), view("f", ST, SEQ - SLOT)]
        b.ao = view("f", ST, C)
        b.azT = [view("r", CC, SLOT) for _ in range(2)]
        b.qT = [[view("r", SLOT) for _ in range(2)] for _ in range(2)]
        b.kT = [view("r", SEQ) for _ in range(2)]
        b.v = [view("r", SEQ // P, DK) for _ in range(2)]
        b.pT = [[view("r", 2, SLOT) for _ in range(2)] for _ in range(2)]
        b.oT = [view("r", SLOT) for _ in range(2)]
        b.st = sb("bn_parts", [P, 2, GT, 6])
        b.mv = sb("mean_var", [P, 2, GT, 2])
        b.rs = sb("rsqrt_work", [P, 2, 6, GT])
        b.bid = sb("bid_rows", [P, GT, BIDS])
        b.conf = sb("conf_rows", [P, GT, 4])
        b.gw = sb("gate_work", [P, 12, GT])
        b.gt = [sb(f"trans_gate{i}", [P, GT]) for i in range(2)]
        b.cnt = sb("expert1_count", [P, GT + 1])
        b.e16 = sb("expert1_bf16", [P, 2 * GT + 2], BF16)
        b.posi = [sb(f"row_index{i}", [P, GT], I32) for i in range(2)]
        b.padrow = sb("pad_rows", [P, ROW])
        b.padi = sb("pad_index", [P, ST], I32)
        b.n1 = sb("n_expert1", [P, 1])
        b.flag = sb("slot_expert", [P, NSLOT])
        b.flagi = sb("slot_expert_int", [P, NSLOT], I32)
        b.nflag = sb("slot_expert0", [P, NSLOT])
        b.idx = [sb(f"token_index{i}", [P, ST], I32) for i in range(2)]
        b.kbt = sb("slot_k_bias_part", [P, HC])
        b.kbs = [sb(f"slot_k_bias{i}", [P, HC]) for i in range(2)]
        b.mx = sb("row_max", [P, 8, ST])
        b.sum = sb("row_sum", [P, 2, ST])

        b.ps = [ctx.enter_context(nc.psum_tensor(f"bank{i}", [P, 512], F32)) for i in range(4)]
        b.ps4 = ctx.enter_context(nc.psum_tensor("banks4to7", [P, 4, 512], F32))
        b.bank = lambda i: b.ps[i][:, :] if i < 4 else b.ps4[:, i - 4, :]

        b.carry = {e: sem(f"carry_{e}") for e in ("pe", "act", "dve", "pool", "sp")}
        s.barrier, s.fence = sem("phase_done"), sem("fence")
        s.const = sem("const_loaded")
        s.stage = [sem(f"stage_loaded{i}") for i in range(2)]
        s.w_hi, s.pe_set, s.set_done = sem("w_hi"), sem("pe_setup"), sem("setup_done")
        s.memz, s.w_raw, s.link0 = sem("wb_zeroed"), sem("w_s_w_2"), sem("pad_row_zero")
        names = ("stats1", "rs1", "z1", "y1", "T1", "zhi", "zlo", "U", "sigr", "gv", "sigs", "ghi", "glo", "Wo",
                 "x2", "stats2", "rs2", "z2", "T2", "hhi", "hlo", "bid", "bd", "bidT", "b7", "conf", "e", "pref",
                 "posr", "W", "g2", "g2hi", "g2lo", "W3", "rdone", "link", "plink", "n1", "flag", "padi",
                 "sT", "shi", "slo", "Ks", "relu", "hrhi", "sq", "hrlo", "kbs", "Vs", "orow", "res")
        shared = {n: sem(f"f_{n}") for n in names}
        pairs = {n: [sem(f"f_{n}{k}") for k in range(2)] for n in ("x_in", "r_in", "s_in")}
        s.cleared = [*shared.values(), *(one for pair in pairs.values() for one in pair)]
        s.ffn = [dict(shared, **pairs, pad=sem(f"f{i}_pad"), scat=[sem(f"f{i}_scattered{k}") for k in range(2)],
                      o_out=[sem(f"f{i}_slot_out{k}") for k in range(2)]) for i in range(2)]
        names = ("stats", "rs", "z", "T", "zhi", "zlo", "vp", "vs", "vsum", "vhi", "vlo", "qk", "qkhi", "qklo", "S", "nb",
                 "exp", "PT", "pthi", "ptlo", "PV", "ohi", "olo", "Y", "y", "link", "plink", "sequence")
        s.a = dict({n: sem(f"a_{n}") for n in names}, out=sem("a_out"), x_in=[sem(f"a_x_in{k}") for k in range(AX_BUFS)])

        block = ctx.enter_context(nc.Block())
        src = [x, b.x2]
        dst = [b.x1, out]

        def barrier(eng, k):
            eng.drain().then_inc(s.barrier, 1)
            eng.wait_ge(s.barrier, 5 * k)
            eng.sem_inc(s.fence, 1)

        loads = ([("w", w256, 4 * CC * C), ("sf", w_st, 3 * CC * C + CC * BIDS)]
                 + [("k", k_w[:, e], CC * HID) for e in range(2)] + [("v", v_w[:, e], HC * C) for e in range(2)]
                 + [("a", w_qkv, 3 * CC * DK + C)])
        SF = 3 * CC * C

        @block.sync
        def _(sp):
            c = b.carry["sp"]
            for dstv, srcv in ((b.ln, ln), (b.ident, ident), (b.trif, tri), (b.mask, mask), (b.tok, tok),
                               (b.slot_row, slot_row), (b.shares, shares)):
                sp.dma_start(dstv[:], srcv).then_inc(s.const, 16)
            for n, (_, w, cols) in enumerate(loads):
                if n >= 2:
                    sp.wait_ge(s.set_done, n - 1)
                sp.dma_start(b.stage[n % 2][:, 0:cols], w).then_inc(s.stage[n % 2], 16)
            barrier(sp, 1)
            for i in range(2):
                f = s.ffn[i]
                xg = src[i].rearrange("(g t p) c -> g p t c", t=GT, p=P)
                for g in range(2):
                    sp.dma_start(b.x[g][:], xg[g]).then_inc(f["x_in"][g], 16)
                with sp.Fori(0, NG // 2 - 1) as it:
                    for par in range(2):
                        g = it * 2 + 2 + par
                        hold(sp, f["res"], g - 1, c)
                        sp.dma_start(b.x[par][:], xg[g]).then_inc(f["x_in"][par], 16)
                sp.wait_ge(f["res"], NG - 1)
                sp.dma_start(b.x[0][:], xg[NG - 2]).then_inc(f["x_in"][0], 16)
                sp.wait_ge(f["x_in"][0], 16 * (NG // 2 + 1))
                barrier(sp, 2 + 3 * i)
                rg = b.routed[i].rearrange("(j t p) c -> j p t c", t=ST, p=P)

                def slot_in(j, p):
                    hold(sp, f["sT"], j - 1, c)
                    sp.dma_start(b.sz[p][:], rg[j][:, :, 0:C]).then_inc(f["s_in"][p], 16)
                    hold(sp, f["orow"], j - 1, c)
                    sp.dma_start(b.srow[p][:], rg[j][:, :, C:ROW]).then_inc(f["r_in"][p], 16)

                for j in range(2):
                    slot_in(j, j)
                with sp.Fori(0, (NSLOT - 3) // 2) as it:
                    for par in range(2):
                        slot_in(it * 2 + 2 + par, par)
                slot_in(NSLOT - 1, 0)
                barrier(sp, 3 + 3 * i)
                if i == 0:
                    for one in s.cleared:
                        sp.sem_clear(one)
                    attention_sync(sp, b, s.a)
                    barrier(sp, 4)

        @block.tensor
        def _(pe):
            setup_tensor(pe, b, s, loads, SF)
            barrier(pe, 1)
            for i in range(2):
                ffn_a_tensor(pe, b, s.ffn[i])
                barrier(pe, 2 + 3 * i)
                ffn_b_tensor(pe, b, s.ffn[i])
                barrier(pe, 3 + 3 * i)
                if i == 0:
                    attention_tensor(pe, b, s.a)
                    barrier(pe, 4)

        @block.scalar
        def _(act):
            setup_scalar(act, b, s, SF)
            barrier(act, 1)
            for i in range(2):
                ffn_a_scalar(act, b, s.ffn[i])
                barrier(act, 2 + 3 * i)
                ffn_b_scalar(act, b, s.ffn[i])
                barrier(act, 3 + 3 * i)
                if i == 0:
                    attention_scalar(act, b, s.a)
                    barrier(act, 4)

        @block.vector
        def _(dve):
            setup_vector(dve, b, s, SF)
            barrier(dve, 1)
            for i in range(2):
                ffn_a_vector(dve, b, s.ffn[i])
                barrier(dve, 2 + 3 * i)
                ffn_b_vector(dve, b, s.ffn[i])
                barrier(dve, 3 + 3 * i)
                if i == 0:
                    attention_vector(dve, b, s.a)
                    barrier(dve, 4)

        @block.gpsimd
        def _(pool):
            pool.memset(b.half[:], -0.5).then_inc(s.memz, 1)
            barrier(pool, 1)
            for i in range(2):
                ffn_a_gpsimd(pool, b, s.ffn[i], b.routed[i])
                barrier(pool, 2 + 3 * i)
                ffn_b_gpsimd(pool, b, s.ffn[i], dst[i])
                barrier(pool, 3 + 3 * i)
                if i == 0:
                    attention_gpsimd(pool, b, s.a)
                    barrier(pool, 4)



def split_plan(b, SF):
    plan = []
    st = b.stage
    w = st[0][:, 0:4 * CC * C].rearrange("p (m c n) -> p m c n", m=4, c=CC)
    for m, (to, row) in enumerate(((0, 0), (1, 0), (3, 2), (4, None))):
        for c in range(CC):
            plan.append((0, w[:, m, c], None if row is None else b.ln[:, row, c:c + 1],
                         b.W[0][:, to, c], b.W[1][:, to, c]))
    for c in range(CC):
        plan.append((1, b.raw_sf[:, c], b.ln[:, 0, c:c + 1], b.W[0][:, 2, c], b.W[1][:, 2, c]))
    sf = st[1]
    for c in range(CC):
        plan.append((1, b.raw_w3[:, c], None, b.W3[0][:, c], b.W3[1][:, c]))
    wb = sf[:, SF:SF + CC * BIDS].rearrange("p (c n) -> p c n", c=CC)
    for c in range(CC):
        plan.append((1, wb[:, c], b.ln[:, 2, c:c + 1], b.Wb[:, c, 0:BIDS], b.Wb[:, c, BIDS:2 * BIDS]))
    for e in range(2):
        k = st[e % 2][:, 0:CC * HID].rearrange("p (c n) -> p c n", c=CC)
        for c in range(CC):
            plan.append((2 + e, k[:, c], b.ln[:, 2, c:c + 1], b.K[0][:, e, c], b.K[1][:, e, c]))
    for e in range(2):
        v = st[e % 2][:, 0:HC * C].rearrange("p (h n) -> p h n", h=HC)
        plan.append((4 + e, v, None, b.V[0][:, e], b.V[1][:, e]))
    a = st[0]
    qkv = a[:, 0:3 * CC * DK].rearrange("p (m c n) -> p m c n", m=3, c=CC)
    for m in range(2):
        plan.append((6, qkv[:, m], None, b.Wqk[0][:, m], b.Wqk[1][:, m]))
    for c in range(CC):
        plan.append((6, qkv[:, 2, c], None, b.Wvv[:, c, 0:DK], b.Wvv[:, c, DK:2 * DK]))
    plan.append((6, a[:, 3 * CC * DK:3 * CC * DK + C], None, b.Wao[0][:], b.Wao[1][:]))
    return plan


def setup_scalar(act, b, s, SF):
    act.wait_ge(s.const, 16 * 7)
    act.wait_ge(s.memz, 3)
    load = -1
    for n, (ld, raw, scale, hi, _) in enumerate(split_plan(b, SF)):
        if ld != load:
            load = ld
            act.wait_ge(s.stage[ld % 2], 16 * (ld // 2 + 1))
            if ld == 1:
                act.wait_ge(s.pe_set, 2)
                act.copy(b.raw_sf[:, :, :], b.bank(1).rearrange("p (c n) -> p c n", c=CC)).then_inc(s.w_raw, 1)
                act.wait_ge(s.w_raw, 1)
        if scale is None:
            act.copy(hi, raw).then_inc(s.w_hi, 1)
        else:
            act.mul(hi, raw, scale).then_inc(s.w_hi, 1)


def setup_vector(dve, b, s, SF):
    dve.memset(b.Wb[:].bitcast(F32), 0.0).then_inc(s.memz, 1)
    dve.memset(b.bbias[:], 0.0).then_inc(s.memz, 1)
    dve.memset(b.ones4[:], 1.0)
    dve.memset(b.cnt[:], 0.0)
    dve.memset(b.padrow[:], 0.0).then_inc(s.link0, 1)
    dve.wait_ge(s.link0, 1)
    dve.memset(b.padrow[:, 2 * C + 1:ROW].bitcast(I32), ROWS)
    dve.wait_ge(s.const, 16 * 7)
    dve.tensor_copy(b.tri[:], b.trif[:])
    plan = split_plan(b, SF)
    for n, (ld, raw, scale, hi, lo) in enumerate(plan):
        dve.wait_ge(s.w_hi, n + 1)
        last = dve.scalar_tensor_tensor(lo, raw, 1.0 if scale is None else scale, hi.bitcast(F32), ALU.mult,
                                        ALU.subtract)
        if n + 1 == len(plan) or plan[n + 1][0] != ld:
            if ld == 0:
                dve.wait_ge(s.pe_set, 1)
                for m in (0, 1, 3):
                    last = dve.tensor_copy(b.bias[:, m, :], b.bank(0)[:, m * CC:(m + 1) * CC])
            elif ld == 1:
                dve.wait_ge(s.pe_set, 3)
                dve.wait_ge(s.memz, 3)
                dve.tensor_copy(b.bias[:, 2, :], b.bank(2)[:, 0:CC])
                last = dve.tensor_copy(b.bbias[0:BIDS, :], b.bank(2)[0:BIDS, 2 * CC:2 * CC + 1])
            elif ld in (2, 3):
                dve.wait_ge(s.pe_set, 2 + ld)
                last = dve.tensor_copy(b.kbias[:, ld - 2, :], b.bank(ld - 2)[:, 16:16 + HC])
            last.then_inc(s.set_done, 1)


def setup_tensor(pe, b, s, loads, SF):
    def column(bank, col, raw, m, row, size=P):
        for c in range(CC):
            mm = pe.matmul(bank[0:size, col:col + 1], raw(c)[:, m:m + size], b.ln[:, row, c:c + 1],
                           start=(c == 0), stop=(c == CC - 1))
        return mm

    pe.wait_ge(s.const, 16 * 7)
    pe.wait_ge(s.stage[0], 16)
    w = b.stage[0][:, 0:4 * CC * C].rearrange("p (m c n) -> p m c n", m=4, c=CC)
    for m, (to, row) in enumerate(((0, 1), (1, 1), (3, 3))):
        for f in range(CC):
            mm = column(b.bank(0), to * CC + f, lambda c, m=m: w[:, m, c], f * P, row)
    mm.then_inc(s.pe_set, 1)
    pe.wait_ge(s.stage[1], 16)
    sf = b.stage[1][:, 0:2 * CC * C].rearrange("p (m c n) -> p m c n", m=2, c=CC)
    for o in range(CC):
        for k in range(CC):
            mm = pe.matmul(b.bank(1)[:, o * C:(o + 1) * C], sf[:, 0, k, o * P:(o + 1) * P], sf[:, 1, k],
                           start=(k == 0), stop=(k == CC - 1))
    mm.then_inc(s.pe_set, 1)
    pe.wait_ge(s.w_raw, 1)
    for f in range(CC):
        column(b.bank(2), f, lambda c: b.raw_sf[:, c], f * P, 1)
    wb = b.stage[1][:, SF:SF + CC * BIDS].rearrange("p (c n) -> p c n", c=CC)
    column(b.bank(2), 2 * CC, lambda c: wb[:, c], 0, 3, BIDS).then_inc(s.pe_set, 1)
    for e in range(2):
        pe.wait_ge(s.stage[e], 32)
        k = b.stage[e][:, 0:CC * HID].rearrange("p (c n) -> p c n", c=CC)
        if e == 0:
            pe.wait_ge(s.set_done, 1)
        else:
            pe.wait_ge(s.set_done, 2)
        for h in range(HC):
            mm = column(b.bank(e), 16 + h, lambda c: k[:, c], h * P, 3)
        mm.then_inc(s.pe_set, 1)



def passes(pe, outv, w, m, n_first=True, n_last=True):
    for k, (pw, pm) in enumerate(PASSES):
        mm = pe.matmul(outv, w(pw), m(pm), start=(n_first and k == 0), stop=(n_last and k == 2))
    return mm


def ffn_a_tensor(pe, b, f):
    cr = b.carry["pe"]

    def T1(g):
        pe.wait_ge(f["z1"], g + 1)
        pe.sem_inc(cr, 1)
        hold(pe, f["hlo"], 2 * g - 2, cr)
        for c in range(CC):
            for t in range(GT):
                mm = pe.transpose(b.bank(c)[:, t * P:(t + 1) * P], b.z[:, t, c * P:(c + 1) * P], b.ident[:])
        mm.then_inc(f["T1"], 1)

    def U(g, between=None):
        pe.wait_ge(f["zlo"], 2 * g + 2)
        pe.sem_inc(cr, 1)
        for n, (m, fc) in enumerate(((0, 0), (1, 0), (0, 1), (1, 1), (2, 0), (2, 1))):
            if n == 2 and between:
                between()
            if n == 0:
                hold(pe, f["bd"], g - 1, cr)
            if n == 1:
                hold(pe, f["g2"], g * 2 - 3, cr)
            if n == 2:
                hold(pe, f["g2"], g * 2 - 2, cr)
            if n == 3:
                pe.wait_ge(f["sigr"], g * 2 + 1)
                pe.sem_inc(cr, 1)
            if n == 4:
                pe.wait_ge(f["gv"], g * 2 + 1)
                pe.sem_inc(cr, 1)
            if n == 5:
                pe.wait_ge(f["sigr"], g * 2 + 2)
                pe.sem_inc(cr, 1)
            for c in range(CC):
                mm = passes(pe, b.bank(2 + n % 3), lambda p: b.W[p][:, m, c, fc * P:(fc + 1) * P],
                            lambda p: b.zT[p][:, c], c == 0, c == CC - 1)
            mm.then_inc(f["U"], 1)

    def rows_out(g, act, w, bank0, done):
        for t in range(GT):
            for c in range(CC):
                mm = passes(pe, b.bank(bank0 + t // 2)[:, (t % 2) * C:(t % 2 + 1) * C],
                            lambda p: act[p][:, c, t * P:(t + 1) * P], lambda p: w(p, c), c == 0, c == CC - 1)
            if t % 2:
                mm.then_inc(done, 1)

    def Wo(g):
        pe.wait_ge(f["glo"], 2 * g + 2)
        pe.sem_inc(cr, 1)
        hold(pe, f["rdone"], g - 1, cr)
        rows_out(g, b.gT, lambda p, c: b.W[p][:, 4, c], 6, f["Wo"])

    def T2(g):
        pe.wait_ge(f["z2"], g + 1)
        pe.sem_inc(cr, 1)
        pe.wait_ge(f["zlo"], 2 * g + 4)
        pe.sem_inc(cr, 1)
        for c in range(CC):
            for t in range(GT):
                mm = pe.transpose(b.bank(c)[:, t * P:(t + 1) * P], b.rows[g_par(g)][:, t, c * P:(c + 1) * P],
                                  b.ident[:])
        mm.then_inc(f["T2"], 1)

    def bids(g):
        pe.wait_ge(f["hlo"], 2 * g + 2)
        pe.sem_inc(cr, 1)
        pe.wait_ge(f["gv"], gnext(g) * 2 + 2)
        pe.sem_inc(cr, 1)
        for c in range(CC):
            for p in range(2):
                mm = pe.matmul(b.bank(2), b.Wb[:, c], b.hT[p][:, c], start=(c == 0 and p == 0), stop=(c == 1 and p == 1))
        mm.then_inc(f["bid"], 1)

    def W1(g):
        for fc in range(CC):
            pe.wait_ge(f["sigs"], gnext(g) * 2 + 1 + fc)
            pe.sem_inc(cr, 1)
            for c in range(CC):
                mm = passes(pe, b.bank(3 + fc), lambda p: b.W[p][:, 3, c, fc * P:(fc + 1) * P],
                            lambda p: b.hT[p][:, c], c == 0, c == CC - 1)
            mm.then_inc(f["W"], 1)

    def bidT(g):
        pe.wait_ge(f["bd"], g + 1)
        pe.sem_inc(cr, 1)
        hold(pe, f["posr"], g, cr)
        for t in range(GT):
            mm = pe.transpose(b.bank(5)[:, t * P:(t + 1) * P], b.bd[:, t * P:(t + 1) * P], b.ident[:])
        mm.then_inc(f["bidT"], 1)

    def W3(g):
        pe.wait_ge(f["g2lo"], 2 * g + 2)
        pe.sem_inc(cr, 1)
        pe.wait_ge(f["x2"], gnext(g) * 2 + 2)
        pe.sem_inc(cr, 1)
        rows_out(g, b.g2T, lambda p, c: b.W3[p][:, c], 6, f["W3"])

    def prefix(g):
        pe.wait_ge(f["e"], g + 1)
        pe.sem_inc(cr, 1)
        pe.matmul(b.bank(5)[:, 0:GT], b.tri[:, 0], b.e16[:, 0:GT], start=True, stop=False)
        pe.matmul(b.bank(5)[:, 0:GT], b.tri[:, 1], b.e16[:, GT:2 * GT], start=False, stop=True).then_inc(f["pref"], 1)

    par = [0]

    def g_par(g):
        return par[0]

    def gnext(g):
        return g if isinstance(g, int) and g == NG - 1 else g + 1

    def body(g, p, last=False):
        par[0] = p
        before = None if isinstance(g, int) and g == 0 else (lambda: prefix(g - 1))
        if not last:
            U(g + 1, before)
        else:
            before()
        T2(g)
        if not last:
            Wo(g + 1)
        bids(g)
        W1(g)
        bidT(g)
        if not last:
            T1(g + 2)
        W3(g)

    T1(0)
    U(0)
    T1(1)
    Wo(0)
    body(0, 0)
    with pe.Fori(0, (NG - 2) // 2) as it:
        for k in range(2):
            body(it * 2 + 1 + k, (1 + k) % 2)
    body(NG - 1, (NG - 1) % 2, True)
    prefix(NG - 1)
    pe.wait_ge(f["posr"], NG)
    pe.matmul(b.bank(5)[:, 0:1], b.tri[:, 1], b.e16[:, 2 * GT:2 * GT + 1], start=True, stop=True).then_inc(f["n1"], 1)


def ffn_a_scalar(act, b, f):
    cr = b.carry["act"]

    def y(g):
        act.wait_ge(f["rs1"], g + 1)
        act.sem_inc(cr, 1)
        hold(act, f["x2"], g * 2, cr)
        for t in range(GT):
            last = act.activation(b.y[:, t], b.x[par(g)][:, t], ACT.Identity, bias=b.rs[:, 0, 3, t:t + 1],
                                  scale=b.rs[:, 0, 1, t:t + 1])
        last.then_inc(f["y1"], 1)

    def z(g, p):
        act.wait_ge(f["rs1"], g + 1)
        act.sem_inc(cr, 1)
        hold(act, f["T1"], g, cr)
        for t in range(GT):
            last = act.activation(b.z[:, t], b.x[p][:, t], ACT.Identity, bias=b.rs[:, 0, 5, t:t + 1],
                                  scale=b.rs[:, 0, 2, t:t + 1])
        last.then_inc(f["z1"], 1)

    def z2(g, p):
        act.wait_ge(f["rs2"], g + 1)
        act.sem_inc(cr, 1)
        act.wait_ge(f["res"], g + 1)
        act.sem_inc(cr, 1)
        for t in range(GT):
            last = act.activation(b.rows[p][:, t, 0:C], b.xa[:, t], ACT.Identity, bias=b.rs[:, 1, 5, t:t + 1],
                                  scale=b.rs[:, 1, 2, t:t + 1])
        last.then_inc(f["z2"], 1)

    pp = [0]

    def par(g):
        return pp[0]

    def hi(g, T, bank, to, done, prev):
        act.wait_ge(T, g + 1)
        act.sem_inc(cr, 1)
        if prev is not None:
            hold(act, prev[0], prev[1], cr)
        for c in range(CC):
            act.copy(to[0][:, c], b.bank(bank + c)).then_inc(done, 1)

    def sig_r(g, fc):
        hold(act, f["U"], g * 6 + 1 + 2 * fc, cr)
        hold(act, f["glo"], g * 2, cr)
        act.activation(b.rg[:, fc], b.bank(2 + 2 * fc), ACT.Sigmoid, bias=b.bias[:, 0, fc:fc + 1]).then_inc(f["sigr"], 1)

    def g_hi(g, fc):
        act.wait_ge(f["gv"], g * 2 + 1 + fc)
        act.sem_inc(cr, 1)
        hold(act, f["Wo"], g * 2, cr)
        act.copy(b.gT[0][:, fc], b.rg[:, fc]).then_inc(f["ghi"], 1)

    def sig_s(g, fc):
        act.wait_ge(f["U"], g * 6 + 5 + fc)
        act.sem_inc(cr, 1)
        hold(act, f["g2lo"], g * 2 - 2, cr)
        act.activation(b.sg[pp[0]][:, fc], b.bank(3 + fc), ACT.Sigmoid, bias=b.bias[:, 2, fc:fc + 1]).then_inc(f["sigs"], 1)

    def bd(g):
        act.wait_ge(f["bid"], g + 1)
        act.sem_inc(cr, 1)
        hold(act, f["bidT"], g, cr)
        act.activation(b.bd[:, :], b.bank(2), ACT.Identity, bias=b.bbias[:, 0:1]).then_inc(f["bd"], 1)

    def conf(g):
        act.wait_ge(f["b7"], g + 1)
        act.sem_inc(cr, 1)
        act.activation(b.conf[:], b.bid[:, :, 0:4], ACT.Sigmoid).then_inc(f["conf"], 1)

    def g2_hi(g, fc, p):
        act.wait_ge(f["g2"], g * 2 + 1 + fc)
        act.sem_inc(cr, 1)
        if fc == 0:
            hold(act, f["W3"], g * 2, cr)
        act.copy(b.g2T[0][:, fc], b.sg[p][:, fc]).then_inc(f["g2hi"], 1)

    def mix(g, p):
        pp[0] = p
        y(g)
        sig_r(g, 0)
        sig_r(g, 1)
        g_hi(g, 0)
        g_hi(g, 1)
        sig_s(g, 0)
        sig_s(g, 1)

    def z_hi(g):
        hi(g, f["T1"], 0, b.zT, f["zhi"], (f["U"], g * 6))

    def h_hi(g):
        hi(g, f["T2"], 0, b.hT, f["hhi"], (f["W"], g * 2))

    def body(g, p, last=False):
        if not last:
            mix(g + 1, 1 - p)
        h_hi(g)
        bd(g)
        if not last:
            z(g + 2, p)
        conf(g)
        g2_hi(g, 0, p)
        g2_hi(g, 1, p)
        if not last:
            z_hi(g + 2)
            z2(g + 1, 1 - p)

    z(0, 0)
    z_hi(0)
    mix(0, 0)
    z(1, 1)
    z_hi(1)
    z2(0, 0)
    body(0, 0)
    with act.Fori(0, (NG - 2) // 2) as it:
        for k in range(2):
            body(it * 2 + 1 + k, (1 + k) % 2)
    body(NG - 1, (NG - 1) % 2, True)


def ffn_a_gpsimd(pool, b, f, routed):
    cr = b.carry["pool"]
    n = [0]

    def link(ins, v):
        ins.then_inc(f["plink"], 1)
        n[0] += 1
        hold(pool, f["plink"], v(n[0]), cr)

    def rs1(g, v):
        pool.wait_ge(f["stats1"], g + 1)
        pool.sem_inc(cr, 1)
        hold(pool, f["y1"], g, cr)
        hold(pool, f["z1"], g, cr)
        mean, var = b.mv[:, 0, :, 0], b.mv[:, 0, :, 1]
        a, r1, r, sh1, nm, sh = (b.rs[:, 0, k] for k in range(6))
        half = b.half[:, 0:GT]
        pool.tensor_scalar(nm, mean, -1.0, 0.0, ALU.mult, ALU.add)
        link(pool.tensor_scalar(a, var, EPS, 0.0, ALU.add, ALU.add), v)
        link(pool.tensor_tensor(r1, a, half, ALU.pow), v)
        pool.tensor_tensor(sh1, nm, r1, ALU.mult)
        link(pool.tensor_tensor(a, var, r1, ALU.mult), v)
        link(pool.tensor_tensor(a, a, r1, ALU.mult), v)
        link(pool.tensor_scalar(a, a, EPS, 0.0, ALU.add, ALU.add), v)
        link(pool.tensor_tensor(r, a, half, ALU.pow), v)
        link(pool.tensor_tensor(r, r, r1, ALU.mult), v)
        pool.tensor_tensor(sh, nm, r, ALU.mult).then_inc(f["rs1"], 1)

    def rs2(g, v):
        pool.wait_ge(f["stats2"], g + 1)
        pool.sem_inc(cr, 1)
        hold(pool, f["z2"], g, cr)
        mean, var = b.mv[:, 1, :, 0], b.mv[:, 1, :, 1]
        a, r, nm, sh = (b.rs[:, 1, k] for k in (0, 2, 4, 5))
        pool.tensor_scalar(nm, mean, -1.0, 0.0, ALU.mult, ALU.add)
        link(pool.tensor_scalar(a, var, EPS, 0.0, ALU.add, ALU.add), v)
        link(pool.tensor_tensor(r, a, b.half[:, 0:GT], ALU.pow), v)
        pool.tensor_tensor(sh, nm, r, ALU.mult).then_inc(f["rs2"], 1)

    def lo(g, fc, src, to, hi_sem, done):
        pool.wait_ge(hi_sem, g * 2 + 1 + fc)
        pool.sem_inc(cr, 1)
        pool.tensor_tensor(to[1][:, fc], src[:, fc], to[0][:, fc].bitcast(F32), ALU.subtract).then_inc(done, 1)

    def scatter(g, p):
        pool.wait_ge(f["rdone"], g + 1)
        pool.sem_inc(cr, 1)
        pool.wait_ge(f["posr"], g + 1)
        pool.sem_inc(cr, 1)
        for t in range(GT):
            pool.indirect_dma_start(routed, bass.IndirectOffsetOnAxis(b.posi[p][:, t:t + 1].bitcast(U32), 0),
                                    b.rows[p][:, t, :], None).then_inc(f["scat"][p], 16)

    def g_lo(g, fc):
        lo(g, fc, b.rg, b.gT, f["ghi"], f["glo"])

    def g2_lo(g, p):
        for fc in range(CC):
            lo(g, fc, b.sg[p], b.g2T, f["g2hi"], f["g2lo"])

    def body(g, p, v, last=False):
        if not last:
            g_lo(g + 1, 0)
        if not (isinstance(g, int) and g == 0):
            scatter(g - 1, 1 - p)
        if not last:
            g_lo(g + 1, 1)
            rs1(g + 2, v)
            rs2(g + 1, v)
        g2_lo(g, p)

    PER = 9
    fixed = lambda k: k
    rs1(0, fixed)
    rs1(1, fixed)
    g_lo(0, 0)
    g_lo(0, 1)
    rs2(0, fixed)
    body(0, 0, fixed)
    with pool.Fori(0, (NG - 2) // 2) as it:
        for k in range(2):
            body(it * 2 + 1 + k, (1 + k) % 2, lambda q: it * (2 * PER) + q)
    body(NG - 1, (NG - 1) % 2, fixed, True)
    scatter(NG - 1, (NG - 1) % 2)
    pool.wait_ge(f["padi"], 1)
    for t in range(ST):
        pool.indirect_dma_start(routed, bass.IndirectOffsetOnAxis(b.padi[:, t:t + 1].bitcast(U32), 0),
                                b.padrow[:], None).then_inc(f["pad"], 16)
    pool.wait_ge(f["pad"], 16 * ST)
    for p in range(2):
        pool.wait_ge(f["scat"][p], 16 * GT * NG // 2)


def ffn_a_vector(dve, b, f):
    cr = b.carry["dve"]
    n = [0]
    pp = [0]

    def stats(which, src, g, done, v):
        for t in range(GT):
            last = dve.bn_stats(b.st[:, which, t], src[:, t])
        last.then_inc(f["link"], 1)
        n[0] += 1
        hold(dve, f["link"], v(n[0]), cr)
        for t in range(GT):
            last = dve.bn_aggr(b.mv[:, which, t], b.st[:, which, t])
        last.then_inc(done, 1)

    def link(ins, v):
        ins.then_inc(f["link"], 1)
        n[0] += 1
        hold(dve, f["link"], v(n[0]), cr)

    def norm1(g, p, v):
        hold(dve, f["x_in"][p], (g // 2 + 1) * 16 if isinstance(g, int) else x_count(g), cr)
        hold(dve, f["rs1"], g, cr)
        stats(0, b.x[p], g, f["stats1"], v)

    xc = [None]

    def x_count(g):
        return xc[0]

    def lo(g, hi_sem, bank, to, done):
        for c in range(CC):
            dve.wait_ge(hi_sem, g * 2 + 1 + c)
            dve.sem_inc(cr, 1)
            dve.tensor_tensor(to[1][:, c], b.bank(bank + c), to[0][:, c].bitcast(F32), ALU.subtract).then_inc(done, 1)

    def gv(g, fc):
        dve.wait_ge(f["sigr"], g * 2 + 1 + fc)
        dve.sem_inc(cr, 1)
        hold(dve, f["U"], g * 6 + 2 + 2 * fc, cr)
        bank = b.bank(3 if fc == 0 else 2)
        dve.scalar_tensor_tensor(b.rg[:, fc], bank, b.bias[:, 1, fc:fc + 1], b.rg[:, fc], ALU.add,
                                 ALU.mult).then_inc(f["gv"], 1)

    def x2(g, v):
        dve.wait_ge(f["y1"], g + 1)
        dve.sem_inc(cr, 1)
        hold(dve, f["z2"], g, cr)
        for q in range(GT // 2):
            dve.wait_ge(f["Wo"], g * 2 + 1 + q)
            dve.sem_inc(cr, 1)
            dve.tensor_tensor(b.xa[:, 2 * q:2 * q + 2], b.bank(6 + q).rearrange("p (t c) -> p t c", t=2),
                              b.y[:, 2 * q:2 * q + 2], ALU.add).then_inc(f["x2"], 1)
        dve.wait_ge(f["x2"], g * 2 + 2)
        dve.sem_inc(cr, 1)
        stats(1, b.xa, g, f["stats2"], v)

    def residual(g, p):
        hold(dve, f["scat"][p], 16 * GT * (g // 2) if isinstance(g, int) else sc[0], cr)
        dve.scalar_tensor_tensor(b.rows[p][:, :, C:2 * C], b.xa[:, :, :], 0.5, b.x[p][:, :, :], ALU.mult,
                                 ALU.add).then_inc(f["res"], 1)

    sc = [None]

    def gates(g, v):
        dve.wait_ge(f["bidT"], g + 1)
        dve.sem_inc(cr, 1)
        raw = b.bank(5).rearrange("p (t k) -> p t k", t=GT)
        link(dve.tensor_copy(b.bid[:], raw[:, :, BIDS:2 * BIDS]), v)
        dve.tensor_tensor(b.bid[:], raw[:, :, 0:BIDS], b.bid[:], ALU.add).then_inc(f["b7"], 1)
        w = lambda k: b.gw[:, k]
        dve.wait_ge(f["conf"], g + 1)
        dve.sem_inc(cr, 1)
        for e in range(3):
            last = dve.scalar_tensor_tensor(w(e), b.conf[:, :, e], b.shares[:, e:e + 1], b.conf[:, :, 3], ALU.mult,
                                            ALU.mult)
        link(last, v)
        for e in range(3):
            last = dve.tensor_tensor(w(e), w(e), b.bid[:, :, 4 + e], ALU.add)
        link(last, v)
        dve.tensor_tensor(w(3), w(1), w(0), ALU.is_gt)
        dve.tensor_tensor(w(4), w(0), w(1), ALU.max)
        link(dve.tensor_tensor(w(6), b.conf[:, :, 1], b.conf[:, :, 0], ALU.subtract), v)
        dve.tensor_tensor(w(5), w(2), w(4), ALU.is_gt)
        link(dve.tensor_tensor(w(6), w(6), w(3), ALU.mult), v)
        dve.tensor_copy(b.e16[:, 0:GT], w(3))
        link(dve.tensor_copy(b.cnt[:, 0:1], b.cnt[:, GT:GT + 1]), v)
        link(dve.tensor_tensor_scan(b.cnt[:, 1:GT + 1], b.ones4[:], w(3), b.cnt[:, 0:1], ALU.mult, ALU.add), v)
        dve.tensor_copy(b.e16[:, 2 * GT:2 * GT + 1], b.cnt[:, GT:GT + 1])
        dve.tensor_copy(b.e16[:, GT:2 * GT], b.cnt[:, 0:GT]).then_inc(f["e"], 1)

    def win(g, p, v, tokc):
        w = lambda k: b.gw[:, k]
        link(dve.tensor_tensor(w(6), w(6), b.conf[:, :, 0], ALU.add), v)
        link(dve.tensor_tensor(w(7), b.conf[:, :, 2], w(6), ALU.subtract), v)
        link(dve.tensor_tensor(w(7), w(7), w(5), ALU.mult), v)
        link(dve.tensor_tensor(w(7), w(7), w(6), ALU.add), v)
        link(dve.tensor_scalar(w(8), w(7), 1e-6, None, ALU.add), v)
        link(dve.reciprocal(w(9), w(8)), v)
        link(dve.scalar_tensor_tensor(w(10), w(7), 0.5, w(9), ALU.mult, ALU.mult), v)
        link(dve.tensor_tensor(b.gt[p][:], w(10), w(5), ALU.mult), v)
        dve.tensor_tensor(b.rows[p][:, :, 2 * C], w(10), b.gt[p][:], ALU.subtract)
        dve.tensor_copy(b.rows[p][:, :, 2 * C + 1].bitcast(I32), b.tok[:, 0, tokc])
        link(dve.tensor_tensor(w(9), w(3), b.tok[:, 1, tokc], ALU.mult), v)
        link(dve.tensor_tensor(w(11), w(9), b.tok[:, 0, tokc], ALU.add), v)

    def rank(g, p):
        dve.wait_ge(f["pref"], g + 1)
        dve.sem_inc(cr, 1)
        dve.tensor_tensor(b.posi[p][:], b.gw[:, 11], b.bank(5)[:, 0:GT], ALU.subtract).then_inc(f["posr"], 1)

    def g2(g, p):
        for fc in range(CC):
            dve.wait_ge(f["W"], g * 2 + 1 + fc)
            dve.sem_inc(cr, 1)
            dve.scalar_tensor_tensor(b.sg[p][:, fc], b.bank(3 + fc), b.bias[:, 3, fc:fc + 1], b.sg[p][:, fc],
                                     ALU.add, ALU.mult).then_inc(f["g2"], 1)

    def w3(g, p):
        for t in range(GT):
            if t % 2 == 0:
                dve.wait_ge(f["W3"], g * 2 + 1 + t // 2)
                dve.sem_inc(cr, 1)
            last = dve.scalar_tensor_tensor(b.rows[p][:, t, C:2 * C], b.bank(6 + t // 2)[:, (t % 2) * C:(t % 2 + 1) * C],
                                            b.gt[p][:, t:t + 1], b.rows[p][:, t, C:2 * C], ALU.mult, ALU.add)
        last.then_inc(f["rdone"], 1)

    fixed = lambda k: k

    def body(g, p, v, tokc, last=False):
        q = 1 - p
        if not (isinstance(g, int) and g == 0):
            w3(g - 1, q)
        if not last:
            gv(g + 1, 0)
        if not (isinstance(g, int) and g == 0):
            rank(g - 1, q)
        if not last:
            norm1(g + 2, p, v)
            gv(g + 1, 1)
        lo(g, f["hhi"], 0, b.hT, f["hlo"])
        if not last:
            x2(g + 1, v)
        g2(g, p)
        gates(g, v)
        if not last:
            lo(g + 2, f["zhi"], 0, b.zT, f["zlo"])
            residual(g + 1, q)
        win(g, p, v, tokc)

    norm1(0, 0, fixed)
    lo(0, f["zhi"], 0, b.zT, f["zlo"])
    norm1(1, 1, fixed)
    gv(0, 0)
    gv(0, 1)
    lo(1, f["zhi"], 0, b.zT, f["zlo"])
    x2(0, fixed)
    residual(0, 0)
    body(0, 0, fixed, slice(0, GT))
    start = n[0]
    with dve.Fori(0, (NG - 2) // 2) as it:
        per = [0]
        for k in range(2):
            g = it * 2 + 1 + k
            xc[0] = it * 16 + 16 * ((3 + k) // 2 + 1)
            sc[0] = it * (16 * GT) + 16 * GT * ((2 + k) // 2)
            v = (lambda q: it * LINKS + q)
            body(g, (1 + k) % 2, v, bass.ds(g * GT, GT))
        assert n[0] - start == LINKS, n[0] - start
    n[0] = start + LINKS * ((NG - 2) // 2)
    body(NG - 1, (NG - 1) % 2, fixed, slice((NG - 1) * GT, NG * GT), True)
    w3(NG - 1, (NG - 1) % 2)
    rank(NG - 1, (NG - 1) % 2)
    dve.wait_ge(f["n1"], 1)
    link(dve.tensor_copy(b.n1[:], b.bank(5)[:, 0:1]), fixed)
    dve.tensor_scalar(b.padi[:], b.slot_row[:, NSLOT:NSLOT + ST], b.n1[:, 0:1], None, ALU.subtract).then_inc(f["padi"], 1)
    link(dve.tensor_scalar(b.flag[:], b.slot_row[:, 0:NSLOT], b.n1[:, 0:1], float(N), ALU.add, ALU.is_ge), fixed)
    dve.tensor_scalar(b.nflag[:], b.flag[:], -1.0, 1.0, ALU.mult, ALU.add)
    dve.tensor_copy(b.flagi[:], b.flag[:])
    dve.memset(b.cnt[:], 0.0).then_inc(f["flag"], 1)
    b.link_total = n[0]


LINKS = 38



def slots(eng, first, body):
    first()
    for j in (1, 2):
        body(j, j % 2, False)
    with eng.Fori(0, (NSLOT - 5) // 2) as it:
        for k in range(2):
            body(it * 2 + 3 + k, (3 + k) % 2, False)
    for j in (NSLOT - 2, NSLOT - 1):
        body(j, j % 2, j == NSLOT - 1)


def ffn_b_tensor(pe, b, f):
    cr = b.carry["pe"]

    def sT(j, p, loads):
        pe.wait_ge(f["s_in"][p], loads * 16)
        pe.sem_inc(cr, 1)
        hold(pe, f["slo"], j, cr)
        for c in range(CC):
            for t in range(ST):
                mm = pe.transpose(b.bank(0)[:, c * SLOT + t * P:c * SLOT + (t + 1) * P],
                                  b.sz[p][:, t, c * P:(c + 1) * P], b.ident[:])
        mm.then_inc(f["sT"], 1)

    def K(j, e):
        for q in range(HC // 2):
            hold(pe, f["relu"], j * 4 - 3 + q, cr)
            for h in (2 * q, 2 * q + 1):
                for c in range(CC):
                    mm = passes(pe, b.bank(1 + q)[:, (h % 2) * SLOT:(h % 2 + 1) * SLOT],
                                lambda p: b.K[p][:, e, c, h * P:(h + 1) * P], lambda p: b.shT[p][:, c], c == 0,
                                c == CC - 1)
            mm.then_inc(f["Ks"], 1)

    def V(j, p, e):
        for t in range(ST):
            for h in range(HC):
                mm = passes(pe, b.bank(5)[:, t * C:(t + 1) * C], lambda q: b.hr[p][q][:, h, t * P:(t + 1) * P],
                            lambda q: b.V[q][:, e, h], h == 0, h == HC - 1)
        mm.then_inc(f["Vs"], 1)

    def either(j, run):
        e = pe.value_load(b.flagi[0:1, bass.ds(j, 1)], min_val=0, max_val=1)
        with pe.If(e < 1):
            run(0)
        with pe.Else():
            run(1)

    def Kj(j):
        pe.wait_ge(f["slo"], j + 1)
        pe.sem_inc(cr, 1)
        either(j, lambda e: K(j, e))

    def Vj(j, p):
        pe.wait_ge(f["hrlo"], j * 4 + 4)
        pe.sem_inc(cr, 1)
        hold(pe, f["orow"], j, cr)
        either(j, lambda e: V(j, p, e))

    def first():
        sT(0, 0, 1)
        Kj(0)
        sT(1, 1, 1)

    def body(j, p, last):
        Kj(j)
        if not last:
            sT(j + 1, 1 - p, (j + 1) // 2 + 1 if isinstance(j, int) else loads_of(j, p))
        Vj(j - 1, 1 - p)

    def loads_of(j, p):
        return half[0] + (1 if p else 0)

    half = [None]
    first()
    for j in (1, 2):
        body(j, j % 2, False)
    with pe.Fori(0, (NSLOT - 5) // 2) as it:
        for k in range(2):
            half[0] = it + 2 if k == 0 else it + 3
            body(it * 2 + 3 + k, (3 + k) % 2, False)
    for j in (NSLOT - 2, NSLOT - 1):
        body(j, j % 2, j == NSLOT - 1)
    Vj(NSLOT - 1, (NSLOT - 1) % 2)


def ffn_b_scalar(act, b, f):
    cr = b.carry["act"]

    def shi(j):
        act.wait_ge(f["sT"], j + 1)
        act.sem_inc(cr, 1)
        hold(act, f["Ks"], j * 4, cr)
        act.copy(b.shT[0][:, :, :], b.bank(0).rearrange("p (c n) -> p c n", c=CC)).then_inc(f["shi"], 1)

    def relu(j, p):
        act.wait_ge(f["kbs"], j + 1)
        act.sem_inc(cr, 1)
        for q in range(HC // 2):
            act.wait_ge(f["Ks"], j * 4 + q + 1)
            act.sem_inc(cr, 1)
            if q >= 2 or not (isinstance(j, int) and j == 0):
                hold(act, f["sq"], j * 4 + q - 1, cr)
            for h in (2 * q, 2 * q + 1):
                last = act.activation(b.r[q % 2][:, (h % 2) * SLOT:(h % 2 + 1) * SLOT],
                                      b.bank(1 + q)[:, (h % 2) * SLOT:(h % 2 + 1) * SLOT], ACT.Relu,
                                      bias=b.kbs[p][:, h:h + 1])
            last.then_inc(f["relu"], 1)
            act.wait_ge(f["relu"], j * 4 + q + 1)
            act.sem_inc(cr, 1)
            if q == 0:
                hold(act, f["Vs"], j - 1, cr)
            act.activation(b.hr[p][0][:, 2 * q:2 * q + 2].rearrange("p h n -> p (h n)"), b.r[q % 2][:, :],
                           ACT.Square).then_inc(f["hrhi"], 1)

    def first():
        shi(0)
        relu(0, 0)
        shi(1)

    def body(j, p, last):
        relu(j, p)
        if not last:
            shi(j + 1)

    slots(act, first, body)


def ffn_b_vector(dve, b, f):
    cr = b.carry["dve"]

    def kbs(j, p):
        hold(dve, f["relu"], j * 4 - 4, cr)
        hold(dve, f["kbs"], j, cr)
        at = slice(j, j + 1) if isinstance(j, int) else bass.ds(j, 1)
        dve.tensor_scalar(b.kbt[:], b.kbias[:, 0], b.nflag[:, at], None, ALU.mult).then_inc(f["link"], 1)
        n[0] += 1
        hold(dve, f["link"], n[0] if isinstance(j, int) else base[0] + n[0], cr)
        dve.scalar_tensor_tensor(b.kbs[p][:], b.kbias[:, 1], b.flag[:, at], b.kbt[:], ALU.mult,
                                 ALU.add).then_inc(f["kbs"], 1)

    def slo(j):
        dve.wait_ge(f["shi"], j + 1)
        dve.sem_inc(cr, 1)
        dve.tensor_tensor(b.shT[1][:, :, :], b.bank(0).rearrange("p (c n) -> p c n", c=CC),
                          b.shT[0][:, :, :].bitcast(F32), ALU.subtract).then_inc(f["slo"], 1)

    def sq(j, p):
        for q in range(HC // 2):
            dve.wait_ge(f["relu"], j * 4 + q + 1)
            dve.sem_inc(cr, 1)
            if q >= 2 or not (isinstance(j, int) and j == 0):
                hold(dve, f["hrlo"], j * 4 + q - 1, cr)
            dve.tensor_tensor(b.sq[q % 2][:, :], b.r[q % 2][:, :], b.r[q % 2][:, :], ALU.mult).then_inc(f["sq"], 1)

    def orow(j, p, uses):
        dve.wait_ge(f["Vs"], j + 1)
        dve.sem_inc(cr, 1)
        hold(dve, f["o_out"][p], uses * 16 * ST, cr)
        hold(dve, f["r_in"][p], uses * 16 + 16, cr)
        dve.tensor_copy(b.idx[p][:], b.srow[p][:, :, C + 1].bitcast(I32))
        for t in range(ST):
            last = dve.scalar_tensor_tensor(b.o[p][:, t], b.bank(5)[:, t * C:(t + 1) * C],
                                            b.srow[p][:, t, C:C + 1], b.srow[p][:, t, 0:C], ALU.mult,
                                            ALU.add)
        last.then_inc(f["orow"], 1)

    n, base = [b.link_total], [0]

    def body(j, p, last, uses):
        if not last:
            kbs(j + 1, 1 - p)
        sq(j, p)
        if not last:
            slo(j + 1)
        orow(j - 1, 1 - p, uses)

    kbs(0, 0)
    slo(0)
    kbs(1, 1)
    sq(0, 0)
    slo(1)
    for j in (1, 2):
        body(j, j % 2, False, 0)
    n0 = n[0]
    with dve.Fori(0, (NSLOT - 5) // 2) as it:
        base[0] = it * 2
        for k in range(2):
            body(it * 2 + 3 + k, (3 + k) % 2, False, it + 1)
    n[0] = n0 + NSLOT - 5
    for j in (NSLOT - 2, NSLOT - 1):
        body(j, j % 2, j == NSLOT - 1, (j - 1) // 2)
    orow(NSLOT - 1, (NSLOT - 1) % 2, (NSLOT - 1) // 2)


def ffn_b_gpsimd(pool, b, f, dst):
    cr = b.carry["pool"]

    def hrlo(j, p):
        for q in range(HC // 2):
            pool.wait_ge(f["hrhi"], j * 4 + q + 1)
            pool.sem_inc(cr, 1)
            pool.wait_ge(f["sq"], j * 4 + q + 1)
            pool.sem_inc(cr, 1)
            pool.tensor_tensor(b.hr[p][1][:, 2 * q:2 * q + 2].rearrange("p h n -> p (h n)"), b.sq[q % 2][:, :],
                               b.hr[p][0][:, 2 * q:2 * q + 2].rearrange("p h n -> p (h n)").bitcast(F32),
                               ALU.subtract).then_inc(f["hrlo"], 1)

    def send(j, p):
        pool.wait_ge(f["orow"], j + 1)
        pool.sem_inc(cr, 1)
        for t in range(ST):
            pool.indirect_dma_start(dst, bass.IndirectOffsetOnAxis(b.idx[p][:, t:t + 1].bitcast(U32), 0),
                                    b.o[p][:, t, :], None, bounds_check=N - 1, oob_is_err=False
                                    ).then_inc(f["o_out"][p], 16)

    def body(j, p, last):
        hrlo(j, p)
        send(j - 1, 1 - p)

    slots(pool, lambda: hrlo(0, 0), body)
    send(NSLOT - 1, (NSLOT - 1) % 2)
    pool.wait_ge(f["o_out"][0], 16 * ST * ((NSLOT + 1) // 2))
    pool.wait_ge(f["o_out"][1], 16 * ST * (NSLOT // 2))



def pairs_before(q):
    return q * (q + 1) // 2


PAIRS = pairs_before(QB)


def sequences(eng, a, carry, run):
    with eng.Fori(0, BATCH) as bt:
        run(bt * QB, bt * PAIRS, bt)
        eng.drain().then_inc(a["sequence"], 1)
        hold(eng, a["sequence"], bt * 5 + 5, carry)


def attention_sync(sp, b, a):
    cr = b.carry["sp"]
    xin = b.x1.rearrange("(n t p) c -> n p t c", t=ST, p=P)
    xout = b.x2.rearrange("(n t p) c -> n p t c", t=ST, p=P)

    def run(n0, m0, bt):
        def load(q):
            if q >= AX_BUFS:
                hold(sp, a["y"], n0 + q - AX_BUFS + 1, cr)
            sp.dma_start(b.ax[q % AX_BUFS][:], xin[n0 + q]).then_inc(a["x_in"][q % AX_BUFS], 16)

        for q in range(AX_BUFS):
            load(q)
        for q in range(QB):
            sp.wait_ge(a["y"], n0 + q + 1)
            sp.sem_inc(cr, 1)
            sp.dma_start(xout[n0 + q], b.ao[:]).then_inc(a["out"], 16)
            if q + AX_BUFS < QB:
                load(q + AX_BUFS)
        sp.wait_ge(a["out"], (n0 + QB) * 16)
        sp.sem_inc(cr, 1)

    sequences(sp, a, cr, run)


def attention_tensor(pe, b, a):
    cr = b.carry["pe"]

    def run(n0, m0, bt):
        def zT(q):
            pe.wait_ge(a["z"], n0 + q + 1)
            pe.sem_inc(cr, 1)
            for c in range(CC):
                for t in range(ST):
                    mm = pe.transpose(b.bank(3)[:, c * SLOT + t * P:c * SLOT + (t + 1) * P],
                                      b.az[:, t, c * P:(c + 1) * P], b.ident[:])
            mm.then_inc(a["T"], 1)

        def project(q):
            pe.wait_ge(a["zlo"], n0 + q + 1)
            pe.sem_inc(cr, 1)
            for t in range(ST):
                for c in range(CC):
                    for p in range(2):
                        mm = pe.matmul(b.bank(3)[:, t * C:(t + 1) * C], b.azT[p][:, c, t * P:(t + 1) * P],
                                       b.Wvv[:, c], start=(c == 0 and p == 0), stop=(c == 1 and p == 1))
            mm.then_inc(a["vp"], 1)
            pe.wait_ge(a["vsum"], n0 + q + 1)
            pe.sem_inc(cr, 1)
            for m in range(2):
                for c in range(CC):
                    mm = passes(pe, b.bank(3)[:, m * SLOT:(m + 1) * SLOT], lambda p: b.Wqk[p][:, m, c],
                                lambda p: b.azT[p][:, c], c == 0, c == CC - 1)
            mm.then_inc(a["qk"], 1)

        def scores(q, t):
            pe.wait_ge(a["qklo"], n0 + q + 1)
            pe.sem_inc(cr, 1)
            if q or t:
                hold(pe, a["exp"], (n0 + q) * 2 + t, cr)
            keys = (q + 1) * SLOT
            for k0 in range(0, keys, 512):
                w = min(512, keys - k0)
                mm = passes(pe, b.bank(4 + k0 // 512)[:, 0:w], lambda p: b.qT[q % 2][p][:, t * P:(t + 1) * P],
                            lambda p: b.kT[p][:, k0:k0 + w])
            mm.then_inc(a["S"], 1)

        def turn(q, j):
            m = pairs_before(q) + j
            if m >= 2:
                hold(pe, a["ptlo"], m0 + m - 1, cr)
            for kt in range(2):
                for t in range(ST):
                    mm = pe.transpose(b.bank(m % 2)[:, kt * SLOT + t * P:kt * SLOT + (t + 1) * P],
                                      b.p[1 - q % 2][:, t, (2 * j + kt) * P:(2 * j + kt + 1) * P], b.ident[:])
            mm.then_inc(a["PT"], 1)

        def weigh(q, j):
            m = pairs_before(q) + j
            pe.wait_ge(a["ptlo"], m0 + m + 1)
            pe.sem_inc(cr, 1)
            if j == 0 and q:
                hold(pe, a["y"], n0 + q, cr)
            for kt in range(2):
                mm = passes(pe, b.bank(2)[:, 0:SLOT], lambda p: b.v[p][:, 2 * j + kt],
                            lambda p: b.pT[m % 2][p][:, kt], j == 0 and kt == 0, j == q and kt == 1)
            mm.then_inc(a["PV"], 1)

        def output(q):
            pe.wait_ge(a["olo"], n0 + q + 1)
            pe.sem_inc(cr, 1)
            for t in range(ST):
                mm = passes(pe, b.bank(2)[:, t * C:(t + 1) * C], lambda p: b.oT[p][:, t * P:(t + 1) * P],
                            lambda p: b.Wao[p][:])
            mm.then_inc(a["Y"], 1)

        def weigh_some(q, first, end):
            for j in range(first, end):
                weigh(q - 1, j)
                if j + 2 < q:
                    turn(q - 1, j + 2)

        zT(0)
        project(0)
        for q in range(QB + 1):
            if q:
                hold(pe, a["exp"], (n0 + q) * 2, cr)
            for j in range(min(2, q)):
                turn(q - 1, j)
            if q < QB:
                scores(q, 0)
            if q + 1 < QB:
                zT(q + 1)
            weigh_some(q, 0, q // 2)
            if q + 1 < QB:
                project(q + 1)
            if q < QB:
                scores(q, 1)
            weigh_some(q, q // 2, q)
            if q:
                output(q - 1)

    sequences(pe, a, cr, run)


def attention_scalar(act, b, a):
    cr = b.carry["act"]

    def run(n0, m0, bt):
        def z_hi(q):
            act.wait_ge(a["T"], n0 + q + 1)
            act.sem_inc(cr, 1)
            act.copy(b.azT[0][:, :, :], b.bank(3).rearrange("p (c n) -> p c n", c=CC)).then_inc(a["zhi"], 1)

        def project(q):
            act.wait_ge(a["vp"], n0 + q + 1)
            act.sem_inc(cr, 1)
            act.copy(b.vs[:, :, :], b.bank(3).rearrange("p (t n) -> p t n", t=ST)[:, :, 0:DK]).then_inc(a["vs"], 1)
            act.wait_ge(a["vsum"], n0 + q + 1)
            act.sem_inc(cr, 1)
            act.copy(b.v[0][:, 2 * q:2 * q + 2], b.vt[:, :, :]).then_inc(a["vhi"], 1)
            act.wait_ge(a["qk"], n0 + q + 1)
            act.sem_inc(cr, 1)
            act.copy(b.qT[q % 2][0][:, :], b.bank(3)[:, 0:SLOT])
            act.copy(b.kT[0][:, q * SLOT:(q + 1) * SLOT], b.bank(3)[:, SLOT:2 * SLOT]).then_inc(a["qkhi"], 1)

        def expo(q, t):
            keys = (q + 1) * SLOT
            act.wait_ge(a["nb"], (n0 + q) * 2 + t + 1)
            act.sem_inc(cr, 1)
            if q >= 2:
                hold(act, a["PT"], m0 + pairs_before(q - 1), cr)
            act.activation(b.p[1 - q % 2][:, t, 0:keys], b.ps4[:, :, :].rearrange("p a n -> p (a n)")[:, 0:keys],
                           ACT.Exp, bias=b.mx[:, 4 + q % 2, t:t + 1], scale=SCALE,
                           accum_out=b.sum[:, q % 2, t:t + 1]).then_inc(a["exp"], 1)

        def pairs(q, first, end):
            for j in range(first, end):
                m = pairs_before(q - 1) + j
                act.wait_ge(a["PT"], m0 + m + 1)
                act.sem_inc(cr, 1)
                if m >= 2:
                    hold(act, a["PV"], m0 + m - 1, cr)
                act.copy(b.pT[m % 2][0][:, :, :], b.bank(m % 2).rearrange("p (k n) -> p k n", k=2)
                         ).then_inc(a["pthi"], 1)

        def o_hi(q):
            act.wait_ge(a["PV"], m0 + pairs_before(q + 1))
            act.sem_inc(cr, 1)
            act.copy(b.oT[0][:, :], b.bank(2)[:, 0:SLOT]).then_inc(a["ohi"], 1)

        z_hi(0)
        project(0)
        for q in range(QB + 1):
            pairs(q, 0, min(2, q))
            if q < QB:
                expo(q, 0)
            if q + 1 < QB:
                z_hi(q + 1)
            pairs(q, min(2, q), min(q // 2 + 2, q))
            if q + 1 < QB:
                project(q + 1)
            if q < QB:
                expo(q, 1)
            pairs(q, min(q // 2 + 2, q), q)
            if q:
                o_hi(q - 1)

    sequences(act, a, cr, run)


ATT_LINKS = QB * (1 + 4 + 1)


def attention_vector(dve, b, a):
    cr = b.carry["dve"]

    def run(n0, m0, bt):
        links = [0]

        def link(ins):
            ins.then_inc(a["link"], 1)
            links[0] += 1
            hold(dve, a["link"], bt * ATT_LINKS + links[0], cr)

        def norm(q):
            x = b.ax[q % AX_BUFS]
            dve.wait_ge(a["x_in"][q % AX_BUFS], bt * (16 * QB // AX_BUFS) + 16 * (q // AX_BUFS + 1))
            dve.sem_inc(cr, 1)
            for t in range(ST):
                last = dve.bn_stats(b.st[:, 0, t], x[:, t])
            link(last)
            for t in range(ST):
                last = dve.bn_aggr(b.mv[:, 0, t], b.st[:, 0, t])
            last.then_inc(a["stats"], 1)

        def z(q):
            dve.wait_ge(a["rs"], n0 + q + 1)
            dve.sem_inc(cr, 1)
            if q:
                hold(dve, a["T"], n0 + q, cr)
            for t in range(ST):
                last = dve.tensor_scalar(b.az[:, t], b.ax[q % AX_BUFS][:, t], b.mv[:, 0, t, 0:1],
                                         b.rs[:, 1, 1, t:t + 1], ALU.subtract, ALU.mult)
            last.then_inc(a["z"], 1)

        def z_lo(q):
            dve.wait_ge(a["zhi"], n0 + q + 1)
            dve.sem_inc(cr, 1)
            dve.tensor_tensor(b.azT[1][:, :, :], b.bank(3).rearrange("p (c n) -> p c n", c=CC),
                              b.azT[0][:, :, :].bitcast(F32), ALU.subtract).then_inc(a["zlo"], 1)

        def project(q):
            dve.wait_ge(a["vs"], n0 + q + 1)
            dve.sem_inc(cr, 1)
            if q:
                hold(dve, a["vlo"], n0 + q, cr)
            dve.tensor_tensor(b.vt[:, :, :], b.bank(3).rearrange("p (t n) -> p t n", t=ST)[:, :, DK:2 * DK],
                              b.vs[:, :, :], ALU.add).then_inc(a["vsum"], 1)
            dve.wait_ge(a["vhi"], n0 + q + 1)
            dve.sem_inc(cr, 1)
            dve.tensor_tensor(b.v[1][:, 2 * q:2 * q + 2], b.vt[:, :, :], b.v[0][:, 2 * q:2 * q + 2].bitcast(F32),
                              ALU.subtract).then_inc(a["vlo"], 1)
            dve.wait_ge(a["qkhi"], n0 + q + 1)
            dve.sem_inc(cr, 1)
            dve.tensor_tensor(b.qT[q % 2][1][:, :], b.bank(3)[:, 0:SLOT], b.qT[q % 2][0][:, :].bitcast(F32),
                              ALU.subtract)
            at = slice(q * SLOT, (q + 1) * SLOT)
            dve.tensor_tensor(b.kT[1][:, at], b.bank(3)[:, SLOT:2 * SLOT], b.kT[0][:, at].bitcast(F32),
                              ALU.subtract).then_inc(a["qklo"], 1)

        def maxima(q, t):
            keys = (q + 1) * SLOT
            sc = b.ps4[:, :, :].rearrange("p a n -> p (a n)")
            dve.wait_ge(a["S"], (n0 + q) * 2 + t + 1)
            dve.sem_inc(cr, 1)
            link(dve.tensor_tensor(sc[:, keys - SLOT:keys], sc[:, keys - SLOT:keys], b.mask[:, t], ALU.add))
            link(dve.tensor_reduce(b.mx[:, 0, t:t + 1], sc[:, 0:keys], AX.X, ALU.max))
            dve.tensor_scalar(b.mx[:, 4 + q % 2, t:t + 1], b.mx[:, 0, t:t + 1], -SCALE, None, ALU.mult
                              ).then_inc(a["nb"], 1)

        def pairs(q, first, end):
            for j in range(first, end):
                m = pairs_before(q - 1) + j
                dve.wait_ge(a["pthi"], m0 + m + 1)
                dve.sem_inc(cr, 1)
                dve.tensor_tensor(b.pT[m % 2][1][:, :, :], b.bank(m % 2).rearrange("p (k n) -> p k n", k=2),
                                  b.pT[m % 2][0][:, :, :].bitcast(F32), ALU.subtract).then_inc(a["ptlo"], 1)

        def o_lo(q):
            dve.wait_ge(a["ohi"], n0 + q + 1)
            dve.sem_inc(cr, 1)
            dve.tensor_tensor(b.oT[1][:, :], b.bank(2)[:, 0:SLOT], b.oT[0][:, :].bitcast(F32),
                              ALU.subtract).then_inc(a["olo"], 1)

        def y(q):
            link(dve.reciprocal(b.mx[:, 2, :], b.sum[:, q % 2, :]))
            dve.wait_ge(a["Y"], n0 + q + 1)
            dve.sem_inc(cr, 1)
            if q:
                hold(dve, a["out"], (n0 + q) * 16, cr)
            for t in range(ST):
                last = dve.scalar_tensor_tensor(b.ao[:, t], b.bank(2)[:, t * C:(t + 1) * C], b.mx[:, 2, t:t + 1],
                                                b.ax[q % AX_BUFS][:, t], ALU.mult, ALU.add)
            last.then_inc(a["y"], 1)

        norm(0)
        z(0)
        z_lo(0)
        project(0)
        norm(1)
        z(1)
        for q in range(QB + 1):
            pairs(q, 0, min(2, q))
            if q < QB:
                maxima(q, 0)
            if q + 1 < QB:
                z_lo(q + 1)
            pairs(q, min(2, q), min(q // 2 + 2, q))
            if q + 1 < QB:
                project(q + 1)
            if q + 2 < QB:
                norm(q + 2)
            if q < QB:
                maxima(q, 1)
            if q + 2 < QB:
                z(q + 2)
            pairs(q, min(q // 2 + 2, q), q)
            if q:
                o_lo(q - 1)
                y(q - 1)
        assert links[0] == ATT_LINKS, links

    sequences(dve, a, cr, run)


def attention_gpsimd(pool, b, a):
    cr = b.carry["pool"]

    def run(n0, m0, bt):
        for q in range(QB):
            pool.wait_ge(a["stats"], n0 + q + 1)
            pool.sem_inc(cr, 1)
            var, t, r = (v[:, 0:ST] for v in (b.mv[:, 0, :, 1], b.rs[:, 1, 0], b.rs[:, 1, 1]))
            if q:
                hold(pool, a["z"], n0 + q, cr)
            pool.tensor_scalar(t, var, EPS, 0.0, ALU.add, ALU.add).then_inc(a["plink"], 1)
            pool.wait_ge(a["plink"], n0 + q + 1)
            pool.sem_inc(cr, 1)
            pool.tensor_tensor(r, t, b.half[:, 0:ST], ALU.pow).then_inc(a["rs"], 1)

    sequences(pool, a, cr, run)



def laid_out(inp):
    def chunks(w, k=CC):
        return w.reshape(k, P, -1).transpose(1, 0, 2).reshape(P, -1)

    g = lambda n: np.asarray(inp[n])
    f = "L0_ffn_"
    bid = np.zeros((C, BIDS), np.float32)
    bid[:, 0:2] = g(f + "conf_rwkv").T
    bid[:, 2] = g(f + "conf_trans")
    bid[:, 3] = g(f + "w_diff")
    bid[:, 4:7] = g(f + "W_aff")
    t = np.arange(N, dtype=np.float32).reshape(N // P, P).T
    k = np.arange(P)
    tri = np.stack([(k[:, None] < k[None, :]), np.ones((P, P), bool)], 1).astype(np.float32)
    mask = np.zeros((P, ST, SLOT), np.float32)
    for i in range(ST):
        mask[:, i] = np.where(np.arange(SLOT)[None, :] > k[:, None] + i * P, np.float32(-3e38), np.float32(0))
    slot_row = np.zeros((P, NSLOT + ST), np.float32)
    slot_row[:, 0:NSLOT] = np.arange(NSLOT) * SLOT
    slot_row[:, NSLOT:] = N + k[:, None] + P * np.arange(ST)
    return {
        "x": g("L0_attn_x").reshape(N, C),
        "w256": np.concatenate([chunks(g(f + n)) for n in ("Wr", "Wv", "W1", "Wo")], 1),
        "w_st": np.concatenate([chunks(g(f + "Ws").T), chunks(g(f + "W2")), chunks(g(f + "W3")), chunks(bid)], 1),
        "k_w": np.stack([chunks(g(f + "K_rwkv")[e]) for e in range(2)], 1),
        "v_w": np.stack([chunks(g(f + "V_rwkv")[e], HC) for e in range(2)], 1),
        "w_qkv": np.concatenate([chunks(g("L0_attn_" + n)) for n in ("Wq", "Wk", "Wv")] + [g("L0_attn_Wo")], 1),
        "ln": np.concatenate([g(f + n).reshape(CC, P).T for n in ("ln1_w", "ln1_b", "ln2_w", "ln2_b")], 1
                             ).reshape(P, 4, CC),
        "shares": np.broadcast_to(g(f + "capital_shares")[None, :], (P, 3)),
        "ident": np.eye(P, dtype=np.float32),
        "tri": tri,
        "mask": mask,
        "tok": np.stack([t, ROWS - 1 - t], 1),
        "slot_row": slot_row,
    }


def kernel(**inputs):
    import concourse.bacc as bacc
    from concourse.bass_utils import run_bass_kernel_spmd as run

    nc = bacc.Bacc("TRN2", target_bir_lowering=False, num_devices=1)
    arrays, args = {}, {}
    for name, v in laid_out(inputs).items():
        v = np.ascontiguousarray(v)
        arrays[f"in_{name}"] = v
        args[name] = nc.dram_tensor(f"in_{name}", v.shape, mybir.dt.from_np(v.dtype), kind="ExternalInput").ap()
    out = nc.dram_tensor("out_x", (N, C), F32, kind="ExternalOutput").ap()
    build_kernel(nc, **args, out=out)
    r = run(nc, [arrays], core_ids=[0])
    return r.results[0]["out_x"].reshape(BATCH, SEQ, C)
```

```python
from contextlib import ExitStack

import numpy as np
import concourse.bass as bass
from concourse import mybir

F32, F32R = mybir.dt.float32, mybir.dt.float32r
BF16, I32, U32 = mybir.dt.bfloat16, mybir.dt.int32, mybir.dt.uint32
ALU, ACT, AX = mybir.AluOpType, mybir.ActivationFunctionType, mybir.AxisListType

P = 128
EPS = 1e-5
BATCH, SEQ, C = 2, 2048, 256
N = BATCH * SEQ
CC = C // P
HID = 1024
HC = HID // P
DK = 128
GT = 4
GROUP = GT * P
NG = N // GROUP
ST = 2
SLOT = ST * P
NSLOT = N // SLOT + 1
ROWS = NSLOT * SLOT
ROW = 2 * C + 2
BIDS = 8
QB = SEQ // SLOT
KEYS = 512
SCALE = float(DK) ** -0.5
AX_BUFS = 6
PASSES = ((0, 0), (1, 0), (0, 1))


class Named:
    pass


def hold(eng, sem, value, carrier):
    if isinstance(value, int) and value <= 0:
        return
    eng.wait_ge(sem, value)
    apart(eng, carrier, value)


def apart(eng, carrier, value):
    if not isinstance(value, int):
        eng.sem_inc(carrier, 1)


def build_kernel(nc, x, w256, w_st, k_w, v_w, w_qkv, ln, shares, ident, tri, mask, tok, slot_row, out):
    with ExitStack() as ctx:
        def sb(name, shape, dt=F32):
            return ctx.enter_context(nc.sbuf_tensor(name, shape, dt))

        def sem(name):
            return ctx.enter_context(nc.semaphore(name))

        b, s = Named(), Named()
        b.x1 = nc.dram_tensor("x_after_ffn1", (N, C), F32, kind="Internal").ap()
        b.x2 = nc.dram_tensor("x_after_attention", (N, C), F32, kind="Internal").ap()
        b.routed = [nc.dram_tensor(f"routed_rows{i}", (ROWS, ROW), F32, kind="Internal").ap() for i in range(2)]

        b.W = [sb(f"w_{p}", [P, 5, CC, C], F32R) for p in ("hi", "lo")]
        b.W3 = [sb(f"w3_{p}", [P, CC, C], F32R) for p in ("hi", "lo")]
        b.K = [sb(f"k_{p}", [P, 2, CC, HID], F32R) for p in ("hi", "lo")]
        b.V = [sb(f"v_{p}", [P, 2, HC, C], F32R) for p in ("hi", "lo")]
        b.Wb = sb("w_bid", [P, CC, P], F32R)
        b.Wqk = [sb(f"wqk_{p}", [P, 2, CC, DK], F32R) for p in ("hi", "lo")]
        b.Wvv = sb("wv_hilo", [P, CC, 2 * DK], F32R)
        b.Wao = [sb(f"wao_{p}", [P, C], F32R) for p in ("hi", "lo")]
        b.ln = sb("ln_cols", [P, 4, CC])
        b.ident = sb("ident_sb", [P, P])
        b.trif = sb("tri_f32", [P, 2, P])
        b.tri = sb("tri_sb", [P, 2, P], BF16)
        b.mask = sb("mask_sb", [P, ST, SLOT])
        b.tok = sb("tok_sb", [P, 2, N // P])
        b.slot_row = sb("slot_row_sb", [P, NSLOT + ST])
        b.shares = sb("shares_sb", [P, 3])
        b.bias = sb("bias_cols", [P, 4, CC])
        b.kbias = sb("k_bias", [P, 2, HC])
        b.bbias = sb("bid_bias", [P, 1])
        b.half = sb("minus_half", [P, 8])
        b.ones4 = sb("ones4", [P, GT])
        FA, RA = 13184, 12800
        af, ar = sb("arena_f32", [P, FA]), sb("arena_f32r", [P, RA], F32R)
        pos = {"f": 0, "r": 0}

        def view(which, *dims):
            n = int(np.prod(dims))
            start = pos[which]
            pos[which] += n
            assert pos[which] <= (FA if which == "f" else RA), (pos, dims)
            v = (af if which == "f" else ar)[:, start:start + n]
            if len(dims) == 2:
                v = v.rearrange("p (a b) -> p a b", a=dims[0])
            if len(dims) == 3:
                v = v.rearrange("p (a b c) -> p a b c", a=dims[0], b=dims[1])
            return v

        b.stage = [view("f", 4096) for _ in range(2)]
        b.raw_sf = view("f", CC, C)
        b.raw_w3 = b.stage[1][:, 2 * CC * C:3 * CC * C].rearrange("p (c n) -> p c n", c=CC)
        pos["f"] = pos["r"] = 0
        b.x = [view("f", GT, C) for _ in range(2)]
        b.z = view("f", GT, C)
        b.y = view("f", GT, C)
        b.rg = view("f", CC, GROUP)
        b.sg = [view("f", CC, GROUP) for _ in range(2)]
        b.xa = view("f", GT, C)
        b.rows = [view("f", GT, ROW) for _ in range(2)]
        b.bd = view("f", GROUP)
        b.zT = [view("r", CC, GROUP) for _ in range(2)]
        b.gT = [view("r", CC, GROUP) for _ in range(2)]
        b.hT = [view("r", CC, GROUP) for _ in range(2)]
        b.g2T = [view("r", CC, GROUP) for _ in range(2)]
        fa_end = pos["f"]
        pos["f"] = pos["r"] = 0
        b.sz = [view("f", ST, C) for _ in range(2)]
        b.srow = [view("f", ST, ROW - C) for _ in range(2)]
        b.r = [view("f", 2 * SLOT) for _ in range(2)]
        b.sq = [view("f", 2 * SLOT) for _ in range(2)]
        b.o = [view("f", ST, C) for _ in range(2)]
        b.shT = [view("r", CC, SLOT) for _ in range(2)]
        b.hr = [[view("r", HC, SLOT) for _ in range(2)] for _ in range(2)]
        pos["f"] = pos["r"] = 0
        b.ax = [view("f", ST, C) for _ in range(AX_BUFS)]
        b.az = view("f", ST, C)
        b.vt = view("f", ST, DK)
        b.vs = view("f", ST, DK)
        b.p = [view("f", ST, SEQ), view("f", ST, SEQ - SLOT)]
        b.ao = view("f", ST, C)
        b.azT = [view("r", CC, SLOT) for _ in range(2)]
        b.qT = [[view("r", SLOT) for _ in range(2)] for _ in range(2)]
        b.kT = [view("r", SEQ) for _ in range(2)]
        b.v = [view("r", SEQ // P, DK) for _ in range(2)]
        b.pT = [[view("r", 2, SLOT) for _ in range(2)] for _ in range(2)]
        b.oT = [view("r", SLOT) for _ in range(2)]
        b.st = sb("bn_parts", [P, 2, GT, 6])
        b.mv = sb("mean_var", [P, 2, GT, 2])
        b.rs = sb("rsqrt_work", [P, 2, 6, GT])
        b.bid = sb("bid_rows", [P, GT, BIDS])
        b.conf = sb("conf_rows", [P, GT, 4])
        b.gw = sb("gate_work", [P, 12, GT])
        b.gt = [sb(f"trans_gate{i}", [P, GT]) for i in range(2)]
        b.cnt = sb("expert1_count", [P, GT + 1])
        b.e16 = sb("expert1_bf16", [P, 2 * GT + 2], BF16)
        b.posi = [sb(f"row_index{i}", [P, GT], I32) for i in range(2)]
        b.padrow = sb("pad_rows", [P, ROW])
        b.padi = sb("pad_index", [P, ST], I32)
        b.n1 = sb("n_expert1", [P, 1])
        b.flag = sb("slot_expert", [P, NSLOT])
        b.flagi = sb("slot_expert_int", [P, NSLOT], I32)
        b.nflag = sb("slot_expert0", [P, NSLOT])
        b.idx = [sb(f"token_index{i}", [P, ST], I32) for i in range(2)]
        b.kbt = sb("slot_k_bias_part", [P, HC])
        b.kbs = [sb(f"slot_k_bias{i}", [P, HC]) for i in range(2)]
        b.mx = sb("row_max", [P, 8, ST])
        b.sum = sb("row_sum", [P, 2, ST])
        b.cmax = sb("chunk_max", [P, ST, SEQ // KEYS])
        b.csum = sb("chunk_sum", [P, 2, ST, SEQ // KEYS])

        b.ps = [ctx.enter_context(nc.psum_tensor(f"bank{i}", [P, 512], F32)) for i in range(4)]
        b.ps4 = ctx.enter_context(nc.psum_tensor("banks4to7", [P, 4, 512], F32))
        b.bank = lambda i: b.ps[i][:, :] if i < 4 else b.ps4[:, i - 4, :]

        b.carry = {e: sem(f"carry_{e}") for e in ("pe", "act", "dve", "pool", "sp")}
        s.barrier, s.fence = sem("phase_done"), sem("fence")
        s.const = sem("const_loaded")
        s.stage = [sem(f"stage_loaded{i}") for i in range(2)]
        s.w_hi, s.pe_set, s.set_done = sem("w_hi"), sem("pe_setup"), sem("setup_done")
        s.memz, s.w_raw, s.link0 = sem("wb_zeroed"), sem("w_s_w_2"), sem("pad_row_zero")
        names = ("stats1", "rs1", "z1", "y1", "T1", "zhi", "zlo", "U", "sigr", "gv", "sigs", "ghi", "glo", "Wo",
                 "x2", "stats2", "rs2", "z2", "T2", "hhi", "hlo", "bid", "bd", "bidT", "b7", "conf", "e", "pref",
                 "posr", "W", "g2", "g2hi", "g2lo", "W3", "rdone", "link", "plink", "n1", "flag", "padi",
                 "sT", "shi", "slo", "Ks", "relu", "hrhi", "sq", "hrlo", "kbs", "Vs", "orow", "res")
        shared = {n: sem(f"f_{n}") for n in names}
        pairs = {n: [sem(f"f_{n}{k}") for k in range(2)] for n in ("x_in", "r_in", "s_in")}
        s.cleared = [*shared.values(), *(one for pair in pairs.values() for one in pair)]
        s.ffn = [dict(shared, **pairs, pad=sem(f"f{i}_pad"), scat=[sem(f"f{i}_scattered{k}") for k in range(2)],
                      o_out=[sem(f"f{i}_slot_out{k}") for k in range(2)]) for i in range(2)]
        names = ("stats", "rs", "z", "T", "zhi", "zlo", "vp", "vs", "vsum", "vhi", "vlo", "qk", "qkhi", "qklo", "S", "nb",
                 "exp", "PT", "pthi", "ptlo", "PV", "ohi", "olo", "Y", "y", "link", "plink", "sequence")
        s.a = dict({n: sem(f"a_{n}") for n in names}, out=sem("a_out"), x_in=[sem(f"a_x_in{k}") for k in range(AX_BUFS)])

        block = ctx.enter_context(nc.Block())
        src = [x, b.x2]
        dst = [b.x1, out]

        def barrier(eng, k):
            eng.drain().then_inc(s.barrier, 1)
            eng.wait_ge(s.barrier, 5 * k)
            eng.sem_inc(s.fence, 1)

        loads = ([("w", w256, 4 * CC * C), ("sf", w_st, 3 * CC * C + CC * BIDS)]
                 + [("k", k_w[:, e], CC * HID) for e in range(2)] + [("v", v_w[:, e], HC * C) for e in range(2)]
                 + [("a", w_qkv, 3 * CC * DK + C)])
        SF = 3 * CC * C

        @block.sync
        def _(sp):
            c = b.carry["sp"]
            for dstv, srcv in ((b.ln, ln), (b.ident, ident), (b.trif, tri), (b.mask, mask), (b.tok, tok),
                               (b.slot_row, slot_row), (b.shares, shares)):
                sp.dma_start(dstv[:], srcv).then_inc(s.const, 16)
            for n, (_, w, cols) in enumerate(loads):
                if n >= 2:
                    sp.wait_ge(s.set_done, n - 1)
                sp.dma_start(b.stage[n % 2][:, 0:cols], w).then_inc(s.stage[n % 2], 16)
            barrier(sp, 1)
            for i in range(2):
                f = s.ffn[i]
                xg = src[i].rearrange("(g t p) c -> g p t c", t=GT, p=P)
                for g in range(2):
                    sp.dma_start(b.x[g][:], xg[g]).then_inc(f["x_in"][g], 16)
                with sp.Fori(0, NG // 2 - 1) as it:
                    for par in range(2):
                        g = it * 2 + 2 + par
                        hold(sp, f["res"], g - 1, c)
                        sp.dma_start(b.x[par][:], xg[g]).then_inc(f["x_in"][par], 16)
                sp.wait_ge(f["res"], NG - 1)
                sp.dma_start(b.x[0][:], xg[NG - 2]).then_inc(f["x_in"][0], 16)
                sp.wait_ge(f["x_in"][0], 16 * (NG // 2 + 1))
                barrier(sp, 2 + 3 * i)
                rg = b.routed[i].rearrange("(j t p) c -> j p t c", t=ST, p=P)

                def slot_in(j, p):
                    hold(sp, f["sT"], j - 1, c)
                    sp.dma_start(b.sz[p][:], rg[j][:, :, 0:C]).then_inc(f["s_in"][p], 16)
                    hold(sp, f["orow"], j - 1, c)
                    sp.dma_start(b.srow[p][:], rg[j][:, :, C:ROW]).then_inc(f["r_in"][p], 16)

                for j in range(2):
                    slot_in(j, j)
                with sp.Fori(0, (NSLOT - 3) // 2) as it:
                    for par in range(2):
                        slot_in(it * 2 + 2 + par, par)
                slot_in(NSLOT - 1, 0)
                barrier(sp, 3 + 3 * i)
                if i == 0:
                    for one in s.cleared:
                        sp.sem_clear(one)
                    attention_sync(sp, b, s.a)
                    barrier(sp, 4)

        @block.tensor
        def _(pe):
            setup_tensor(pe, b, s, loads, SF)
            barrier(pe, 1)
            for i in range(2):
                ffn_a_tensor(pe, b, s.ffn[i])
                barrier(pe, 2 + 3 * i)
                ffn_b_tensor(pe, b, s.ffn[i])
                barrier(pe, 3 + 3 * i)
                if i == 0:
                    attention_tensor(pe, b, s.a)
                    barrier(pe, 4)

        @block.scalar
        def _(act):
            setup_scalar(act, b, s, SF)
            barrier(act, 1)
            for i in range(2):
                ffn_a_scalar(act, b, s.ffn[i])
                barrier(act, 2 + 3 * i)
                ffn_b_scalar(act, b, s.ffn[i])
                barrier(act, 3 + 3 * i)
                if i == 0:
                    attention_scalar(act, b, s.a)
                    barrier(act, 4)

        @block.vector
        def _(dve):
            setup_vector(dve, b, s, SF)
            barrier(dve, 1)
            for i in range(2):
                ffn_a_vector(dve, b, s.ffn[i])
                barrier(dve, 2 + 3 * i)
                ffn_b_vector(dve, b, s.ffn[i])
                barrier(dve, 3 + 3 * i)
                if i == 0:
                    attention_vector(dve, b, s.a)
                    barrier(dve, 4)

        @block.gpsimd
        def _(pool):
            pool.memset(b.half[:], -0.5).then_inc(s.memz, 1)
            barrier(pool, 1)
            for i in range(2):
                ffn_a_gpsimd(pool, b, s.ffn[i], b.routed[i])
                barrier(pool, 2 + 3 * i)
                ffn_b_gpsimd(pool, b, s.ffn[i], dst[i])
                barrier(pool, 3 + 3 * i)
                if i == 0:
                    attention_gpsimd(pool, b, s.a)
                    barrier(pool, 4)



def split_plan(b, SF):
    plan = []
    st = b.stage
    w = st[0][:, 0:4 * CC * C].rearrange("p (m c n) -> p m c n", m=4, c=CC)
    for m, (to, row) in enumerate(((0, 0), (1, 0), (3, 2), (4, None))):
        for c in range(CC):
            plan.append((0, w[:, m, c], None if row is None else b.ln[:, row, c:c + 1],
                         b.W[0][:, to, c], b.W[1][:, to, c]))
    for c in range(CC):
        plan.append((1, b.raw_sf[:, c], b.ln[:, 0, c:c + 1], b.W[0][:, 2, c], b.W[1][:, 2, c]))
    sf = st[1]
    for c in range(CC):
        plan.append((1, b.raw_w3[:, c], None, b.W3[0][:, c], b.W3[1][:, c]))
    wb = sf[:, SF:SF + CC * BIDS].rearrange("p (c n) -> p c n", c=CC)
    for c in range(CC):
        plan.append((1, wb[:, c], b.ln[:, 2, c:c + 1], b.Wb[:, c, 0:BIDS], b.Wb[:, c, BIDS:2 * BIDS]))
    for e in range(2):
        k = st[e % 2][:, 0:CC * HID].rearrange("p (c n) -> p c n", c=CC)
        for c in range(CC):
            plan.append((2 + e, k[:, c], b.ln[:, 2, c:c + 1], b.K[0][:, e, c], b.K[1][:, e, c]))
    for e in range(2):
        v = st[e % 2][:, 0:HC * C].rearrange("p (h n) -> p h n", h=HC)
        plan.append((4 + e, v, None, b.V[0][:, e], b.V[1][:, e]))
    a = st[0]
    qkv = a[:, 0:3 * CC * DK].rearrange("p (m c n) -> p m c n", m=3, c=CC)
    for m in range(2):
        plan.append((6, qkv[:, m], None, b.Wqk[0][:, m], b.Wqk[1][:, m]))
    for c in range(CC):
        plan.append((6, qkv[:, 2, c], None, b.Wvv[:, c, 0:DK], b.Wvv[:, c, DK:2 * DK]))
    plan.append((6, a[:, 3 * CC * DK:3 * CC * DK + C], None, b.Wao[0][:], b.Wao[1][:]))
    return plan


def setup_scalar(act, b, s, SF):
    act.wait_ge(s.const, 16 * 7)
    act.wait_ge(s.memz, 3)
    load = -1
    for n, (ld, raw, scale, hi, _) in enumerate(split_plan(b, SF)):
        if ld != load:
            load = ld
            act.wait_ge(s.stage[ld % 2], 16 * (ld // 2 + 1))
            if ld == 1:
                act.wait_ge(s.pe_set, 2)
                act.copy(b.raw_sf[:, :, :], b.bank(1).rearrange("p (c n) -> p c n", c=CC)).then_inc(s.w_raw, 1)
                act.wait_ge(s.w_raw, 1)
        if scale is None:
            act.copy(hi, raw).then_inc(s.w_hi, 1)
        else:
            act.mul(hi, raw, scale).then_inc(s.w_hi, 1)


def setup_vector(dve, b, s, SF):
    dve.memset(b.Wb[:].bitcast(F32), 0.0).then_inc(s.memz, 1)
    dve.memset(b.bbias[:], 0.0).then_inc(s.memz, 1)
    dve.memset(b.ones4[:], 1.0)
    dve.memset(b.cnt[:], 0.0)
    dve.memset(b.padrow[:], 0.0).then_inc(s.link0, 1)
    dve.wait_ge(s.link0, 1)
    dve.memset(b.padrow[:, 2 * C + 1:ROW].bitcast(I32), ROWS)
    dve.wait_ge(s.const, 16 * 7)
    dve.tensor_copy(b.tri[:], b.trif[:])
    plan = split_plan(b, SF)
    for n, (ld, raw, scale, hi, lo) in enumerate(plan):
        dve.wait_ge(s.w_hi, n + 1)
        last = dve.scalar_tensor_tensor(lo, raw, 1.0 if scale is None else scale, hi.bitcast(F32), ALU.mult,
                                        ALU.subtract)
        if n + 1 == len(plan) or plan[n + 1][0] != ld:
            if ld == 0:
                dve.wait_ge(s.pe_set, 1)
                for m in (0, 1, 3):
                    last = dve.tensor_copy(b.bias[:, m, :], b.bank(0)[:, m * CC:(m + 1) * CC])
            elif ld == 1:
                dve.wait_ge(s.pe_set, 3)
                dve.wait_ge(s.memz, 3)
                dve.tensor_copy(b.bias[:, 2, :], b.bank(2)[:, 0:CC])
                last = dve.tensor_copy(b.bbias[0:BIDS, :], b.bank(2)[0:BIDS, 2 * CC:2 * CC + 1])
            elif ld in (2, 3):
                dve.wait_ge(s.pe_set, 2 + ld)
                last = dve.tensor_copy(b.kbias[:, ld - 2, :], b.bank(ld - 2)[:, 16:16 + HC])
            last.then_inc(s.set_done, 1)


def setup_tensor(pe, b, s, loads, SF):
    def column(bank, col, raw, m, row, size=P):
        for c in range(CC):
            mm = pe.matmul(bank[0:size, col:col + 1], raw(c)[:, m:m + size], b.ln[:, row, c:c + 1],
                           start=(c == 0), stop=(c == CC - 1))
        return mm

    pe.wait_ge(s.const, 16 * 7)
    pe.wait_ge(s.stage[0], 16)
    w = b.stage[0][:, 0:4 * CC * C].rearrange("p (m c n) -> p m c n", m=4, c=CC)
    for m, (to, row) in enumerate(((0, 1), (1, 1), (3, 3))):
        for f in range(CC):
            mm = column(b.bank(0), to * CC + f, lambda c, m=m: w[:, m, c], f * P, row)
    mm.then_inc(s.pe_set, 1)
    pe.wait_ge(s.stage[1], 16)
    sf = b.stage[1][:, 0:2 * CC * C].rearrange("p (m c n) -> p m c n", m=2, c=CC)
    for o in range(CC):
        for k in range(CC):
            mm = pe.matmul(b.bank(1)[:, o * C:(o + 1) * C], sf[:, 0, k, o * P:(o + 1) * P], sf[:, 1, k],
                           start=(k == 0), stop=(k == CC - 1))
    mm.then_inc(s.pe_set, 1)
    pe.wait_ge(s.w_raw, 1)
    for f in range(CC):
        column(b.bank(2), f, lambda c: b.raw_sf[:, c], f * P, 1)
    wb = b.stage[1][:, SF:SF + CC * BIDS].rearrange("p (c n) -> p c n", c=CC)
    column(b.bank(2), 2 * CC, lambda c: wb[:, c], 0, 3, BIDS).then_inc(s.pe_set, 1)
    for e in range(2):
        pe.wait_ge(s.stage[e], 32)
        k = b.stage[e][:, 0:CC * HID].rearrange("p (c n) -> p c n", c=CC)
        if e == 0:
            pe.wait_ge(s.set_done, 1)
        else:
            pe.wait_ge(s.set_done, 2)
        for h in range(HC):
            mm = column(b.bank(e), 16 + h, lambda c: k[:, c], h * P, 3)
        mm.then_inc(s.pe_set, 1)



def passes(pe, outv, w, m, n_first=True, n_last=True):
    for k, (pw, pm) in enumerate(PASSES):
        mm = pe.matmul(outv, w(pw), m(pm), start=(n_first and k == 0), stop=(n_last and k == 2))
    return mm


def ffn_a_tensor(pe, b, f):
    cr = b.carry["pe"]

    def T1(g):
        pe.wait_ge(f["z1"], g + 1)
        apart(pe, cr, g)
        hold(pe, f["hlo"], 2 * g - 2, cr)
        for c in range(CC):
            for t in range(GT):
                mm = pe.transpose(b.bank(c)[:, t * P:(t + 1) * P], b.z[:, t, c * P:(c + 1) * P], b.ident[:])
        mm.then_inc(f["T1"], 1)

    def U(g, between=None):
        pe.wait_ge(f["zlo"], 2 * g + 2)
        apart(pe, cr, g)
        for n, (m, fc) in enumerate(((0, 0), (1, 0), (0, 1), (1, 1), (2, 0), (2, 1))):
            if n == 2 and between:
                between()
            if n == 0:
                hold(pe, f["bd"], g - 1, cr)
            if n == 1:
                hold(pe, f["g2"], g * 2 - 3, cr)
            if n == 2:
                hold(pe, f["g2"], g * 2 - 2, cr)
            if n == 3:
                pe.wait_ge(f["sigr"], g * 2 + 1)
                apart(pe, cr, g)
            if n == 4:
                pe.wait_ge(f["gv"], g * 2 + 1)
                apart(pe, cr, g)
            if n == 5:
                pe.wait_ge(f["sigr"], g * 2 + 2)
                apart(pe, cr, g)
            for c in range(CC):
                mm = passes(pe, b.bank(2 + n % 3), lambda p: b.W[p][:, m, c, fc * P:(fc + 1) * P],
                            lambda p: b.zT[p][:, c], c == 0, c == CC - 1)
            mm.then_inc(f["U"], 1)

    def rows_out(g, act, w, bank0, done):
        for t in range(GT):
            for c in range(CC):
                mm = passes(pe, b.bank(bank0 + t // 2)[:, (t % 2) * C:(t % 2 + 1) * C],
                            lambda p: act[p][:, c, t * P:(t + 1) * P], lambda p: w(p, c), c == 0, c == CC - 1)
            if t % 2:
                mm.then_inc(done, 1)

    def Wo(g):
        pe.wait_ge(f["glo"], 2 * g + 2)
        apart(pe, cr, g)
        hold(pe, f["rdone"], g - 1, cr)
        rows_out(g, b.gT, lambda p, c: b.W[p][:, 4, c], 6, f["Wo"])

    def T2(g):
        pe.wait_ge(f["z2"], g + 1)
        apart(pe, cr, g)
        pe.wait_ge(f["zlo"], 2 * g + 4)
        apart(pe, cr, g)
        for c in range(CC):
            for t in range(GT):
                mm = pe.transpose(b.bank(c)[:, t * P:(t + 1) * P], b.rows[g_par(g)][:, t, c * P:(c + 1) * P],
                                  b.ident[:])
        mm.then_inc(f["T2"], 1)

    def bids(g):
        pe.wait_ge(f["hlo"], 2 * g + 2)
        apart(pe, cr, g)
        pe.wait_ge(f["gv"], gnext(g) * 2 + 2)
        apart(pe, cr, g)
        for c in range(CC):
            for p in range(2):
                mm = pe.matmul(b.bank(2), b.Wb[:, c], b.hT[p][:, c], start=(c == 0 and p == 0), stop=(c == 1 and p == 1))
        mm.then_inc(f["bid"], 1)

    def W1(g):
        for fc in range(CC):
            pe.wait_ge(f["sigs"], gnext(g) * 2 + 1 + fc)
            apart(pe, cr, g)
            for c in range(CC):
                mm = passes(pe, b.bank(3 + fc), lambda p: b.W[p][:, 3, c, fc * P:(fc + 1) * P],
                            lambda p: b.hT[p][:, c], c == 0, c == CC - 1)
            mm.then_inc(f["W"], 1)

    def bidT(g):
        pe.wait_ge(f["bd"], g + 1)
        apart(pe, cr, g)
        hold(pe, f["posr"], g, cr)
        for t in range(GT):
            mm = pe.transpose(b.bank(5)[:, t * P:(t + 1) * P], b.bd[:, t * P:(t + 1) * P], b.ident[:])
        mm.then_inc(f["bidT"], 1)

    def W3(g):
        pe.wait_ge(f["g2lo"], 2 * g + 2)
        apart(pe, cr, g)
        pe.wait_ge(f["x2"], gnext(g) * 2 + 2)
        apart(pe, cr, g)
        rows_out(g, b.g2T, lambda p, c: b.W3[p][:, c], 6, f["W3"])

    def prefix(g):
        pe.wait_ge(f["e"], g + 1)
        apart(pe, cr, g)
        pe.matmul(b.bank(5)[:, 0:GT], b.tri[:, 0], b.e16[:, 0:GT], start=True, stop=False)
        pe.matmul(b.bank(5)[:, 0:GT], b.tri[:, 1], b.e16[:, GT:2 * GT], start=False, stop=True).then_inc(f["pref"], 1)

    par = [0]

    def g_par(g):
        return par[0]

    def gnext(g):
        return g if isinstance(g, int) and g == NG - 1 else g + 1

    def body(g, p, last=False):
        par[0] = p
        def W3_before():
            W3(g - 1)
            prefix(g - 1)

        if last:
            W3_before()
        else:
            U(g + 1, None if isinstance(g, int) and g == 0 else W3_before)
        T2(g)
        if not last:
            Wo(g + 1)
            T1(g + 2)
        bids(g)
        W1(g)
        bidT(g)

    T1(0)
    U(0)
    T1(1)
    Wo(0)
    body(0, 0)
    with pe.Fori(0, (NG - 2) // 2) as it:
        for k in range(2):
            body(it * 2 + 1 + k, (1 + k) % 2)
    body(NG - 1, (NG - 1) % 2, True)
    W3(NG - 1)
    prefix(NG - 1)
    pe.wait_ge(f["posr"], NG)
    pe.matmul(b.bank(5)[:, 0:1], b.tri[:, 1], b.e16[:, 2 * GT:2 * GT + 1], start=True, stop=True).then_inc(f["n1"], 1)


def ffn_a_scalar(act, b, f):
    cr = b.carry["act"]

    def y(g):
        act.wait_ge(f["rs1"], g + 1)
        apart(act, cr, g)
        hold(act, f["x2"], g * 2, cr)
        for t in range(GT):
            last = act.activation(b.y[:, t], b.x[par(g)][:, t], ACT.Identity, bias=b.rs[:, 0, 3, t:t + 1],
                                  scale=b.rs[:, 0, 1, t:t + 1])
        last.then_inc(f["y1"], 1)

    def z(g, p):
        act.wait_ge(f["rs1"], g + 1)
        apart(act, cr, g)
        hold(act, f["T1"], g, cr)
        for t in range(GT):
            last = act.activation(b.z[:, t], b.x[p][:, t], ACT.Identity, bias=b.rs[:, 0, 5, t:t + 1],
                                  scale=b.rs[:, 0, 2, t:t + 1])
        last.then_inc(f["z1"], 1)

    def z2(g, p):
        act.wait_ge(f["rs2"], g + 1)
        apart(act, cr, g)
        act.wait_ge(f["res"], g + 1)
        apart(act, cr, g)
        for t in range(GT):
            last = act.activation(b.rows[p][:, t, 0:C], b.xa[:, t], ACT.Identity, bias=b.rs[:, 1, 5, t:t + 1],
                                  scale=b.rs[:, 1, 2, t:t + 1])
        last.then_inc(f["z2"], 1)

    pp = [0]

    def par(g):
        return pp[0]

    def hi(g, T, bank, to, done, prev):
        act.wait_ge(T, g + 1)
        apart(act, cr, g)
        if prev is not None:
            hold(act, prev[0], prev[1], cr)
        for c in range(CC):
            act.copy(to[0][:, c], b.bank(bank + c)).then_inc(done, 1)

    def sig_r(g, fc):
        hold(act, f["U"], g * 6 + 1 + 2 * fc, cr)
        hold(act, f["glo"], g * 2, cr)
        act.activation(b.rg[:, fc], b.bank(2 + 2 * fc), ACT.Sigmoid, bias=b.bias[:, 0, fc:fc + 1]).then_inc(f["sigr"], 1)

    def g_hi(g, fc):
        act.wait_ge(f["gv"], g * 2 + 1 + fc)
        apart(act, cr, g)
        hold(act, f["Wo"], g * 2, cr)
        act.copy(b.gT[0][:, fc], b.rg[:, fc]).then_inc(f["ghi"], 1)

    def sig_s(g, fc):
        act.wait_ge(f["U"], g * 6 + 5 + fc)
        apart(act, cr, g)
        hold(act, f["g2lo"], g * 2 - 2, cr)
        act.activation(b.sg[pp[0]][:, fc], b.bank(3 + fc), ACT.Sigmoid, bias=b.bias[:, 2, fc:fc + 1]).then_inc(f["sigs"], 1)

    def bd(g):
        act.wait_ge(f["bid"], g + 1)
        apart(act, cr, g)
        hold(act, f["bidT"], g, cr)
        act.activation(b.bd[:, :], b.bank(2), ACT.Identity, bias=b.bbias[:, 0:1]).then_inc(f["bd"], 1)

    def conf(g):
        act.wait_ge(f["b7"], g + 1)
        apart(act, cr, g)
        act.activation(b.conf[:], b.bid[:, :, 0:4], ACT.Sigmoid).then_inc(f["conf"], 1)

    def g2_hi(g, fc, p):
        act.wait_ge(f["g2"], g * 2 + 1 + fc)
        apart(act, cr, g)
        if fc == 0:
            hold(act, f["W3"], g * 2, cr)
        act.copy(b.g2T[0][:, fc], b.sg[p][:, fc]).then_inc(f["g2hi"], 1)

    def mix(g, p, between=None):
        pp[0] = p
        sig_r(g, 0)
        if between:
            between()
        y(g)
        sig_r(g, 1)
        g_hi(g, 0)
        g_hi(g, 1)

    def z_hi(g):
        hi(g, f["T1"], 0, b.zT, f["zhi"], (f["U"], g * 6))

    def h_hi(g):
        hi(g, f["T2"], 0, b.hT, f["hhi"], (f["W"], g * 2))

    def body(g, p, last=False):
        if not last:
            mix(g + 1, 1 - p, lambda: z2(g, p))
        else:
            z2(g, p)
        h_hi(g)
        if not last:
            z(g + 2, p)
            sig_s(g + 1, 0)
            sig_s(g + 1, 1)
            z_hi(g + 2)
        bd(g)
        g2_hi(g, 0, p)
        g2_hi(g, 1, p)
        conf(g)

    z(0, 0)
    z_hi(0)
    mix(0, 0)
    sig_s(0, 0)
    sig_s(0, 1)
    z(1, 1)
    z_hi(1)
    body(0, 0)
    with act.Fori(0, (NG - 2) // 2) as it:
        for k in range(2):
            body(it * 2 + 1 + k, (1 + k) % 2)
    body(NG - 1, (NG - 1) % 2, True)


def ffn_a_gpsimd(pool, b, f, routed):
    cr = b.carry["pool"]
    n = [0]

    def link(ins, v):
        ins.then_inc(f["plink"], 1)
        n[0] += 1
        hold(pool, f["plink"], v(n[0]), cr)

    def rs1(g, v):
        pool.wait_ge(f["stats1"], g + 1)
        apart(pool, cr, g)
        hold(pool, f["y1"], g, cr)
        hold(pool, f["z1"], g, cr)
        mean, var = b.mv[:, 0, :, 0], b.mv[:, 0, :, 1]
        a, r1, r, sh1, nm, sh = (b.rs[:, 0, k] for k in range(6))
        half = b.half[:, 0:GT]
        pool.tensor_scalar(nm, mean, -1.0, 0.0, ALU.mult, ALU.add)
        link(pool.tensor_scalar(a, var, EPS, 0.0, ALU.add, ALU.add), v)
        link(pool.tensor_tensor(r1, a, half, ALU.pow), v)
        pool.tensor_tensor(sh1, nm, r1, ALU.mult)
        link(pool.tensor_tensor(a, var, r1, ALU.mult), v)
        link(pool.tensor_tensor(a, a, r1, ALU.mult), v)
        link(pool.tensor_scalar(a, a, EPS, 0.0, ALU.add, ALU.add), v)
        link(pool.tensor_tensor(r, a, half, ALU.pow), v)
        link(pool.tensor_tensor(r, r, r1, ALU.mult), v)
        pool.tensor_tensor(sh, nm, r, ALU.mult).then_inc(f["rs1"], 1)

    def rs2(g, v):
        pool.wait_ge(f["stats2"], g + 1)
        apart(pool, cr, g)
        hold(pool, f["z2"], g, cr)
        mean, var = b.mv[:, 1, :, 0], b.mv[:, 1, :, 1]
        a, r, nm, sh = (b.rs[:, 1, k] for k in (0, 2, 4, 5))
        pool.tensor_scalar(nm, mean, -1.0, 0.0, ALU.mult, ALU.add)
        link(pool.tensor_scalar(a, var, EPS, 0.0, ALU.add, ALU.add), v)
        link(pool.tensor_tensor(r, a, b.half[:, 0:GT], ALU.pow), v)
        pool.tensor_tensor(sh, nm, r, ALU.mult).then_inc(f["rs2"], 1)

    def lo(g, fc, src, to, hi_sem, done):
        pool.wait_ge(hi_sem, g * 2 + 1 + fc)
        apart(pool, cr, g)
        pool.tensor_tensor(to[1][:, fc], src[:, fc], to[0][:, fc].bitcast(F32), ALU.subtract).then_inc(done, 1)

    def scatter(g, p):
        pool.wait_ge(f["rdone"], g + 1)
        apart(pool, cr, g)
        pool.wait_ge(f["posr"], g + 1)
        apart(pool, cr, g)
        for t in range(GT):
            pool.indirect_dma_start(routed, bass.IndirectOffsetOnAxis(b.posi[p][:, t:t + 1].bitcast(U32), 0),
                                    b.rows[p][:, t, :], None).then_inc(f["scat"][p], 16)

    def g2_lo(g, p):
        lo(g, 0, b.sg[p], b.g2T, f["g2hi"], f["g2lo"])

    def body(g, p, v, last=False):
        if not last:
            rs1(g + 2, v)
        if not (isinstance(g, int) and g == 0):
            scatter(g - 1, 1 - p)
        if not last:
            rs2(g + 1, v)
        g2_lo(g, p)

    PER = 9
    fixed = lambda k: k
    rs1(0, fixed)
    rs1(1, fixed)
    rs2(0, fixed)
    body(0, 0, fixed)
    with pool.Fori(0, (NG - 2) // 2) as it:
        for k in range(2):
            body(it * 2 + 1 + k, (1 + k) % 2, lambda q: it * (2 * PER) + q)
    body(NG - 1, (NG - 1) % 2, fixed, True)
    scatter(NG - 1, (NG - 1) % 2)
    pool.wait_ge(f["padi"], 1)
    for t in range(ST):
        pool.indirect_dma_start(routed, bass.IndirectOffsetOnAxis(b.padi[:, t:t + 1].bitcast(U32), 0),
                                b.padrow[:], None).then_inc(f["pad"], 16)
    pool.wait_ge(f["pad"], 16 * ST)
    for p in range(2):
        pool.wait_ge(f["scat"][p], 16 * GT * NG // 2)


def ffn_a_vector(dve, b, f):
    cr = b.carry["dve"]
    n = [0]
    pp = [0]

    def stats(which, src, t):
        dve.bn_stats(b.st[:, which, t], src[:, t]).then_inc(f["link"], 1)
        n[0] += 1

    def mean_var(which, done, v):
        hold(dve, f["link"], v(n[0]), cr)
        for t in range(GT):
            last = dve.bn_aggr(b.mv[:, which, t], b.st[:, which, t])
        last.then_inc(done, 1)

    def link(ins, v, meanwhile=None):
        ins.then_inc(f["link"], 1)
        n[0] += 1
        k = n[0]
        if meanwhile:
            meanwhile()
        hold(dve, f["link"], v(k), cr)

    def norm1(g, p, t):
        if t == 0:
            hold(dve, f["x_in"][p], (g // 2 + 1) * 16 if isinstance(g, int) else x_count(g), cr)
            hold(dve, f["rs1"], g, cr)
        stats(0, b.x[p], t)

    xc = [None]

    def x_count(g):
        return xc[0]

    def lo(g, hi_sem, bank, to, done):
        for c in range(CC):
            dve.wait_ge(hi_sem, g * 2 + 1 + c)
            apart(dve, cr, g)
            dve.tensor_tensor(to[1][:, c], b.bank(bank + c), to[0][:, c].bitcast(F32), ALU.subtract).then_inc(done, 1)

    def gv(g, fc):
        dve.wait_ge(f["sigr"], g * 2 + 1 + fc)
        apart(dve, cr, g)
        hold(dve, f["U"], g * 6 + 2 + 2 * fc, cr)
        bank = b.bank(3 if fc == 0 else 2)
        dve.scalar_tensor_tensor(b.rg[:, fc], bank, b.bias[:, 1, fc:fc + 1], b.rg[:, fc], ALU.add,
                                 ALU.mult).then_inc(f["gv"], 1)

    def x2(g, v):
        dve.wait_ge(f["y1"], g + 1)
        apart(dve, cr, g)
        hold(dve, f["z2"], g, cr)
        for q in range(GT // 2):
            dve.wait_ge(f["Wo"], g * 2 + 1 + q)
            apart(dve, cr, g)
            dve.tensor_tensor(b.xa[:, 2 * q:2 * q + 2], b.bank(6 + q).rearrange("p (t c) -> p t c", t=2),
                              b.y[:, 2 * q:2 * q + 2], ALU.add).then_inc(f["x2"], 1)
        dve.wait_ge(f["x2"], g * 2 + 2)
        apart(dve, cr, g)
        for t in range(GT):
            stats(1, b.xa, t)
        mean_var(1, f["stats2"], v)

    def residual(g, p):
        hold(dve, f["scat"][p], 16 * GT * (g // 2) if isinstance(g, int) else sc[0], cr)
        dve.scalar_tensor_tensor(b.rows[p][:, :, C:2 * C], b.xa[:, :, :], 0.5, b.x[p][:, :, :], ALU.mult,
                                 ALU.add).then_inc(f["res"], 1)

    sc = [None]

    def g2_lo(g, p):
        dve.wait_ge(f["g2hi"], g * 2 + 2)
        apart(dve, cr, g)
        dve.tensor_tensor(b.g2T[1][:, 1], b.sg[p][:, 1], b.g2T[0][:, 1].bitcast(F32),
                          ALU.subtract).then_inc(f["g2lo"], 1)

    def gates(g, p, v, between):
        dve.wait_ge(f["bidT"], g + 1)
        apart(dve, cr, g)
        raw = b.bank(5).rearrange("p (t k) -> p t k", t=GT)
        link(dve.tensor_copy(b.bid[:], raw[:, :, BIDS:2 * BIDS]), v)
        dve.tensor_tensor(b.bid[:], raw[:, :, 0:BIDS], b.bid[:], ALU.add).then_inc(f["b7"], 1)
        w = lambda k: b.gw[:, k]
        if between:
            between()
        dve.wait_ge(f["conf"], g + 1)
        apart(dve, cr, g)
        for e in range(3):
            last = dve.scalar_tensor_tensor(w(e), b.conf[:, :, e], b.shares[:, e:e + 1], b.conf[:, :, 3], ALU.mult,
                                            ALU.mult)
        link(last, v, lambda: g2_lo(g, p))
        for e in range(3):
            last = dve.tensor_tensor(w(e), w(e), b.bid[:, :, 4 + e], ALU.add)
        link(last, v)
        dve.tensor_tensor(w(3), w(1), w(0), ALU.is_gt)
        dve.tensor_tensor(w(4), w(0), w(1), ALU.max)
        link(dve.tensor_tensor(w(6), b.conf[:, :, 1], b.conf[:, :, 0], ALU.subtract), v)
        dve.tensor_tensor(w(5), w(2), w(4), ALU.is_gt)
        link(dve.tensor_tensor(w(6), w(6), w(3), ALU.mult), v)
        dve.tensor_copy(b.e16[:, 0:GT], w(3))
        link(dve.tensor_copy(b.cnt[:, 0:1], b.cnt[:, GT:GT + 1]), v)
        link(dve.tensor_tensor_scan(b.cnt[:, 1:GT + 1], b.ones4[:], w(3), b.cnt[:, 0:1], ALU.mult, ALU.add), v)
        dve.tensor_copy(b.e16[:, 2 * GT:2 * GT + 1], b.cnt[:, GT:GT + 1])
        dve.tensor_copy(b.e16[:, GT:2 * GT], b.cnt[:, 0:GT]).then_inc(f["e"], 1)

    def win(g, p, v, part):
        tokc = slice(g * GT, g * GT + GT) if isinstance(g, int) else bass.ds(g * GT, GT)
        w = lambda k: b.gw[:, k]
        dve.tensor_tensor(w(9), w(3), b.tok[:, 1, tokc], ALU.mult)
        link(dve.tensor_tensor(w(6), w(6), b.conf[:, :, 0], ALU.add), v, lambda: part(0))
        dve.tensor_tensor(w(11), w(9), b.tok[:, 0, tokc], ALU.add)
        link(dve.tensor_tensor(w(7), b.conf[:, :, 2], w(6), ALU.subtract), v, lambda: part(1))
        link(dve.tensor_tensor(w(7), w(7), w(5), ALU.mult), v, lambda: part(2))
        link(dve.tensor_tensor(w(7), w(7), w(6), ALU.add), v, lambda: part(3))
        link(dve.tensor_scalar(w(8), w(7), 1e-6, None, ALU.add), v)
        link(dve.reciprocal(w(9), w(8)), v)
        link(dve.scalar_tensor_tensor(w(10), w(7), 0.5, w(9), ALU.mult, ALU.mult), v)
        link(dve.tensor_tensor(b.gt[p][:], w(10), w(5), ALU.mult), v)
        dve.tensor_tensor(b.rows[p][:, :, 2 * C], w(10), b.gt[p][:], ALU.subtract)
        dve.tensor_copy(b.rows[p][:, :, 2 * C + 1].bitcast(I32), b.tok[:, 0, tokc])

    def rank(g, p):
        dve.wait_ge(f["pref"], g + 1)
        apart(dve, cr, g)
        dve.tensor_tensor(b.posi[p][:], b.gw[:, 11], b.bank(5)[:, 0:GT], ALU.subtract).then_inc(f["posr"], 1)

    def g2(g, p):
        for fc in range(CC):
            dve.wait_ge(f["W"], g * 2 + 1 + fc)
            apart(dve, cr, g)
            dve.scalar_tensor_tensor(b.sg[p][:, fc], b.bank(3 + fc), b.bias[:, 3, fc:fc + 1], b.sg[p][:, fc],
                                     ALU.add, ALU.mult).then_inc(f["g2"], 1)

    def w3(g, p):
        for t in range(GT):
            if t % 2 == 0:
                dve.wait_ge(f["W3"], g * 2 + 1 + t // 2)
                apart(dve, cr, g)
            last = dve.scalar_tensor_tensor(b.rows[p][:, t, C:2 * C], b.bank(6 + t // 2)[:, (t % 2) * C:(t % 2 + 1) * C],
                                            b.gt[p][:, t:t + 1], b.rows[p][:, t, C:2 * C], ALU.mult, ALU.add)
        last.then_inc(f["rdone"], 1)

    fixed = lambda k: k

    def g_lo(g):
        for fc in range(CC):
            dve.wait_ge(f["ghi"], g * 2 + 1 + fc)
            apart(dve, cr, g)
            dve.tensor_tensor(b.gT[1][:, fc], b.rg[:, fc], b.gT[0][:, fc].bitcast(F32),
                              ALU.subtract).then_inc(f["glo"], 1)

    def body(g, p, v, last=False):
        q = 1 - p
        part = (lambda t: None) if last else (lambda t: norm1(g + 2, p, t))
        if not last:
            gv(g + 1, 0)
        if isinstance(g, int) and g == 0:
            for t in range(GT):
                part(t)
        else:
            win(g - 1, q, v, part)
        if not last:
            mean_var(0, f["stats1"], v)
        if not (isinstance(g, int) and g == 0):
            w3(g - 1, q)
            rank(g - 1, q)
        if not last:
            gv(g + 1, 1)
            g_lo(g + 1)
        lo(g, f["hhi"], 0, b.hT, f["hlo"])
        if not last:
            x2(g + 1, v)
            lo(g + 2, f["zhi"], 0, b.zT, f["zlo"])
        g2(g, p)
        gates(g, p, v, None if last else (lambda: residual(g + 1, q)))

    for t in range(GT):
        norm1(0, 0, t)
    mean_var(0, f["stats1"], fixed)
    lo(0, f["zhi"], 0, b.zT, f["zlo"])
    for t in range(GT):
        norm1(1, 1, t)
    mean_var(0, f["stats1"], fixed)
    gv(0, 0)
    gv(0, 1)
    g_lo(0)
    lo(1, f["zhi"], 0, b.zT, f["zlo"])
    x2(0, fixed)
    residual(0, 0)
    body(0, 0, fixed)
    start = n[0]
    with dve.Fori(0, (NG - 2) // 2) as it:
        per = [0]
        for k in range(2):
            g = it * 2 + 1 + k
            xc[0] = it * 16 + 16 * ((3 + k) // 2 + 1)
            sc[0] = it * (16 * GT) + 16 * GT * ((2 + k) // 2)
            v = (lambda q: it * LINKS + q)
            body(g, (1 + k) % 2, v)
        assert n[0] - start == LINKS, n[0] - start
    n[0] = start + LINKS * ((NG - 2) // 2)
    body(NG - 1, (NG - 1) % 2, fixed, True)
    win(NG - 1, (NG - 1) % 2, fixed, lambda t: None)
    w3(NG - 1, (NG - 1) % 2)
    rank(NG - 1, (NG - 1) % 2)
    dve.wait_ge(f["n1"], 1)
    link(dve.tensor_copy(b.n1[:], b.bank(5)[:, 0:1]), fixed)
    dve.tensor_scalar(b.padi[:], b.slot_row[:, NSLOT:NSLOT + ST], b.n1[:, 0:1], None, ALU.subtract).then_inc(f["padi"], 1)
    link(dve.tensor_scalar(b.flag[:], b.slot_row[:, 0:NSLOT], b.n1[:, 0:1], float(N), ALU.add, ALU.is_ge), fixed)
    dve.tensor_scalar(b.nflag[:], b.flag[:], -1.0, 1.0, ALU.mult, ALU.add)
    dve.tensor_copy(b.flagi[:], b.flag[:])
    dve.memset(b.cnt[:], 0.0).then_inc(f["flag"], 1)
    b.link_total = n[0]


LINKS = 46



def slots(eng, first, body):
    first()
    for j in (1, 2):
        body(j, j % 2, False)
    with eng.Fori(0, (NSLOT - 5) // 2) as it:
        for k in range(2):
            body(it * 2 + 3 + k, (3 + k) % 2, False)
    for j in (NSLOT - 2, NSLOT - 1):
        body(j, j % 2, j == NSLOT - 1)


def ffn_b_tensor(pe, b, f):
    cr = b.carry["pe"]

    def sT(j, p, loads):
        pe.wait_ge(f["s_in"][p], loads * 16)
        apart(pe, cr, loads)
        hold(pe, f["slo"], j, cr)
        for c in range(CC):
            for t in range(ST):
                mm = pe.transpose(b.bank(0)[:, c * SLOT + t * P:c * SLOT + (t + 1) * P],
                                  b.sz[p][:, t, c * P:(c + 1) * P], b.ident[:])
        mm.then_inc(f["sT"], 1)

    def K(j, e):
        for q in range(HC // 2):
            hold(pe, f["relu"], j * 4 - 3 + q, cr)
            for h in (2 * q, 2 * q + 1):
                for c in range(CC):
                    mm = passes(pe, b.bank(1 + q)[:, (h % 2) * SLOT:(h % 2 + 1) * SLOT],
                                lambda p: b.K[p][:, e, c, h * P:(h + 1) * P], lambda p: b.shT[p][:, c], c == 0,
                                c == CC - 1)
            mm.then_inc(f["Ks"], 1)

    def V(j, p, e):
        for t in range(ST):
            for h in range(HC):
                mm = passes(pe, b.bank(5)[:, t * C:(t + 1) * C], lambda q: b.hr[p][q][:, h, t * P:(t + 1) * P],
                            lambda q: b.V[q][:, e, h], h == 0, h == HC - 1)
        mm.then_inc(f["Vs"], 1)

    def expert(j):
        return pe.value_load(b.flagi[0:1, bass.ds(j, 1)], min_val=0, max_val=1)

    def either(e, run):
        with pe.If(e < 1):
            run(0)
        with pe.Else():
            run(1)

    def Kj(j, e):
        pe.wait_ge(f["slo"], j + 1)
        apart(pe, cr, j)
        either(e, lambda e: K(j, e))

    def Vj(j, p, e):
        pe.wait_ge(f["hrlo"], j * 4 + 4)
        apart(pe, cr, j)
        hold(pe, f["orow"], j, cr)
        either(e, lambda e: V(j, p, e))

    def first():
        sT(0, 0, 1)
        Kj(0, expert(0))
        sT(1, 1, 1)

    def body(j, p, last):
        before, this = expert(j - 1), expert(j)
        Kj(j, this)
        if not last:
            sT(j + 1, 1 - p, (j + 1) // 2 + 1 if isinstance(j, int) else loads_of(j, p))
        Vj(j - 1, 1 - p, before)

    def loads_of(j, p):
        return half[0] + (1 if p else 0)

    half = [None]
    first()
    for j in (1, 2):
        body(j, j % 2, False)
    with pe.Fori(0, (NSLOT - 5) // 2) as it:
        for k in range(2):
            half[0] = it + 2 if k == 0 else it + 3
            body(it * 2 + 3 + k, (3 + k) % 2, False)
    for j in (NSLOT - 2, NSLOT - 1):
        body(j, j % 2, j == NSLOT - 1)
    Vj(NSLOT - 1, (NSLOT - 1) % 2, expert(NSLOT - 1))


def ffn_b_scalar(act, b, f):
    cr = b.carry["act"]

    def shi(j):
        act.wait_ge(f["sT"], j + 1)
        apart(act, cr, j)
        hold(act, f["Ks"], j * 4, cr)
        act.copy(b.shT[0][:, :, :], b.bank(0).rearrange("p (c n) -> p c n", c=CC)).then_inc(f["shi"], 1)

    def relu(j, p):
        act.wait_ge(f["kbs"], j + 1)
        apart(act, cr, j)
        for q in range(HC // 2):
            act.wait_ge(f["Ks"], j * 4 + q + 1)
            apart(act, cr, j)
            if q >= 2 or not (isinstance(j, int) and j == 0):
                hold(act, f["sq"], j * 4 + q - 1, cr)
            for h in (2 * q, 2 * q + 1):
                last = act.activation(b.r[q % 2][:, (h % 2) * SLOT:(h % 2 + 1) * SLOT],
                                      b.bank(1 + q)[:, (h % 2) * SLOT:(h % 2 + 1) * SLOT], ACT.Relu,
                                      bias=b.kbs[p][:, h:h + 1])
            last.then_inc(f["relu"], 1)
            act.wait_ge(f["relu"], j * 4 + q + 1)
            apart(act, cr, j)
            if q == 0:
                hold(act, f["Vs"], j - 1, cr)
            act.activation(b.hr[p][0][:, 2 * q:2 * q + 2].rearrange("p h n -> p (h n)"), b.r[q % 2][:, :],
                           ACT.Square).then_inc(f["hrhi"], 1)

    def first():
        shi(0)
        relu(0, 0)
        shi(1)

    def body(j, p, last):
        relu(j, p)
        if not last:
            shi(j + 1)

    slots(act, first, body)


def ffn_b_vector(dve, b, f):
    cr = b.carry["dve"]

    def kbs(j, p):
        hold(dve, f["relu"], j * 4 - 4, cr)
        hold(dve, f["kbs"], j, cr)
        at = slice(j, j + 1) if isinstance(j, int) else bass.ds(j, 1)
        dve.tensor_scalar(b.kbt[:], b.kbias[:, 0], b.nflag[:, at], None, ALU.mult).then_inc(f["link"], 1)
        n[0] += 1
        hold(dve, f["link"], n[0] if isinstance(j, int) else base[0] + n[0], cr)
        dve.scalar_tensor_tensor(b.kbs[p][:], b.kbias[:, 1], b.flag[:, at], b.kbt[:], ALU.mult,
                                 ALU.add).then_inc(f["kbs"], 1)

    def slo(j):
        dve.wait_ge(f["shi"], j + 1)
        apart(dve, cr, j)
        dve.tensor_tensor(b.shT[1][:, :, :], b.bank(0).rearrange("p (c n) -> p c n", c=CC),
                          b.shT[0][:, :, :].bitcast(F32), ALU.subtract).then_inc(f["slo"], 1)

    def sq(j, p):
        for q in range(HC // 2):
            dve.wait_ge(f["relu"], j * 4 + q + 1)
            apart(dve, cr, j)
            if q >= 2 or not (isinstance(j, int) and j == 0):
                hold(dve, f["hrlo"], j * 4 + q - 1, cr)
            dve.tensor_tensor(b.sq[q % 2][:, :], b.r[q % 2][:, :], b.r[q % 2][:, :], ALU.mult).then_inc(f["sq"], 1)

    def orow(j, p, uses):
        dve.wait_ge(f["Vs"], j + 1)
        apart(dve, cr, j)
        hold(dve, f["o_out"][p], uses * 16 * ST, cr)
        hold(dve, f["r_in"][p], uses * 16 + 16, cr)
        dve.tensor_copy(b.idx[p][:], b.srow[p][:, :, C + 1].bitcast(I32))
        for t in range(ST):
            last = dve.scalar_tensor_tensor(b.o[p][:, t], b.bank(5)[:, t * C:(t + 1) * C],
                                            b.srow[p][:, t, C:C + 1], b.srow[p][:, t, 0:C], ALU.mult,
                                            ALU.add)
        last.then_inc(f["orow"], 1)

    n, base = [b.link_total], [0]

    def body(j, p, last, uses):
        if not last:
            kbs(j + 1, 1 - p)
        sq(j, p)
        if not last:
            slo(j + 1)
        orow(j - 1, 1 - p, uses)

    kbs(0, 0)
    slo(0)
    kbs(1, 1)
    sq(0, 0)
    slo(1)
    for j in (1, 2):
        body(j, j % 2, False, 0)
    n0 = n[0]
    with dve.Fori(0, (NSLOT - 5) // 2) as it:
        base[0] = it * 2
        for k in range(2):
            body(it * 2 + 3 + k, (3 + k) % 2, False, it + 1)
    n[0] = n0 + NSLOT - 5
    for j in (NSLOT - 2, NSLOT - 1):
        body(j, j % 2, j == NSLOT - 1, (j - 1) // 2)
    orow(NSLOT - 1, (NSLOT - 1) % 2, (NSLOT - 1) // 2)


def ffn_b_gpsimd(pool, b, f, dst):
    cr = b.carry["pool"]

    def hrlo(j, p):
        for q in range(HC // 2):
            pool.wait_ge(f["hrhi"], j * 4 + q + 1)
            apart(pool, cr, j)
            pool.wait_ge(f["sq"], j * 4 + q + 1)
            apart(pool, cr, j)
            pool.tensor_tensor(b.hr[p][1][:, 2 * q:2 * q + 2].rearrange("p h n -> p (h n)"), b.sq[q % 2][:, :],
                               b.hr[p][0][:, 2 * q:2 * q + 2].rearrange("p h n -> p (h n)").bitcast(F32),
                               ALU.subtract).then_inc(f["hrlo"], 1)

    def send(j, p):
        pool.wait_ge(f["orow"], j + 1)
        apart(pool, cr, j)
        for t in range(ST):
            pool.indirect_dma_start(dst, bass.IndirectOffsetOnAxis(b.idx[p][:, t:t + 1].bitcast(U32), 0),
                                    b.o[p][:, t, :], None, bounds_check=N - 1, oob_is_err=False
                                    ).then_inc(f["o_out"][p], 16)

    def body(j, p, last):
        hrlo(j, p)
        send(j - 1, 1 - p)

    slots(pool, lambda: hrlo(0, 0), body)
    send(NSLOT - 1, (NSLOT - 1) % 2)
    pool.wait_ge(f["o_out"][0], 16 * ST * ((NSLOT + 1) // 2))
    pool.wait_ge(f["o_out"][1], 16 * ST * (NSLOT // 2))



def pairs_before(q):
    return q * (q + 1) // 2


def chunks_of(q):
    return q // 2 + 1


def chunks_before(q, t=0):
    return sum(ST * chunks_of(i) for i in range(q)) + t * chunks_of(q)


def halves(q):
    h = (q + 1) // 2
    return h, min(q, h + 2)


PAIRS = pairs_before(QB)
CHUNKS = chunks_before(QB)


def sequences(eng, a, carry, run):
    with eng.Fori(0, BATCH) as bt:
        run(bt * QB, bt * PAIRS, bt * CHUNKS, bt)
        eng.drain().then_inc(a["sequence"], 1)
        hold(eng, a["sequence"], bt * 5 + 5, carry)


def attention_sync(sp, b, a):
    cr = b.carry["sp"]
    xin = b.x1.rearrange("(n t p) c -> n p t c", t=ST, p=P)
    xout = b.x2.rearrange("(n t p) c -> n p t c", t=ST, p=P)

    def run(n0, m0, c0, bt):
        def load(q):
            if q >= AX_BUFS:
                hold(sp, a["y"], n0 + q - AX_BUFS + 1, cr)
            sp.dma_start(b.ax[q % AX_BUFS][:], xin[n0 + q]).then_inc(a["x_in"][q % AX_BUFS], 16)

        for q in range(AX_BUFS):
            load(q)
        for q in range(QB):
            sp.wait_ge(a["y"], n0 + q + 1)
            apart(sp, cr, n0)
            sp.dma_start(xout[n0 + q], b.ao[:]).then_inc(a["out"], 16)
            if q + AX_BUFS < QB:
                load(q + AX_BUFS)
        sp.wait_ge(a["out"], (n0 + QB) * 16)
        apart(sp, cr, n0)

    sequences(sp, a, cr, run)


def attention_tensor(pe, b, a):
    cr = b.carry["pe"]

    def run(n0, m0, c0, bt):
        def zT(q):
            pe.wait_ge(a["z"], n0 + q + 1)
            apart(pe, cr, n0)
            for c in range(CC):
                for t in range(ST):
                    mm = pe.transpose(b.bank(3)[:, c * SLOT + t * P:c * SLOT + (t + 1) * P],
                                      b.az[:, t, c * P:(c + 1) * P], b.ident[:])
            mm.then_inc(a["T"], 1)

        def project_v(q):
            pe.wait_ge(a["zlo"], n0 + q + 1)
            apart(pe, cr, n0)
            for t in range(ST):
                for c in range(CC):
                    for p in range(2):
                        mm = pe.matmul(b.bank(3)[:, t * C:(t + 1) * C], b.azT[p][:, c, t * P:(t + 1) * P],
                                       b.Wvv[:, c], start=(c == 0 and p == 0), stop=(c == 1 and p == 1))
            mm.then_inc(a["vp"], 1)

        def project_qk(q):
            pe.wait_ge(a["vsum"], n0 + q + 1)
            apart(pe, cr, n0)
            for m in range(2):
                for c in range(CC):
                    mm = passes(pe, b.bank(3)[:, m * SLOT:(m + 1) * SLOT], lambda p: b.Wqk[p][:, m, c],
                                lambda p: b.azT[p][:, c], c == 0, c == CC - 1)
            mm.then_inc(a["qk"], 1)

        def scores(q, t):
            pe.wait_ge(a["qklo"], n0 + q + 1)
            apart(pe, cr, n0)
            before = chunks_before(q, t)
            last = chunks_of(q) if t else chunks_of(q - 1)
            for c in range(chunks_of(q)):
                if before and c < last:
                    hold(pe, a["exp"], c0 + before - last + c + 1, cr)
                w = min(KEYS, (q + 1) * SLOT - c * KEYS)
                mm = passes(pe, b.bank(4 + c)[:, 0:w], lambda p: b.qT[q % 2][p][:, t * P:(t + 1) * P],
                            lambda p: b.kT[p][:, c * KEYS:c * KEYS + w])
                mm.then_inc(a["S"], 1)

        def turn(q, j):
            m = pairs_before(q) + j
            if m >= 2:
                hold(pe, a["ptlo"], m0 + m - 1, cr)
            pe.wait_ge(a["exp"], c0 + chunks_before(q, 1) + j // 2 + 1)
            apart(pe, cr, c0)
            for kt in range(2):
                for t in range(ST):
                    mm = pe.transpose(b.bank(m % 2)[:, kt * SLOT + t * P:kt * SLOT + (t + 1) * P],
                                      b.p[1 - q % 2][:, t, (2 * j + kt) * P:(2 * j + kt + 1) * P], b.ident[:])
            mm.then_inc(a["PT"], 1)

        def weigh(q, j):
            m = pairs_before(q) + j
            pe.wait_ge(a["ptlo"], m0 + m + 1)
            apart(pe, cr, m0)
            if j == 0 and q:
                hold(pe, a["y"], n0 + q, cr)
            for kt in range(2):
                mm = passes(pe, b.bank(2)[:, 0:SLOT], lambda p: b.v[p][:, 2 * j + kt],
                            lambda p: b.pT[m % 2][p][:, kt], j == 0 and kt == 0, j == q and kt == 1)
            mm.then_inc(a["PV"], 1)

        def output(q):
            pe.wait_ge(a["olo"], n0 + q + 1)
            apart(pe, cr, n0)
            for t in range(ST):
                mm = passes(pe, b.bank(2)[:, t * C:(t + 1) * C], lambda p: b.oT[p][:, t * P:(t + 1) * P],
                            lambda p: b.Wao[p][:])
            mm.then_inc(a["Y"], 1)

        def weigh_some(q, first, end):
            for j in range(first, end):
                weigh(q - 1, j)
                if j + 2 < q:
                    turn(q - 1, j + 2)

        zT(0)
        project_v(0)
        project_qk(0)
        for q in range(QB + 1):
            h, h2 = halves(q)
            for j in range(min(2, q)):
                turn(q - 1, j)
            if q >= 2:
                output(q - 2)
            if q < QB:
                scores(q, 0)
            if q + 1 < QB:
                zT(q + 1)
            weigh_some(q, 0, h)
            if q + 1 < QB:
                project_v(q + 1)
            if q < QB:
                scores(q, 1)
            weigh_some(q, h, h2)
            if q + 1 < QB:
                project_qk(q + 1)
            weigh_some(q, h2, q)
        output(QB - 1)

    sequences(pe, a, cr, run)


def attention_scalar(act, b, a):
    cr = b.carry["act"]

    def run(n0, m0, c0, bt):
        def z_hi(q):
            act.wait_ge(a["T"], n0 + q + 1)
            apart(act, cr, n0)
            act.copy(b.azT[0][:, :, :], b.bank(3).rearrange("p (c n) -> p c n", c=CC)).then_inc(a["zhi"], 1)

        def v_hi(q):
            act.wait_ge(a["vp"], n0 + q + 1)
            apart(act, cr, n0)
            act.copy(b.vs[:, :, :], b.bank(3).rearrange("p (t n) -> p t n", t=ST)[:, :, 0:DK]).then_inc(a["vs"], 1)
            act.wait_ge(a["vsum"], n0 + q + 1)
            apart(act, cr, n0)
            act.copy(b.v[0][:, 2 * q:2 * q + 2], b.vt[:, :, :]).then_inc(a["vhi"], 1)

        def qk_hi(q):
            act.wait_ge(a["qk"], n0 + q + 1)
            apart(act, cr, n0)
            act.copy(b.qT[q % 2][0][:, :], b.bank(3)[:, 0:SLOT])
            act.copy(b.kT[0][:, q * SLOT:(q + 1) * SLOT], b.bank(3)[:, SLOT:2 * SLOT]).then_inc(a["qkhi"], 1)

        def expo(q, t, between):
            act.wait_ge(a["nb"], (n0 + q) * 2 + t + 1)
            apart(act, cr, n0)
            if q >= 2:
                hold(act, a["PT"], m0 + pairs_before(q - 1), cr)
            for c in range(chunks_of(q)):
                w = min(KEYS, (q + 1) * SLOT - c * KEYS)
                act.activation(b.p[1 - q % 2][:, t, c * KEYS:c * KEYS + w], b.bank(4 + c)[:, 0:w], ACT.Exp,
                               bias=b.mx[:, 4 + q % 2, t:t + 1], scale=SCALE,
                               accum_out=b.csum[:, q % 2, t, c:c + 1]).then_inc(a["exp"], 1)
                if c == (chunks_of(q) - 1) // 2:
                    between()

        def pairs(q, first, end):
            for j in range(first, end):
                m = pairs_before(q - 1) + j
                act.wait_ge(a["PT"], m0 + m + 1)
                apart(act, cr, m0)
                if m >= 2:
                    hold(act, a["PV"], m0 + m - 1, cr)
                act.copy(b.pT[m % 2][0][:, :, :], b.bank(m % 2).rearrange("p (k n) -> p k n", k=2)
                         ).then_inc(a["pthi"], 1)

        def o_hi(q):
            act.wait_ge(a["PV"], m0 + pairs_before(q + 1))
            apart(act, cr, m0)
            act.copy(b.oT[0][:, :], b.bank(2)[:, 0:SLOT]).then_inc(a["ohi"], 1)

        z_hi(0)
        v_hi(0)
        qk_hi(0)
        ahead = 0
        for q in range(QB + 1):
            h, h2 = halves(q)
            pairs(q, min(ahead, q), min(3, q, h + 2))
            if q + 1 < QB:
                z_hi(q + 1)
            if q < QB:
                expo(q, 0, lambda: pairs(q, min(3, q, h + 2), min(4, q, h + 2)))
                pairs(q, min(4, q, h + 2), min(h + 2, q))
            else:
                pairs(q, min(3, q, h + 2), min(h + 2, q))
            if q + 1 < QB:
                v_hi(q + 1)
            mid = min(h + 3, q) if h2 > h else min(h + 2, q)
            pairs(q, min(h + 2, q), mid)
            early = q and h2 == q
            if early:
                pairs(q, mid, q)
            ahead = 1 if early and q < QB else 0

            def amid():
                if q + 1 < QB:
                    qk_hi(q + 1)
                if early:
                    o_hi(q - 1)
                    pairs(q + 1, 0, 1)
                else:
                    pairs(q, mid, min(mid + 1, q))

            if q < QB:
                expo(q, 1, amid)
            if q and not early:
                pairs(q, min(mid + 1, q) if q < QB else mid, q)
                o_hi(q - 1)

    sequences(act, a, cr, run)


ATT_LINKS = sum(1 + 2 + ST * (3 if chunks_of(q) > 1 else 2) for q in range(QB))


def attention_vector(dve, b, a):
    cr = b.carry["dve"]

    def run(n0, m0, c0, bt):
        links = [0]

        def link(ins):
            ins.then_inc(a["link"], 1)
            links[0] += 1
            hold(dve, a["link"], bt * ATT_LINKS + links[0], cr)

        def norm(q):
            x = b.ax[q % AX_BUFS]
            loads = len(range(q % AX_BUFS, QB, AX_BUFS))
            hold(dve, a["x_in"][q % AX_BUFS], bt * (16 * loads) + 16 * (q // AX_BUFS) + 16, cr)
            for t in range(ST):
                last = dve.bn_stats(b.st[:, 0, t], x[:, t])
            link(last)
            for t in range(ST):
                last = dve.bn_aggr(b.mv[:, 0, t], b.st[:, 0, t])
            last.then_inc(a["stats"], 1)

        def z(q):
            dve.wait_ge(a["rs"], n0 + q + 1)
            apart(dve, cr, n0)
            if q:
                hold(dve, a["T"], n0 + q, cr)
            for t in range(ST):
                last = dve.tensor_scalar(b.az[:, t], b.ax[q % AX_BUFS][:, t], b.mv[:, 0, t, 0:1],
                                         b.rs[:, 1, 1, t:t + 1], ALU.subtract, ALU.mult)
            last.then_inc(a["z"], 1)

        def z_lo(q):
            dve.wait_ge(a["zhi"], n0 + q + 1)
            apart(dve, cr, n0)
            dve.tensor_tensor(b.azT[1][:, :, :], b.bank(3).rearrange("p (c n) -> p c n", c=CC),
                              b.azT[0][:, :, :].bitcast(F32), ALU.subtract).then_inc(a["zlo"], 1)

        def v_sum(q):
            dve.wait_ge(a["vs"], n0 + q + 1)
            apart(dve, cr, n0)
            if q:
                hold(dve, a["vlo"], n0 + q, cr)
            dve.tensor_tensor(b.vt[:, :, :], b.bank(3).rearrange("p (t n) -> p t n", t=ST)[:, :, DK:2 * DK],
                              b.vs[:, :, :], ALU.add).then_inc(a["vsum"], 1)

        def v_lo(q):
            dve.wait_ge(a["vhi"], n0 + q + 1)
            apart(dve, cr, n0)
            dve.tensor_tensor(b.v[1][:, 2 * q:2 * q + 2], b.vt[:, :, :], b.v[0][:, 2 * q:2 * q + 2].bitcast(F32),
                              ALU.subtract).then_inc(a["vlo"], 1)

        def qk_lo(q):
            dve.wait_ge(a["qkhi"], n0 + q + 1)
            apart(dve, cr, n0)
            dve.tensor_tensor(b.qT[q % 2][1][:, :], b.bank(3)[:, 0:SLOT], b.qT[q % 2][0][:, :].bitcast(F32),
                              ALU.subtract)
            at = slice(q * SLOT, (q + 1) * SLOT)
            dve.tensor_tensor(b.kT[1][:, at], b.bank(3)[:, SLOT:2 * SLOT], b.kT[0][:, at].bitcast(F32),
                              ALU.subtract).then_inc(a["qklo"], 1)

        def maxima(q, t):
            n = chunks_of(q)
            for c in range(n):
                w = min(KEYS, (q + 1) * SLOT - c * KEYS)
                sc = b.bank(4 + c)
                dve.wait_ge(a["S"], c0 + chunks_before(q, t) + c + 1)
                apart(dve, cr, c0)
                if c == n - 1:
                    link(dve.tensor_tensor(sc[:, w - SLOT:w], sc[:, w - SLOT:w], b.mask[:, t], ALU.add))
                top = dve.tensor_reduce(b.cmax[:, t, c:c + 1], sc[:, 0:w], AX.X, ALU.max)
            link(top)
            if n > 1:
                link(dve.tensor_reduce(b.cmax[:, t, 0:1], b.cmax[:, t, 0:n], AX.X, ALU.max))
            dve.tensor_scalar(b.mx[:, 4 + q % 2, t:t + 1], b.cmax[:, t, 0:1], -SCALE, None, ALU.mult
                              ).then_inc(a["nb"], 1)

        def pairs(q, first, end):
            for j in range(first, end):
                m = pairs_before(q - 1) + j
                dve.wait_ge(a["pthi"], m0 + m + 1)
                apart(dve, cr, m0)
                dve.tensor_tensor(b.pT[m % 2][1][:, :, :], b.bank(m % 2).rearrange("p (k n) -> p k n", k=2),
                                  b.pT[m % 2][0][:, :, :].bitcast(F32), ALU.subtract).then_inc(a["ptlo"], 1)

        def o_lo(q):
            dve.wait_ge(a["ohi"], n0 + q + 1)
            apart(dve, cr, n0)
            dve.tensor_tensor(b.oT[1][:, :], b.bank(2)[:, 0:SLOT], b.oT[0][:, :].bitcast(F32),
                              ALU.subtract).then_inc(a["olo"], 1)

        def y(q):
            link(dve.tensor_reduce(b.sum[:, q % 2, :], b.csum[:, q % 2, :, 0:chunks_of(q)], AX.X, ALU.add))
            link(dve.reciprocal(b.mx[:, 2, :], b.sum[:, q % 2, :]))
            dve.wait_ge(a["Y"], n0 + q + 1)
            apart(dve, cr, n0)
            if q:
                hold(dve, a["out"], (n0 + q) * 16, cr)
            for t in range(ST):
                last = dve.scalar_tensor_tensor(b.ao[:, t], b.bank(2)[:, t * C:(t + 1) * C], b.mx[:, 2, t:t + 1],
                                                b.ax[q % AX_BUFS][:, t], ALU.mult, ALU.add)
            last.then_inc(a["y"], 1)

        norm(0)
        z(0)
        z_lo(0)
        v_sum(0)
        v_lo(0)
        qk_lo(0)
        norm(1)
        for q in range(QB + 1):
            h, h2 = halves(q)
            pairs(q, 0, min(2, q))
            if q + 1 < QB:
                z(q + 1)
            if q >= 2:
                y(q - 2)
            if q < QB:
                maxima(q, 0)
            pairs(q, min(2, q), min(3, q, h + 2))
            if q + 1 < QB:
                z_lo(q + 1)
            pairs(q, min(3, q, h + 2), min(h + 2, q))
            if q + 1 < QB:
                v_sum(q + 1)
            if q < QB:
                maxima(q, 1)
            if q + 1 < QB:
                v_lo(q + 1)
                qk_lo(q + 1)
            pairs(q, min(h + 2, q), q)
            if q:
                o_lo(q - 1)
            if q + 2 < QB:
                norm(q + 2)
        y(QB - 1)
        assert links[0] == ATT_LINKS, links

    sequences(dve, a, cr, run)


def attention_gpsimd(pool, b, a):
    cr = b.carry["pool"]

    def run(n0, m0, c0, bt):
        for q in range(QB):
            pool.wait_ge(a["stats"], n0 + q + 1)
            apart(pool, cr, n0)
            var, t, r = (v[:, 0:ST] for v in (b.mv[:, 0, :, 1], b.rs[:, 1, 0], b.rs[:, 1, 1]))
            if q:
                hold(pool, a["z"], n0 + q, cr)
            pool.tensor_scalar(t, var, EPS, 0.0, ALU.add, ALU.add).then_inc(a["plink"], 1)
            pool.wait_ge(a["plink"], n0 + q + 1)
            apart(pool, cr, n0)
            pool.tensor_tensor(r, t, b.half[:, 0:ST], ALU.pow).then_inc(a["rs"], 1)

    sequences(pool, a, cr, run)



def laid_out(inp):
    def chunks(w, k=CC):
        return w.reshape(k, P, -1).transpose(1, 0, 2).reshape(P, -1)

    g = lambda n: np.asarray(inp[n])
    f = "L0_ffn_"
    bid = np.zeros((C, BIDS), np.float32)
    bid[:, 0:2] = g(f + "conf_rwkv").T
    bid[:, 2] = g(f + "conf_trans")
    bid[:, 3] = g(f + "w_diff")
    bid[:, 4:7] = g(f + "W_aff")
    t = np.arange(N, dtype=np.float32).reshape(N // P, P).T
    k = np.arange(P)
    tri = np.stack([(k[:, None] < k[None, :]), np.ones((P, P), bool)], 1).astype(np.float32)
    mask = np.zeros((P, ST, SLOT), np.float32)
    for i in range(ST):
        mask[:, i] = np.where(np.arange(SLOT)[None, :] > k[:, None] + i * P, np.float32(-3e38), np.float32(0))
    slot_row = np.zeros((P, NSLOT + ST), np.float32)
    slot_row[:, 0:NSLOT] = np.arange(NSLOT) * SLOT
    slot_row[:, NSLOT:] = N + k[:, None] + P * np.arange(ST)
    return {
        "x": g("L0_attn_x").reshape(N, C),
        "w256": np.concatenate([chunks(g(f + n)) for n in ("Wr", "Wv", "W1", "Wo")], 1),
        "w_st": np.concatenate([chunks(g(f + "Ws").T), chunks(g(f + "W2")), chunks(g(f + "W3")), chunks(bid)], 1),
        "k_w": np.stack([chunks(g(f + "K_rwkv")[e]) for e in range(2)], 1),
        "v_w": np.stack([chunks(g(f + "V_rwkv")[e], HC) for e in range(2)], 1),
        "w_qkv": np.concatenate([chunks(g("L0_attn_" + n)) for n in ("Wq", "Wk", "Wv")] + [g("L0_attn_Wo")], 1),
        "ln": np.concatenate([g(f + n).reshape(CC, P).T for n in ("ln1_w", "ln1_b", "ln2_w", "ln2_b")], 1
                             ).reshape(P, 4, CC),
        "shares": np.broadcast_to(g(f + "capital_shares")[None, :], (P, 3)),
        "ident": np.eye(P, dtype=np.float32),
        "tri": tri,
        "mask": mask,
        "tok": np.stack([t, ROWS - 1 - t], 1),
        "slot_row": slot_row,
    }


def kernel(**inputs):
    import concourse.bacc as bacc
    from concourse.bass_utils import run_bass_kernel_spmd as run

    nc = bacc.Bacc("TRN2", target_bir_lowering=False, num_devices=1)
    arrays, args = {}, {}
    for name, v in laid_out(inputs).items():
        v = np.ascontiguousarray(v)
        arrays[f"in_{name}"] = v
        args[name] = nc.dram_tensor(f"in_{name}", v.shape, mybir.dt.from_np(v.dtype), kind="ExternalInput").ap()
    out = nc.dram_tensor("out_x", (N, C), F32, kind="ExternalOutput").ap()
    build_kernel(nc, **args, out=out)
    r = run(nc, [arrays], core_ids=[0])
    return r.results[0]["out_x"].reshape(BATCH, SEQ, C)
```
